# Optimizing a Trainium2 kernel written in Bass

```python
import numpy as np
import jax
import jax.numpy as jnp

def _softmax(x, axis=-1):
    return jax.nn.softmax(x, axis=axis)

def _gelu(x):
    return jax.nn.gelu(x, approximate=True)

def _silu(x):
    return jax.nn.silu(x)

def _sigmoid(x):
    return jax.nn.sigmoid(x)

def _layernorm(x, axis=-1, eps=1e-05):
    m = jnp.mean(x, axis=axis, keepdims=True)
    v = jnp.var(x, axis=axis, keepdims=True)
    return (x - m) / jnp.sqrt(v + eps)

def _scatter_add(tgt, idx, src, axis=0):
    return tgt.at[idx].add(src)

def _segment_sum(src, seg, n):
    return jax.ops.segment_sum(src, seg, n)
kernel_name = 'mk_flamingo_gated_d2_seqx_r4_c50695'

def setup_inputs(seed: int=0):
    np.random.seed(seed)
    _w = jnp.asarray

    def _rec_inputs():
        import jax
        import jax.numpy as jnp
        _rk = jax.random.key(seed)
        x = -0.0002928 + 1 * jax.random.normal(jax.random.fold_in(_rk, 1), (16, 128, 256), jnp.float32)
        _lenS = 128 - jax.random.randint(jax.random.fold_in(_rk, 7), (16,), 0, max(1, 128 // 4) + 1, jnp.int32)
        _lenS2 = 128 - jax.random.randint(jax.random.fold_in(_rk, 8), (16,), 0, max(1, 128 // 4) + 1, jnp.int32)
        _ctx_1024P = jax.random.normal(jax.random.fold_in(_rk, 11), (16, 16, 256), jnp.float32)
        _ctx_1024c = jax.random.dirichlet(jax.random.fold_in(_rk, 511), 0.3 * jnp.ones((16,), jnp.float32), (16, 128))
        _ctx_1024t = jnp.einsum('bsk,bkd->bsd', _ctx_1024c, _ctx_1024P)
        _ctx_1024t = _ctx_1024t * jax.lax.rsqrt(jnp.mean(jnp.square(_ctx_1024t)) + 1e-12) * 0.953939
        ctx_1024 = -1.39393e-06 + 0.999914 * (_ctx_1024t + 0.3 * jax.random.normal(jax.random.fold_in(_rk, 611), (16, 128, 256), jnp.float32))
        _g = jax.random.normal(jax.random.fold_in(_rk, 9001), (2, 2), jnp.float32)
        _g = jnp.sign(_g) * jnp.maximum(jnp.abs(_g), 1.0) + (_g == 0) * 1.0
        g_xattn = _g[0]
        g_ffn = _g[1]
        return (x, ctx_1024, g_xattn, g_ffn)
    x, ctx_1024, g_xattn, g_ffn = _rec_inputs()

    def _L0_xattn_setup():
        import jax, jax.numpy as jnp
        import numpy as np
        EMB = 256
        HID = 256
        HEADS = 16
        HEAD_DIM = HID // HEADS

        def _split_heads(x):
            B, S, H = x.shape
            return x.reshape(B, S, HEADS, H // HEADS).transpose(0, 2, 1, 3)
        key = jax.random.key(seed)
        ks = jax.random.split(key, 11)
        B, S = (2, 512)
        sc = 0.02
        return {'q': jax.random.normal(ks[0], (B, S, EMB), jnp.float32), 'k': jax.random.normal(ks[1], (B, S, EMB), jnp.float32), 'v': jax.random.normal(ks[2], (B, S, EMB), jnp.float32), 'Wq': jax.random.normal(ks[3], (EMB, HID), jnp.float32) * sc, 'bq': jnp.zeros((HID,), jnp.float32), 'Wk': jax.random.normal(ks[4], (EMB, HID), jnp.float32) * sc, 'bk': jnp.zeros((HID,), jnp.float32), 'Wv': jax.random.normal(ks[5], (EMB, HID), jnp.float32) * sc, 'bv': jnp.zeros((HID,), jnp.float32), 'Wo': jax.random.normal(ks[6], (HID, EMB), jnp.float32) * sc, 'bo': jnp.zeros((EMB,), jnp.float32)}
    _L0_xattn_all = _L0_xattn_setup()
    _L0_xattn_in = {k: v for k, v in _L0_xattn_all.items() if k in ('Wq', 'bq', 'Wk', 'bk', 'Wv', 'bv', 'Wo', 'bo')}
    del _L0_xattn_all

    def _L0_ffn_setup():
        import jax, jax.numpy as jnp
        import numpy as np
        D_MODEL = 256
        EXPERT_DIM = 512
        N_EXPERTS = 8
        LN_EPS = 1e-05

        def _bit_quant(W):
            scale = jnp.clip(jnp.mean(jnp.abs(W), axis=-1, keepdims=True), 1e-05, None)
            w_q = jnp.clip(jnp.round(W / scale), -1.0, 1.0) * scale
            return W + jax.lax.stop_gradient(w_q - W)
        key = jax.random.key(seed)
        ks = jax.random.split(key, 7)
        x = jax.random.normal(ks[0], (4, 512, D_MODEL), dtype=jnp.float32)
        shared_w1 = jax.random.normal(ks[1], (EXPERT_DIM, D_MODEL), dtype=jnp.float32) / np.sqrt(EXPERT_DIM)
        shared_w2 = jax.random.normal(ks[2], (D_MODEL, EXPERT_DIM), dtype=jnp.float32) / np.sqrt(D_MODEL)
        expert_w1 = jax.random.normal(ks[3], (N_EXPERTS, EXPERT_DIM, D_MODEL), dtype=jnp.float32) / np.sqrt(EXPERT_DIM)
        expert_w2 = jax.random.normal(ks[4], (N_EXPERTS, D_MODEL, EXPERT_DIM), dtype=jnp.float32) / np.sqrt(D_MODEL)
        router_w = 0.02 * jax.random.normal(ks[5], (N_EXPERTS, D_MODEL), dtype=jnp.float32)
        ln_gamma = jnp.ones((D_MODEL,), dtype=jnp.float32)
        ln_beta = jnp.zeros((D_MODEL,), dtype=jnp.float32)
        return {'x': x, 'shared_w1': shared_w1, 'shared_w2': shared_w2, 'expert_w1': expert_w1, 'expert_w2': expert_w2, 'router_w': router_w, 'ln_gamma': ln_gamma, 'ln_beta': ln_beta}
    _L0_ffn_all = _L0_ffn_setup()
    _L0_ffn_in = {k: v for k, v in _L0_ffn_all.items() if k in ('shared_w1', 'shared_w2', 'expert_w1', 'expert_w2', 'router_w', 'ln_gamma', 'ln_beta')}
    del _L0_ffn_all

    def _L1_xattn_setup():
        import jax, jax.numpy as jnp
        import numpy as np
        B, M, N, DIM, DH, H = (8, 1024, 64, 256, 128, 8)
        INNER = DH * H
        EPS = 1e-05

        def _layernorm(x, g, b):
            mu = jnp.mean(x, axis=-1, keepdims=True)
            var = jnp.var(x, axis=-1, keepdims=True)
            return (x - mu) * jax.lax.rsqrt(var + EPS) * g + b
        key = jax.random.key(seed)
        ks = jax.random.split(key, 8)
        sd = 0.02
        return {'x': jax.random.normal(ks[0], (B, M, DIM), jnp.float32), 'latents': jax.random.normal(ks[1], (B, N, DIM), jnp.float32), 'gamma_media': jnp.ones((DIM,), jnp.float32), 'beta_media': jnp.zeros((DIM,), jnp.float32), 'gamma_lat': jnp.ones((DIM,), jnp.float32), 'beta_lat': jnp.zeros((DIM,), jnp.float32), 'Wq': jax.random.normal(ks[2], (DIM, INNER), jnp.float32) * sd, 'bq': jnp.zeros((INNER,), jnp.float32), 'Wkv': jax.random.normal(ks[3], (DIM, 2 * INNER), jnp.float32) * sd, 'bkv': jnp.zeros((2 * INNER,), jnp.float32), 'Wo': jax.random.normal(ks[4], (INNER, DIM), jnp.float32) * sd, 'bo': jnp.zeros((DIM,), jnp.float32)}
    _L1_xattn_all = _L1_xattn_setup()
    _L1_xattn_in = {k: v for k, v in _L1_xattn_all.items() if k in ('gamma_media', 'beta_media', 'gamma_lat', 'beta_lat', 'Wq', 'bq', 'Wkv', 'bkv', 'Wo', 'bo')}
    del _L1_xattn_all

    def _L1_ffn_setup():
        import jax, jax.numpy as jnp
        import numpy as np
        import math
        B, T, C = (4, 512, 256)
        E, K = (8, 2)
        EH, SH = (512, 1024)
        CAP_FACTOR = 1.25
        SCALING = 1.0
        FC_MULT = 1.0

        def _capacity(N, k):
            avg = math.ceil(N * k / E)
            return max(int(math.ceil(avg * CAP_FACTOR)), 1)
        key = jax.random.key(seed)
        ks = jax.random.split(key, 6)
        sd = 0.02
        return {'x': jax.random.normal(ks[0], (B, T, C), jnp.float32), 'proj_w': jax.random.normal(ks[1], (E, C), jnp.float32) * sd, 'proj_b': jnp.zeros((E,), jnp.float32), 'expert_bias': jnp.zeros((E,), jnp.float32), 'fc1_w': jax.random.normal(ks[2], (E, EH, C), jnp.float32) * sd, 'fc1_b': jnp.zeros((E, EH), jnp.float32), 'fc2_w': jax.random.normal(ks[3], (E, C, EH), jnp.float32) * sd, 'fc2_b': jnp.zeros((E, C), jnp.float32), 'sh1_w': jax.random.normal(ks[4], (SH, C), jnp.float32) * sd, 'sh1_b': jnp.zeros((SH,), jnp.float32), 'sh2_w': jax.random.normal(ks[5], (C, SH), jnp.float32) * sd, 'sh2_b': jnp.zeros((C,), jnp.float32)}
    _L1_ffn_all = _L1_ffn_setup()
    _L1_ffn_in = {k: v for k, v in _L1_ffn_all.items() if k in ('proj_w', 'proj_b', 'expert_bias', 'fc1_w', 'fc1_b', 'fc2_w', 'fc2_b', 'sh1_w', 'sh1_b', 'sh2_w', 'sh2_b')}
    del _L1_ffn_all
    return {'x': x, 'ctx_1024': ctx_1024, 'g_xattn': g_xattn, 'g_ffn': g_ffn, 'L0_xattn_Wq': _L0_xattn_in['Wq'], 'L0_xattn_bq': _L0_xattn_in['bq'], 'L0_xattn_Wk': _L0_xattn_in['Wk'], 'L0_xattn_bk': _L0_xattn_in['bk'], 'L0_xattn_Wv': _L0_xattn_in['Wv'], 'L0_xattn_bv': _L0_xattn_in['bv'], 'L0_xattn_Wo': _L0_xattn_in['Wo'], 'L0_xattn_bo': _L0_xattn_in['bo'], 'L0_ffn_shared_w1': _L0_ffn_in['shared_w1'], 'L0_ffn_shared_w2': _L0_ffn_in['shared_w2'], 'L0_ffn_expert_w1': _L0_ffn_in['expert_w1'], 'L0_ffn_expert_w2': _L0_ffn_in['expert_w2'], 'L0_ffn_router_w': _L0_ffn_in['router_w'], 'L0_ffn_ln_gamma': _L0_ffn_in['ln_gamma'], 'L0_ffn_ln_beta': _L0_ffn_in['ln_beta'], 'L1_xattn_gamma_media': _L1_xattn_in['gamma_media'], 'L1_xattn_beta_media': _L1_xattn_in['beta_media'], 'L1_xattn_gamma_lat': _L1_xattn_in['gamma_lat'], 'L1_xattn_beta_lat': _L1_xattn_in['beta_lat'], 'L1_xattn_Wq': _L1_xattn_in['Wq'], 'L1_xattn_bq': _L1_xattn_in['bq'], 'L1_xattn_Wkv': _L1_xattn_in['Wkv'], 'L1_xattn_bkv': _L1_xattn_in['bkv'], 'L1_xattn_Wo': _L1_xattn_in['Wo'], 'L1_xattn_bo': _L1_xattn_in['bo'], 'L1_ffn_proj_w': _L1_ffn_in['proj_w'], 'L1_ffn_proj_b': _L1_ffn_in['proj_b'], 'L1_ffn_expert_bias': _L1_ffn_in['expert_bias'], 'L1_ffn_fc1_w': _L1_ffn_in['fc1_w'], 'L1_ffn_fc1_b': _L1_ffn_in['fc1_b'], 'L1_ffn_fc2_w': _L1_ffn_in['fc2_w'], 'L1_ffn_fc2_b': _L1_ffn_in['fc2_b'], 'L1_ffn_sh1_w': _L1_ffn_in['sh1_w'], 'L1_ffn_sh1_b': _L1_ffn_in['sh1_b'], 'L1_ffn_sh2_w': _L1_ffn_in['sh2_w'], 'L1_ffn_sh2_b': _L1_ffn_in['sh2_b']}

def reference(x, ctx_1024, g_xattn, g_ffn, L0_xattn_Wq, L0_xattn_bq, L0_xattn_Wk, L0_xattn_bk, L0_xattn_Wv, L0_xattn_bv, L0_xattn_Wo, L0_xattn_bo, L0_ffn_shared_w1, L0_ffn_shared_w2, L0_ffn_expert_w1, L0_ffn_expert_w2, L0_ffn_router_w, L0_ffn_ln_gamma, L0_ffn_ln_beta, L1_xattn_gamma_media, L1_xattn_beta_media, L1_xattn_gamma_lat, L1_xattn_beta_lat, L1_xattn_Wq, L1_xattn_bq, L1_xattn_Wkv, L1_xattn_bkv, L1_xattn_Wo, L1_xattn_bo, L1_ffn_proj_w, L1_ffn_proj_b, L1_ffn_expert_bias, L1_ffn_fc1_w, L1_ffn_fc1_b, L1_ffn_fc2_w, L1_ffn_fc2_b, L1_ffn_sh1_w, L1_ffn_sh1_b, L1_ffn_sh2_w, L1_ffn_sh2_b):
    import jax
    import jax.numpy as jnp

    def _L0_xattn_ref(q, k, v, Wq, bq, Wk, bk, Wv, bv, Wo, bo):
        import jax, jax.numpy as jnp
        import numpy as np
        EMB = 256
        HID = 256
        HEADS = 16
        HEAD_DIM = HID // HEADS

        def _split_heads(x):
            B, S, H = x.shape
            return x.reshape(B, S, HEADS, H // HEADS).transpose(0, 2, 1, 3)
        qh = _split_heads(q @ Wq + bq)
        kh = _split_heads(k @ Wk + bk)
        vh = _split_heads(v @ Wv + bv)
        scale = 1.0 / jnp.sqrt(jnp.asarray(HEAD_DIM, qh.dtype))
        scores = jnp.einsum('bhqd,bhkd->bhqk', qh, kh) * scale
        attn = jax.nn.softmax(scores, axis=-1)
        out = jnp.einsum('bhqk,bhkd->bhqd', attn, vh)
        B, _, S, _ = out.shape
        out = out.transpose(0, 2, 1, 3).reshape(B, S, HID)
        return out @ Wo + bo

    def _L0_ffn_ref(x, shared_w1, shared_w2, expert_w1, expert_w2, router_w, ln_gamma, ln_beta):
        import jax, jax.numpy as jnp
        import numpy as np
        D_MODEL = 256
        EXPERT_DIM = 512
        N_EXPERTS = 8
        LN_EPS = 1e-05

        def _bit_quant(W):
            scale = jnp.clip(jnp.mean(jnp.abs(W), axis=-1, keepdims=True), 1e-05, None)
            w_q = jnp.clip(jnp.round(W / scale), -1.0, 1.0) * scale
            return W + jax.lax.stop_gradient(w_q - W)
        mu = jnp.mean(x, axis=-1, keepdims=True)
        var = jnp.mean(jnp.square(x - mu), axis=-1, keepdims=True)
        h = (x - mu) / jnp.sqrt(var + LN_EPS) * ln_gamma + ln_beta
        sw1, sw2 = (_bit_quant(shared_w1), _bit_quant(shared_w2))
        shared_out = jax.nn.silu(jnp.einsum('btd,fd->btf', h, sw1)) @ sw2.T
        probs = jax.nn.softmax(h @ router_w.T, axis=-1)
        top_prob = jnp.max(probs, axis=-1)
        top_idx = jnp.argmax(probs, axis=-1)
        ew1, ew2 = (_bit_quant(expert_w1), _bit_quant(expert_w2))
        h1 = jax.nn.silu(jnp.einsum('btd,efd->ebtf', h, ew1))
        eo = jnp.einsum('ebtf,edf->ebtd', h1, ew2)
        gate = jax.nn.one_hot(top_idx, N_EXPERTS, dtype=h.dtype) * top_prob[..., None]
        routed_out = jnp.einsum('ebtd,bte->btd', eo, gate)
        return shared_out + routed_out

    def _L1_xattn_ref(x, latents, gamma_media, beta_media, gamma_lat, beta_lat, Wq, bq, Wkv, bkv, Wo, bo):
        import jax, jax.numpy as jnp
        import numpy as np
        B, M, N, DIM, DH, H = (8, 1024, 64, 256, 128, 8)
        INNER = DH * H
        EPS = 1e-05

        def _layernorm(x, g, b):
            mu = jnp.mean(x, axis=-1, keepdims=True)
            var = jnp.var(x, axis=-1, keepdims=True)
            return (x - mu) * jax.lax.rsqrt(var + EPS) * g + b
        b = x.shape[0]
        xn = _layernorm(x, gamma_media, beta_media)
        ln = _layernorm(latents, gamma_lat, beta_lat)
        q = ln @ Wq + bq
        kv_input = jnp.concatenate([xn, ln], axis=1)
        kv = kv_input @ Wkv + bkv
        k, v = jnp.split(kv, 2, axis=-1)

        def to_heads(t):
            return t.reshape(b, t.shape[1], H, DH).transpose(0, 2, 1, 3)
        q, k, v = (to_heads(q), to_heads(k), to_heads(v))
        q = q * DH ** (-0.5)
        sim = jnp.einsum('bhid,bhjd->bhij', q, k)
        attn = jax.nn.softmax(sim, axis=-1)
        out = jnp.einsum('bhij,bhjd->bhid', attn, v)
        out = out.transpose(0, 2, 1, 3).reshape(b, -1, INNER)
        return out @ Wo + bo

    def _L1_ffn_ref(x, proj_w, proj_b, expert_bias, fc1_w, fc1_b, fc2_w, fc2_b, sh1_w, sh1_b, sh2_w, sh2_b):
        import jax, jax.numpy as jnp
        import numpy as np
        import math
        B, T, C = (4, 512, 256)
        E, K = (8, 2)
        EH, SH = (512, 1024)
        CAP_FACTOR = 1.25
        SCALING = 1.0
        FC_MULT = 1.0

        def _capacity(N, k):
            avg = math.ceil(N * k / E)
            return max(int(math.ceil(avg * CAP_FACTOR)), 1)
        Bx, Tx, Cx = x.shape
        N = Bx * Tx
        xf = x.reshape(N, Cx)
        z = xf @ proj_w.T + proj_b
        s = jax.nn.sigmoid(z) + expert_bias
        logits = jnp.log(jnp.clip(s, 1e-12)) * SCALING
        probs = jax.nn.softmax(logits, axis=-1)
        topk_w, topk_idx = jax.lax.top_k(probs, K)
        topk_w = topk_w / jnp.clip(topk_w.sum(-1, keepdims=True), 1e-12)
        pair_e = topk_idx.reshape(-1)
        pair_w = topk_w.reshape(-1)
        pair_tok = jnp.repeat(jnp.arange(N), K)
        cap = _capacity(N, K)
        assigned = pair_e[None, :] == jnp.arange(E)[:, None]
        wmat = jnp.where(assigned, pair_w[None, :], -jnp.inf)
        kept_w, kept_pair = jax.lax.top_k(wmat, cap)
        valid = kept_w > -jnp.inf
        kept_w = jnp.where(valid, kept_w, 0.0)
        kept_tok = pair_tok[kept_pair]
        xe = xf[kept_tok]
        h = jax.nn.gelu(jnp.einsum('ecd,ehd->ech', xe, fc1_w) + fc1_b[:, None, :], approximate=False)
        oe = jnp.einsum('ech,edh->ecd', h, fc2_w) + fc2_b[:, None, :]
        contrib = oe * kept_w[..., None]
        y = jnp.zeros((N, Cx), x.dtype).at[kept_tok.reshape(-1)].add(contrib.reshape(-1, Cx))
        sh = jax.nn.gelu(xf @ sh1_w.T + sh1_b, approximate=False) @ sh2_w.T + sh2_b
        return ((sh + y) * FC_MULT).reshape(Bx, Tx, Cx)
    x = x + jnp.tanh(g_xattn[0]) * _L0_xattn_ref(_layernorm(x, axis=-1), ctx_1024, ctx_1024, L0_xattn_Wq, L0_xattn_bq, L0_xattn_Wk, L0_xattn_bk, L0_xattn_Wv, L0_xattn_bv, L0_xattn_Wo, L0_xattn_bo)
    x = x + jnp.tanh(g_ffn[0]) * _L0_ffn_ref(_layernorm(x, axis=-1), L0_ffn_shared_w1, L0_ffn_shared_w2, L0_ffn_expert_w1, L0_ffn_expert_w2, L0_ffn_router_w, L0_ffn_ln_gamma, L0_ffn_ln_beta)
    x = x + jnp.tanh(g_xattn[1]) * _L1_xattn_ref(ctx_1024, _layernorm(x, axis=-1), L1_xattn_gamma_media, L1_xattn_beta_media, L1_xattn_gamma_lat, L1_xattn_beta_lat, L1_xattn_Wq, L1_xattn_bq, L1_xattn_Wkv, L1_xattn_bkv, L1_xattn_Wo, L1_xattn_bo)
    x = x + jnp.tanh(g_ffn[1]) * _L1_ffn_ref(_layernorm(x, axis=-1), L1_ffn_proj_w, L1_ffn_proj_b, L1_ffn_expert_bias, L1_ffn_fc1_w, L1_ffn_fc1_b, L1_ffn_fc2_w, L1_ffn_fc2_b, L1_ffn_sh1_w, L1_ffn_sh1_b, L1_ffn_sh2_w, L1_ffn_sh2_b)
    return x

_drawn_inputs = setup_inputs


def setup_inputs(seed=0):
    import zlib

    import numpy as np

    out = dict(_drawn_inputs(seed))
    spreads = {'g_ffn': (-1.0, 0.6),
     'L0_xattn_bq': (0.0, 0.8),
     'L0_xattn_bk': (0.0, 2.0),
     'L0_xattn_bv': (0.0, 0.295),
     'L0_xattn_bo': (0.0, 0.1),
     'L0_ffn_ln_gamma': (1.0, 0.2),
     'L0_ffn_ln_beta': (0.0, 0.372),
     'L1_xattn_gamma_media': (1.0, 0.6),
     'L1_xattn_beta_media': (0.0, 0.746),
     'L1_xattn_gamma_lat': (1.0, 0.6),
     'L1_xattn_beta_lat': (0.0, 0.793),
     'L1_xattn_bq': (0.0, 2.0),
     'L1_xattn_bkv': (0.0, 0.1),
     'L1_xattn_bo': (0.0, 0.1),
     'L1_ffn_proj_b': (0.0, 0.267),
     'L1_ffn_expert_bias': (0.0, 0.1),
     'L1_ffn_fc1_b': (0.0, 0.725),
     'L1_ffn_fc2_b': (0.0, 0.1),
     'L1_ffn_sh1_b': (0.0, 0.306),
     'L1_ffn_sh2_b': (0.0, 0.1)}
    factors = {'L0_xattn_Wq': 8.0, 'L0_xattn_Wk': 8.0, 'L1_xattn_Wq': 8.0}
    for name, (base, spread) in spreads.items():
        noise = np.random.default_rng([zlib.crc32(name.encode()), seed]).standard_normal(out[name].shape)
        drawn = base * np.exp(spread * noise) if base else spread * noise
        out[name] = jnp.asarray(drawn.astype(out[name].dtype))
    for name, factor in factors.items():
        out[name] = (out[name] * factor).astype(out[name].dtype)
    return out
```

```python
from contextlib import ExitStack

import concourse.bass as bass
from concourse import mybir

F32 = mybir.dt.float32
F32R = mybir.dt.float32r
BF16 = mybir.dt.bfloat16
I32 = mybir.dt.int32
U32 = mybir.dt.uint32
ALU = mybir.AluOpType
ACT = mybir.ActivationFunctionType
AX = mybir.AxisListType

P = 128
LN_EPS = 1e-5


def recycle(nc):
    used = sorted(x for x in nc.released_uncleared_semaphores)
    with nc.Block() as block:
        @block.gpsimd
        def _(pool):
            start = 0
            for n in range(1, len(used) + 1):
                if n == len(used) or used[n] != used[n - 1] + 1:
                    pool.sem_clear(range(used[start], used[n - 1] + 1))
                    start = n


class Steps:

    def __init__(self, eng, sem, base=0):
        self.eng, self.sem, self.base, self.n = eng, sem, base, 0

    def step(self, ins):
        ins.then_inc(self.sem, 1)
        self.n += 1
        self.eng.wait_ge(self.sem, self.base + self.n)


def rsqrt_steps(dve, s, y, v, a, b):
    vi, ai = v.bitcast(I32), a.bitcast(I32)
    s.step(dve.tensor_scalar(ai, vi, 1, None, ALU.logical_shift_right))
    s.step(dve.tensor_scalar(y.bitcast(I32), ai, -1.0, float(0x5F3759DF), ALU.mult, ALU.add))
    for _ in range(4):
        s.step(dve.tensor_tensor(a, y, y, ALU.mult))
        s.step(dve.tensor_tensor(b, a, v, ALU.mult))
        s.step(dve.tensor_scalar(a, b, -0.5, 1.5, ALU.mult, ALU.add))
        s.step(dve.tensor_tensor(y, y, a, ALU.mult))


def norm_steps(dve, s, stats, mean, rstd, tmp, twice):
    a, b, v = tmp
    s.step(dve.tensor_tensor(mean, stats[:, :, 1], stats[:, :, 4], ALU.add))
    s.step(dve.tensor_scalar(mean, mean, 0.5, None, ALU.mult))
    s.step(dve.tensor_tensor(a, stats[:, :, 1], stats[:, :, 4], ALU.subtract))
    s.step(dve.scalar_tensor_tensor(out=b, in0=a, scalar=0.25, in1=a, op0=ALU.mult, op1=ALU.mult))
    s.step(dve.tensor_tensor(a, stats[:, :, 2], stats[:, :, 5], ALU.add))
    s.step(dve.scalar_tensor_tensor(out=v, in0=a, scalar=1.0 / 256, in1=b, op0=ALU.mult, op1=ALU.add))
    s.step(dve.tensor_scalar(a, v, LN_EPS, None, ALU.add))
    if not twice:
        s.step(dve.tensor_copy(v, a))
        rsqrt_steps(dve, s, rstd, v, a, b)
        return
    s.step(dve.scalar_tensor_tensor(out=v, in0=a, scalar=LN_EPS, in1=v, op0=ALU.mult, op1=ALU.add))
    rsqrt_steps(dve, s, rstd, v, a, b)


def program(nc, A, out):
    NB, S, D = A["x"].shape
    assert S == P and D == 256
    KD = D // P
    ctx = ExitStack()

    def sb(name, shape, dt=F32, where=ctx):
        return where.enter_context(nc.sbuf_tensor(name, shape, dt))

    def ps(name, shape, dt=F32, where=ctx):
        return where.enter_context(nc.psum_tensor(name, shape, dt))

    def sem(name, where=ctx):
        return where.enter_context(nc.semaphore(name))

    with ctx:
        x_sb = sb("x_sb", [P, NB, D])
        ctx_sb = sb("ctx_sb", [P, NB, D])
        ident = sb("ident", [P, P])
        gates = sb("gates", [P, 4])
        x_mean, x_rstd = sb("x_mean", [P, NB]), sb("x_rstd", [P, NB])
        c_mean, c_rstd = sb("c_mean", [P, NB]), sb("c_rstd", [P, NB])
        x_stats, c_stats = sb("x_stats", [P, NB, 6]), sb("c_stats", [P, NB, 6])
        nt = [sb(f"norm_tmp{i}", [P, NB]) for i in range(3)]
        g = dict(nc=nc, A=A, sb=sb, ps=ps, sem=sem, NB=NB, D=D, KD=KD, x_sb=x_sb, ctx_sb=ctx_sb, ident=ident,
                 gates=gates, x_mean=x_mean, x_rstd=x_rstd, c_mean=c_mean, c_rstd=c_rstd,
                 x_stats=x_stats, c_stats=c_stats, nt=nt)
        attention_0(**g)
        mixture_0(**g)
        attention_1(**g)
        recycle(nc)
        mixture_1(**g)
        out_done = sem("out_done")
        with nc.Block() as block:
            @block.sync
            def _(sp):
                sp.dma_start(out.rearrange("b p d -> p b d"), x_sb[:]).then_inc(out_done, 16)
                sp.wait_ge(out_done, 16)


def attention_0(nc, A, sb, ps, sem, NB, D, KD, x_sb, ctx_sb, ident, gates, x_mean, x_rstd, c_mean, c_rstd,
                x_stats, c_stats, nt):
    NH = 16
    HD = D // NH
    NG = 4
    with ExitStack() as c:
        W = {n: sb(f"a0_w{n}", [P, KD, D], F32, c) for n in "qkvo"}
        bq, bk = sb("a0_bq", [P, KD], F32, c), sb("a0_bk", [P, KD], F32, c)
        bv, bo = sb("a0_bv", [P, D], F32, c), sb("a0_bo", [P, D], F32, c)
        pidx = sb("a0_pidx", [P, 1], I32, c)
        mask = sb("a0_mask", [P, 2], F32, c)
        cst = sb("a0_cst", [P, D], F32, c)
        xn = sb("a0_xn", [P, D], F32, c)
        xcT = sb("a0_xcT", [P, 4, P], F32, c)
        qm = sb("a0_qm", [P, 2, 2, P], F32, c)
        kT = sb("a0_kT", [P, 2, P], F32, c)
        v = sb("a0_v", [P, D], F32, c)
        nmax = sb("a0_nmax", [P, NH], F32, c)
        probs = sb("a0_probs", [P, NH, P], F32, c)
        sums, rsum = sb("a0_sums", [P, NH], F32, c), sb("a0_rsum", [P, NH], F32, c)
        pT = sb("a0_pT", [P, NH, P], F32, c)
        o = sb("a0_o", [P, D], F32, c)
        oT = sb("a0_oT", [P, 2, P], F32, c)
        psS = [ps(f"a0_psS{j}", [P, NG, P], F32, c) for j in range(NG)]
        psT = [ps(f"a0_psT{j}", [P, NG, P], F32, c) for j in range(2)]
        psM0 = ps("a0_psM0", [P, 512], F32, c)
        psM1 = ps("a0_psM1", [P, 512], F32, c)
        names = ("x_in w_in small_in gates_done dve_steps ident_zero ident_done pidx_done bo_done stats_done xn_done cst_done "
                 "resid_done tx_done txc_done qk_done v_done qm_done kT_done vs_done s_done max_done exp_done "
                 "rsum_done t_done tcA_done tcV_done pv_done o_done ot_done oTc_done y_done x_done").split()
        s = {n: sem(f"a0_{n}", c) for n in names}

        def head(j, slot):
            m, parity = divmod(slot, 2)
            return m * 8 + 2 * j + parity

        with nc.Block() as block:
            @block.sync
            def _(sp):
                sp.dma_start(x_sb[:], A["x"].rearrange("b p d -> p b d")).then_inc(s["x_in"], 16)
                for n, key in (("q", "Wq"), ("k", "Wk"), ("v", "Wv"), ("o", "Wo")):
                    sp.dma_start(W[n][:], A["L0_xattn_" + key].rearrange("(k p) n -> p k n", p=P)).then_inc(s["w_in"], 16)

            @block.gpsimd
            def _(pool):
                pool.memset(ident[:], 0.0).then_inc(s["ident_zero"], 1)
                pool.iota(pidx[:], pattern=[[0, 1]], base=0, channel_multiplier=1).then_inc(s["pidx_done"], 1)
                pool.wait_ge(s["ident_zero"], 1)
                pool.affine_select(out=ident[:], in_=ident[:], compare_op=ALU.not_equal, fill=1.0, base=0,
                                   pattern=[[-1, P]], channel_multiplier=1).then_inc(s["ident_done"], 1)
                pool.wait_ge(s["bo_done"], 1)
                pool.wait_ge(s["x_in"], 32)

                def stage_context(i, first):
                    if not first:
                        pool.wait_ge(s["tx_done"], i)
                    pool.tensor_copy(cst[:], ctx_sb[:, i, :]).then_inc(s["cst_done"], 1)

                def residual(i):
                    pool.wait_ge(s["xn_done"], i + 1)
                    pool.tensor_tensor(x_sb[:, i, :], x_sb[:, i, :], bo[:], ALU.add).then_inc(s["resid_done"], 1)

                stage_context(0, True)
                with pool.Fori(1, NB) as i:
                    residual(i - 1)
                    stage_context(i, False)
                residual(NB - 1)

            @block.scalar
            def _(act):
                for dst, src in ((bq[:], A["L0_xattn_bq"].rearrange("(k p) -> p k", p=P)),
                                 (bk[:], A["L0_xattn_bk"].rearrange("(k p) -> p k", p=P)),
                                 (bv[:], A["L0_xattn_bv"].partition_broadcast(P)),
                                 (bo[:], A["L0_xattn_bo"].partition_broadcast(P)),
                                 (gates[:, 0:2], A["g_xattn"].partition_broadcast(P)),
                                 (gates[:, 2:4], A["g_ffn"].partition_broadcast(P))):
                    with nc.allow_non_contiguous_dma(reason="a few hundred small parameters"):
                        act.dma_start(dst, src).then_inc(s["small_in"], 16)
                act.dma_start(ctx_sb[:], A["ctx_1024"].rearrange("b p d -> p b d")).then_inc(s["x_in"], 16)
                act.wait_ge(s["small_in"], 96)
                act.activation(gates[:], gates[:], ACT.Tanh).then_inc(s["gates_done"], 1)

                def front(i, first):
                    if not first:
                        act.wait_ge(s["v_done"], i)
                    act.wait_ge(s["tx_done"], i + 1)
                    act.activation(xcT[:], psM0[:].rearrange("p (a t) -> p a t", a=4), ACT.Copy).then_inc(s["txc_done"], 1)

                def copies(i):
                    for gr in (0, 2):
                        act.wait_ge(s["t_done"], i * 4 + gr + 1)
                        if gr == 0:
                            act.wait_ge(s["exp_done"], i * 16 + 16)
                        act.activation(pT[:, 4 * gr:4 * gr + 4, :], psT[0][:], ACT.Copy).then_inc(s["tcA_done"], 1)

                def keys(i):
                    act.wait_ge(s["qm_done"], i + 1)
                    for m in range(2):
                        ins = act.activation(kT[:, m, :], psM1[:, (2 + m) * P:(3 + m) * P], ACT.Identity, bias=bk[:, m:m + 1])
                    ins.then_inc(s["kT_done"], 1)

                def exps(i, js):
                    for j in js:
                        act.wait_ge(s["max_done"], i * 4 + j + 1)
                        for slot in range(NG):
                            act.activation(probs[:, 4 * j + slot, :], psS[j][:, slot, :], ACT.Exp,
                                           bias=nmax[:, 4 * j + slot:4 * j + slot + 1],
                                           accum_out=sums[:, 4 * j + slot:4 * j + slot + 1]).then_inc(s["exp_done"], 1)

                def heads_turned(i):
                    act.wait_ge(s["ot_done"], i + 1)
                    act.activation(oT[:], psM1[:, 0:2 * P].rearrange("p (a t) -> p a t", a=2), ACT.Copy).then_inc(s["oTc_done"], 1)

                front(0, True)
                keys(0)
                exps(0, range(4))
                with act.Fori(1, NB) as i:
                    front(i, False)
                    copies(i - 1)
                    keys(i)
                    exps(i, [0])
                    heads_turned(i - 1)
                    exps(i, [1, 2, 3])
                copies(NB - 1)
                heads_turned(NB - 1)

            @block.vector
            def _(dve):
                k = Steps(dve, s["dve_steps"])
                dve.wait_ge(s["pidx_done"], 1)
                k.step(dve.tensor_scalar(pidx[:], pidx[:], 16, None, ALU.bitwise_and))
                k.step(dve.tensor_scalar(mask[:, 1:2], pidx[:], 1.0 / 64, None, ALU.mult))
                k.step(dve.tensor_scalar(mask[:, 0:1], mask[:, 1:2], -1.0, 0.25, ALU.mult, ALU.add))
                dve.wait_ge(s["gates_done"], 1)
                dve.tensor_scalar(bo[:], bo[:], gates[:, 0:1], None, ALU.mult).then_inc(s["bo_done"], 1)
                dve.wait_ge(s["x_in"], 32)
                for j in range(NB):
                    ins = dve.bn_stats(x_stats[:, j, :], x_sb[:, j, :])
                k.step(ins)
                norm_steps(dve, k, x_stats, x_mean[:], x_rstd[:], [t[:] for t in nt], False)

                def front(i, first):
                    if not first:
                        dve.wait_ge(s["tx_done"], i)
                    dve.tensor_scalar(xn[:], x_sb[:, i, :], x_mean[:, bass.ds(i, 1)], x_rstd[:, bass.ds(i, 1)],
                                      ALU.subtract, ALU.mult).then_inc(s["xn_done"], 1)

                def copies(i):
                    for gr in (1, 3):
                        dve.wait_ge(s["t_done"], i * 4 + gr + 1)
                        dve.tensor_copy(pT[:, 4 * gr:4 * gr + 4, :], psT[1][:]).then_inc(s["tcV_done"], 1)

                def queries(i):
                    dve.wait_ge(s["qk_done"], i + 1)
                    for m in range(2):
                        for par in range(2):
                            ins = dve.tensor_scalar(qm[:, m, par, :], psM1[:, m * P:(m + 1) * P], bq[:, m:m + 1],
                                                    mask[:, par:par + 1], ALU.add, ALU.mult)
                    ins.then_inc(s["qm_done"], 1)

                def recip(i):
                    dve.wait_ge(s["exp_done"], i * 16 + 16)
                    dve.reciprocal(rsum[:], sums[:]).then_inc(s["rsum_done"], 1)

                def values(i, first):
                    dve.wait_ge(s["v_done"], i + 1)
                    if not first:
                        dve.wait_ge(s["pv_done"], i)
                    dve.tensor_tensor(v[:], psM0[:, 0:D], bv[:], ALU.add).then_inc(s["vs_done"], 1)

                def normalize(i):
                    dve.wait_ge(s["rsum_done"], i + 1)
                    dve.wait_ge(s["pv_done"], i + 1)
                    dve.tensor_tensor(o[:].rearrange("p (h d) -> p h d", h=NH), psM0[:, D:2 * D].rearrange("p (h d) -> p h d", h=NH),
                                      rsum_by_head, ALU.mult).then_inc(s["o_done"], 1)

                def maxima(i):
                    for j in range(4):
                        dve.wait_ge(s["s_done"], i * 4 + j + 1)
                        dve.tensor_reduce(nmax[:, 4 * j:4 * j + 4], psS[j][:], AX.X, ALU.max, negate=True)\
                           .then_inc(s["max_done"], 1)

                def residual(i):
                    dve.wait_ge(s["y_done"], i + 1)
                    dve.wait_ge(s["resid_done"], i + 1)
                    dve.scalar_tensor_tensor(out=x_sb[:, i, :], in0=psM1[:, D:2 * D], scalar=gates[:, 0:1],
                                             in1=x_sb[:, i, :], op0=ALU.mult, op1=ALU.add).then_inc(s["x_done"], 1)

                rsum_by_head = rsum[:].unsqueeze(2).to_broadcast([P, NH, D // NH])
                front(0, True)
                queries(0)
                values(0, True)
                maxima(0)
                with dve.Fori(1, NB) as i:
                    front(i, False)
                    copies(i - 1)
                    queries(i)
                    recip(i - 1)
                    values(i, False)
                    normalize(i - 1)
                    maxima(i)
                    residual(i - 1)
                copies(NB - 1)
                recip(NB - 1)
                normalize(NB - 1)
                residual(NB - 1)

            @block.tensor
            def _(pe):
                def turn_in(i, first=False, second=False):
                    pe.wait_ge(s["xn_done"], i + 1)
                    pe.wait_ge(s["cst_done"], i + 1)
                    if not first:
                        pe.wait_ge(s["vs_done"], i)
                        if not second:
                            pe.wait_ge(s["o_done"], i - 1)
                    for a in range(KD):
                        pe.transpose(psM0[:, a * P:(a + 1) * P], xn[:, a * P:(a + 1) * P], ident[:])
                    for a in range(KD):
                        ins = pe.transpose(psM0[:, (2 + a) * P:(3 + a) * P], cst[:, a * P:(a + 1) * P], ident[:])
                    ins.then_inc(s["tx_done"], 1)

                def turn_probs(i):
                    pe.wait_ge(s["exp_done"], i * 16 + 16)
                    for gr in range(4):
                        if gr == 2:
                            pe.wait_ge(s["tcA_done"], i * 2 + 1)
                        if gr == 3:
                            pe.wait_ge(s["tcV_done"], i * 2 + 1)
                        for h in range(4):
                            ins = pe.transpose(psT[gr % 2][:, h, :], probs[:, 4 * gr + h, :], ident[:])
                        ins.then_inc(s["t_done"], 1)

                def project(i, first=False, second=False):
                    pe.wait_ge(s["txc_done"], i + 1)
                    if not first:
                        if not second:
                            pe.wait_ge(s["x_done"], i - 1)
                    for b, (w, src) in enumerate((("q", 0), ("q", 0), ("k", 2), ("k", 2))):
                        for a in range(KD):
                            m = b % 2
                            ins = pe.matmul(psM1[:, b * P:(b + 1) * P], W[w][:, a, m * P:(m + 1) * P], xcT[:, src + a, :],
                                            start=(a == 0), stop=(a == KD - 1))
                    ins.then_inc(s["qk_done"], 1)
                    for a in range(KD):
                        ins = pe.matmul(psM0[:, 0:D], xcT[:, 2 + a, :], W["v"][:, a, :], start=(a == 0), stop=(a == KD - 1))
                    ins.then_inc(s["v_done"], 1)

                def weigh(i):
                    pe.wait_ge(s["vs_done"], i + 1)
                    pe.wait_ge(s["tcA_done"], i * 2 + 2)
                    pe.wait_ge(s["tcV_done"], i * 2 + 2)
                    for n in range(NH):
                        h = head(*divmod(n, 4))
                        ins = pe.matmul(psM0[:, D + n * HD:D + (n + 1) * HD], pT[:, n, :], v[:, h * HD:(h + 1) * HD],
                                        start=True, stop=True)
                    ins.then_inc(s["pv_done"], 1)

                def scores(i):
                    pe.wait_ge(s["qm_done"], i + 1)
                    pe.wait_ge(s["kT_done"], i + 1)
                    for slot in range(4):
                        m, par = divmod(slot, 2)
                        for j in range(4):
                            r = slice(32 * j, 32 * j + 32)
                            ins = pe.matmul(psS[j][:, slot, :], qm[r, m, par, :], kT[r, m, :], start=True, stop=True)
                            if slot == 3:
                                ins.then_inc(s["s_done"], 1)

                def output(i):
                    pe.wait_ge(s["o_done"], i + 1)
                    for a in range(KD):
                        ins = pe.transpose(psM1[:, a * P:(a + 1) * P], o[:, a * P:(a + 1) * P], ident[:])
                    ins.then_inc(s["ot_done"], 1)
                    pe.wait_ge(s["oTc_done"], i + 1)
                    for a in range(KD):
                        ins = pe.matmul(psM1[:, D:2 * D], oT[:, a, :], W["o"][:, a, :], start=(a == 0), stop=(a == KD - 1))
                    ins.then_inc(s["y_done"], 1)

                pe.wait_ge(s["ident_done"], 1)
                pe.wait_ge(s["w_in"], 64)
                turn_in(0, True)
                project(0, True)
                scores(0)

                def both(i, second=False):
                    turn_in(i, second=second)
                    turn_probs(i - 1)
                    project(i, second=second)
                    weigh(i - 1)
                    scores(i)
                    output(i - 1)

                both(1, second=True)
                with pe.Fori(2, NB) as i:
                    both(i)
                turn_probs(NB - 1)
                weigh(NB - 1)
                output(NB - 1)


def prefix_steps(dve, s, src, bufs, n):
    a, b = src, bufs[0]
    shift, turn = 1, 0
    while shift < n:
        dve.tensor_copy(b[:, 0:shift], a[:, 0:shift])
        s.step(dve.tensor_tensor(b[:, shift:n], a[:, shift:n], a[:, 0:n - shift], ALU.add))
        turn += 1
        a, b = b, bufs[turn % 2]
        shift *= 2
    return a


def mixture_0(nc, A, sb, ps, sem, NB, D, KD, x_sb, ctx_sb, ident, gates, x_mean, x_rstd, c_mean, c_rstd,
              x_stats, c_stats, nt):
    NE = A["L0_ffn_expert_w1"].shape[0]
    F = A["L0_ffn_expert_w1"].shape[1]
    KF = F // P
    NT = NB + NE
    SH = NE
    xg = nc.dram_tensor("m0_sorted", (NT * P, D), F32, kind="Internal").ap()
    yg = nc.dram_tensor("m0_expert_out", (NT * P, D), F32, kind="Internal").ap()
    with ExitStack() as c:
        w1t = sb("m0_w1t", [P, NE + 1, KD, F], F32R, c)
        w2t = sb("m0_w2t", [P, NE + 1, KF, D], F32R, c)
        s1 = sb("m0_s1", [P, NE + 1, KF], F32, c)
        s2 = sb("m0_s2", [P, NE + 1, D], F32, c)
        logits = sb("m0_logits", [P, NB, NE], F32, c)
        prob = sb("m0_prob", [P, NB], F32, c)
        pos = sb("m0_pos", [P, NB], U32, c)
        owner = sb("m0_owner", [P, NT], I32, c)
        gamma, beta = sb("m0_gamma", [P, KD], F32, c), sb("m0_beta", [P, KD], F32, c)
        router = sb("m0_router", [P, KD, NE], F32, c)
        zeros = sb("m0_zeros", [P, D], F32, c)
        ones = sb("m0_ones", [P, P], F32, c)
        upper = sb("m0_upper", [P, P], F32, c)
        scattered = sem("m0_scattered", c)
        ternary_weights(nc, A, sb, ps, sem, NE, F, KF, KD, D, w1t, w2t, s1, s2, ident, ones, zeros, xg,
                        gamma, beta, router, upper)
        n_sb = sb("m0_n", [P, NB, D], F32, c)
        sh = sb("m0_shared", [P, NB, D], F32, c)
        with ExitStack() as turned:
            hT = [sb(f"m0_hT{n}", [P, KD, NB, P], F32R, turned) for n in ("hi", "lo")]
            token_norms(nc, sb, ps, sem, NB, D, KD, x_sb, ident, x_mean, x_rstd, x_stats, nt, n_sb, hT,
                        logits, router, gamma, beta, NE, "m0", True)
            route_top1(nc, sb, ps, sem, NB, NE, NT, D, logits, prob, pos, owner, ones, upper, gates)
            shared_ternary(nc, sb, ps, sem, NB, D, KD, KF, SH, hT, w1t, w2t, s1, sh, n_sb, pos, xg, scattered)
        expert_tiles(nc, sb, ps, sem, NB, NT, D, KD, KF, SH, x_sb, sh, s2, s1, w1t, w2t, gamma, beta, ident, owner,
                     xg, yg, n_sb, pos, prob, gates, scattered, x_stats)


def ternary_weights(nc, A, sb, ps, sem, NE, F, KF, KD, D, w1t, w2t, s1, s2, ident, ones, zeros, xg,
                    gamma, beta, router, upper):
    with ExitStack() as c:
        raw1 = [sb(f"t_raw1_{i}", [P, KF, D], F32, c) for i in range(2)]
        raw2 = [sb(f"t_raw2_{i}", [P, KD, F], F32, c) for i in range(2)]
        identb = sb("t_identb", [P, P], BF16, c)
        mag = sb("t_mag", [P, KF + KD], F32, c)
        thr, nthr = sb("t_thr", [P, KF + KD], F32, c), sb("t_nthr", [P, KF + KD], F32, c)
        neg = sb("t_neg", [P, KF * D + KD * F], BF16, c)
        tern = sb("t_tern", [P, KF * D + KD * F], BF16, c)
        diag = sb("t_diag", [P, KD, P], F32, c)
        psA = [ps(f"t_ps{i}", [P, 8, P], BF16, c) for i in range(2)]
        psB = ps("t_psB", [P, D], F32, c)
        names = ("const_done upper_zero raw0 raw1 small_in zero_out steps mag_done tern_done turned1 turned2 spread "
                 "w1_done w2_done s2_done").split()
        s = {n: sem(f"t_{n}", c) for n in names}
        raw_in = [s["raw0"], s["raw1"]]

        def source(e):
            if isinstance(e, int) and e == NE:
                return A["L0_ffn_shared_w1"], A["L0_ffn_shared_w2"]
            return A["L0_ffn_expert_w1"][e], A["L0_ffn_expert_w2"][e]

        with nc.Block() as block:
            @block.sync
            def _(sp):
                with nc.allow_non_contiguous_dma(reason="a few hundred small parameters"):
                    sp.dma_start(gamma[:], A["L0_ffn_ln_gamma"].rearrange("(k p) -> p k", p=P)).then_inc(s["small_in"], 16)
                    sp.dma_start(beta[:], A["L0_ffn_ln_beta"].rearrange("(k p) -> p k", p=P)).then_inc(s["small_in"], 16)
                    sp.dma_start(router[:], A["router_T"].rearrange("(k p) e -> p k e", p=P)).then_inc(s["small_in"], 16)

                def load(e, buf):
                    a, b = source(e)
                    sp.dma_start(raw1[buf][:], a.rearrange("(t p) d -> p t d", p=P)).then_inc(raw_in[buf], 16)
                    sp.dma_start(raw2[buf][:], b.rearrange("(t p) f -> p t f", p=P)).then_inc(raw_in[buf], 16)

                load(NE, 0)
                load(0, 1)
                sp.wait_ge(s["const_done"], 2)
                sp.dma_start(xg.rearrange("(t p) d -> p t d", p=P), zeros[:].unsqueeze(1).to_broadcast([P, xg.shape[0] // P, D]))\
                  .then_inc(s["zero_out"], 16)
                with sp.Fori(0, NE // 2 - 1) as i:
                    for half in range(2):
                        sp.wait_ge(s["tern_done"], i * 2 + half + 1)
                        load(i * 2 + half + 1, half)
                sp.wait_ge(s["tern_done"], NE - 1)
                load(NE - 1, 0)
                sp.wait_ge(s["zero_out"], 16)
                sp.wait_ge(s["small_in"], 48)

            @block.gpsimd
            def _(pool):
                pool.memset(zeros[:], 0.0).then_inc(s["const_done"], 1)
                pool.memset(ones[:], 1.0).then_inc(s["const_done"], 1)
                pool.wait_ge(s["const_done"], 2)
                pool.affine_select(out=upper[:], in_=ones[:], compare_op=ALU.is_gt, fill=0.0, base=0,
                                   pattern=[[1, P]], channel_multiplier=-1).then_inc(s["const_done"], 1)

            @block.vector
            def _(dve):
                dve.tensor_copy(identb[:], ident[:]).then_inc(s["steps"], 1)
                per = 4

                def signs(n, e, buf, first=False):
                    k = Steps(dve, s["steps"], 1 + n * per)
                    dve.wait_ge(raw_in[buf], loads_of(n, buf))
                    if not first:
                        dve.wait_ge(s["tern_done"], n)
                    dve.tensor_reduce(mag[:, 0:KF], raw1[buf][:], AX.X, ALU.add, apply_absolute_value=True)
                    k.step(dve.tensor_reduce(mag[:, KF:], raw2[buf][:], AX.X, ALU.add, apply_absolute_value=True))
                    dve.tensor_scalar(mag[:, 0:KF], mag[:, 0:KF], 1.0 / D, 1e-5, ALU.mult, ALU.max)
                    k.step(dve.tensor_scalar(mag[:, KF:], mag[:, KF:], 1.0 / F, 1e-5, ALU.mult, ALU.max))
                    dve.tensor_scalar(thr[:], mag[:], 0.5, None, ALU.mult)
                    k.step(dve.tensor_scalar(nthr[:], mag[:], -0.5, None, ALU.mult))
                    rows = [(raw1[buf][:, t, :], t * D, D) for t in range(KF)] + \
                           [(raw2[buf][:, t, :], KF * D + t * F, F) for t in range(KD)]
                    for t, (w, at, width) in enumerate(rows):
                        ins = dve.tensor_scalar(neg[:, at:at + width], w, nthr[:, t:t + 1], None, ALU.is_lt)
                    k.step(ins)
                    assert k.n == per
                    if not first:
                        dve.wait_ge(s["spread"], n)
                    for t, (w, at, width) in enumerate(rows):
                        dve.scalar_tensor_tensor(out=tern[:, at:at + width], in0=w, scalar=thr[:, t:t + 1],
                                                 in1=neg[:, at:at + width], op0=ALU.is_gt, op1=ALU.subtract)
                    for t in range(KD):
                        dve.tensor_scalar(diag[:, t, :], ident[:], mag[:, KF + t:KF + t + 1], None, ALU.mult)
                    dve.tensor_copy(s1[:, e, :], mag[:, 0:KF]).then_inc(s["tern_done"], 1)

                def loads_of(n, buf):
                    return (n - buf) * 16 + 32

                signs(0, NE, 0, True)
                with dve.Fori(0, NE // 2) as i:
                    signs(i * 2 + 1, i * 2, 1)
                    signs(i * 2 + 2, i * 2 + 1, 0)

            @block.tensor
            def _(pe):
                pe.wait_ge(s["const_done"], 3)

                def turn(n, first=False):
                    pe.wait_ge(s["tern_done"], n + 1)
                    if not first:
                        pe.wait_ge(s["w1_done"], n)
                    for a in range(KD):
                        for t in range(KF):
                            ins = pe.transpose(psA[0][:, a * KF + t, :], tern[:, t * D + a * P:t * D + (a + 1) * P], identb[:])
                    ins.then_inc(s["turned1"], 1)
                    if not first:
                        pe.wait_ge(s["w2_done"], n)
                    for a in range(KF):
                        for t in range(KD):
                            at = KF * D + t * F + a * P
                            ins = pe.transpose(psA[1][:, a * KD + t, :], tern[:, at:at + P], identb[:])
                    ins.then_inc(s["turned2"], 1)
                    if not first:
                        pe.wait_ge(s["s2_done"], n)
                    for t in range(KD):
                        ins = pe.matmul(psB[:, t * P:(t + 1) * P], ones[:], diag[:, t, :], start=True, stop=True)
                    ins.then_inc(s["spread"], 1)

                turn(0, True)
                with pe.Fori(1, NE + 1) as n:
                    turn(n)

            @block.scalar
            def _(act):
                def keep(n, e):
                    act.wait_ge(s["turned1"], n + 1)
                    act.activation(w1t[:, e, :, :].rearrange("p k f -> p (k f)"), psA[0][:].rearrange("p a t -> p (a t)"),
                                   ACT.Copy).then_inc(s["w1_done"], 1)
                    act.wait_ge(s["turned2"], n + 1)
                    act.activation(w2t[:, e, :, :].rearrange("p k f -> p (k f)"), psA[1][:].rearrange("p a t -> p (a t)"),
                                   ACT.Copy).then_inc(s["w2_done"], 1)
                    act.wait_ge(s["spread"], n + 1)
                    act.activation(s2[:, e, :], psB[:], ACT.Copy).then_inc(s["s2_done"], 1)

                keep(0, NE)
                with act.Fori(1, NE + 1) as n:
                    keep(n, n - 1)


def token_norms(nc, sb, ps, sem, NB, D, KD, x_sb, ident, x_mean, x_rstd, x_stats, nt, n_sb, hT,
                logits, router, gamma, beta, NE, tag, twice):
    with ExitStack() as c:
        n_t = [sb(f"{tag}_nt{i}", [P, D], F32, c) for i in range(2)]
        h = [sb(f"{tag}_h{i}", [P, KD, P], F32, c) for i in range(2)]
        psT = [ps(f"{tag}_psN{i}", [P, KD, P], F32, c) for i in range(2)]
        psL = [ps(f"{tag}_psL{i}", [P, NE], F32, c) for i in range(2)]
        s = {n: sem(f"{tag}_n_{n}", c) for n in ("steps normed kept turned scaled split scored logits_out".split())}
        with nc.Block() as block:
            @block.vector
            def _(dve):
                k = Steps(dve, s["steps"])
                for j in range(NB):
                    ins = dve.bn_stats(x_stats[:, j, :], x_sb[:, j, :])
                k.step(ins)
                norm_steps(dve, k, x_stats, x_mean[:], x_rstd[:], [t[:] for t in nt], twice)
                base = k.n

                def norm(i, b, first=False):
                    if not first:
                        dve.wait_ge(s["turned"], i - 1)
                        dve.wait_ge(s["kept"], i - 1)
                    dve.tensor_scalar(n_t[b][:], x_sb[:, i, :], x_mean[:, bass.ds(i, 1)], x_rstd[:, bass.ds(i, 1)],
                                      ALU.subtract, ALU.mult).then_inc(s["normed"], 1)

                def split(i, b):
                    dve.wait_ge(s["scaled"], i + 1)
                    k = Steps(dve, s["steps"], base + i)
                    k.step(dve.tensor_copy(hT[0][:, :, i, :], h[b][:]))
                    dve.tensor_tensor(hT[1][:, :, i, :], h[b][:], hT[0][:, :, i, :].bitcast(F32), ALU.subtract)\
                       .then_inc(s["split"], 1)
                    dve.wait_ge(s["scored"], i + 1)
                    dve.tensor_copy(logits[:, i, :], psL[b][:]).then_inc(s["logits_out"], 1)

                norm(0, 0, True)
                norm(1, 1, True)
                with dve.Fori(0, NB // 2 - 1) as i:
                    for b in range(2):
                        split(i * 2 + b, b)
                        norm(i * 2 + b + 2, b)
                for b in range(2):
                    split(NB - 2 + b, b)

            @block.gpsimd
            def _(pool):
                with pool.Fori(0, NB // 2) as i:
                    for b in range(2):
                        pool.wait_ge(s["normed"], i * 2 + b + 1)
                        pool.tensor_copy(n_sb[:, i * 2 + b, :], n_t[b][:]).then_inc(s["kept"], 1)

            @block.tensor
            def _(pe):
                def turn(i, b, first=False):
                    pe.wait_ge(s["normed"], i + 1)
                    if not first:
                        pe.wait_ge(s["scaled"], i - 1)
                    for a in range(KD):
                        ins = pe.transpose(psT[b][:, a, :], n_t[b][:, a * P:(a + 1) * P], ident[:])
                    ins.then_inc(s["turned"], 1)

                def score(i, b, first=False):
                    pe.wait_ge(s["scaled"], i + 1)
                    if not first:
                        pe.wait_ge(s["logits_out"], i - 1)
                    for a in range(KD):
                        ins = pe.matmul(psL[b][:], h[b][:, a, :], router[:, a, :], start=(a == 0), stop=(a == KD - 1))
                    ins.then_inc(s["scored"], 1)

                turn(0, 0, True)
                turn(1, 1, True)
                score(0, 0, True)
                turn(2, 0)
                score(1, 1, True)
                turn(3, 1)
                with pe.Fori(1, NB // 2 - 1) as i:
                    for b in range(2):
                        score(i * 2 + b, b)
                        turn(i * 2 + b + 2, b)
                for b in range(2):
                    score(NB - 2 + b, b)

            @block.scalar
            def _(act):
                def scale(i, b, first=False):
                    act.wait_ge(s["turned"], i + 1)
                    if not first:
                        act.wait_ge(s["scored"], i - 1)
                        act.wait_ge(s["split"], i - 1)
                    if gamma is None:
                        act.activation(h[b][:], psT[b][:], ACT.Copy).then_inc(s["scaled"], 1)
                        return
                    for a in range(KD):
                        ins = act.activation(h[b][:, a, :], psT[b][:, a, :], ACT.Identity, bias=beta[:, a:a + 1],
                                             scale=gamma[:, a:a + 1])
                    ins.then_inc(s["scaled"], 1)

                scale(0, 0, True)
                scale(1, 1, True)
                with act.Fori(1, NB // 2) as i:
                    for b in range(2):
                        scale(i * 2 + b, b)


def route_top1(nc, sb, ps, sem, NB, NE, NT, D, logits, prob, pos, owner, ones, upper, gates):
    with ExitStack() as c:
        best = sb("r0_best", [P, NB, 8], F32, c)
        index = sb("r0_index", [P, NB, 8], U32, c)
        shifted = sb("r0_shifted", [P, NB, NE], F32, c)
        expd = sb("r0_exp", [P, NB, NE], F32, c)
        which = sb("r0_which", [P, NB], F32, c)
        iota_i = sb("r0_iota_i", [P, NT], I32, c)
        iota = sb("r0_iota", [P, NT], F32, c)
        hot = sb("r0_hot", [P, NB, NE], F32, c)
        rank = sb("r0_rank", [P, NB, NE], F32, c)
        tot = sb("r0_tot", [P, NB, NE], F32, c)
        pre = [sb(f"r0_pre{i}", [P, NB, NE], F32, c) for i in range(2)]
        cnt_i = sb("r0_cnt_i", [P, NE], I32, c)
        tiles = sb("r0_tiles", [P, NE], F32, c)
        ends = [sb(f"r0_ends{i}", [P, NE], F32, c) for i in range(2)]
        base = sb("r0_base", [P, NE], F32, c)
        after = sb("r0_after", [P, NT, NE], F32, c)
        nown = sb("r0_nown", [P, NT], F32, c)
        posf = sb("r0_posf", [P, NB], F32, c)
        psR = ps("r0_ps", [P, 2, NB * NE], F32, c)
        s = {n: sem(f"r0_{n}", c) for n in "steps iota_done shifted_done exp_done hot_done ranked".split()}

        with nc.Block() as block:
            @block.gpsimd
            def _(pool):
                pool.iota(iota_i[:], pattern=[[1, NT]], base=0, channel_multiplier=0).then_inc(s["iota_done"], 1)

            @block.scalar
            def _(act):
                act.wait_ge(s["shifted_done"], 1)
                act.activation(expd[:], shifted[:], ACT.Exp).then_inc(s["exp_done"], 1)

            @block.tensor
            def _(pe):
                pe.wait_ge(s["hot_done"], 1)
                flat = hot[:].rearrange("p b e -> p (b e)")
                pe.matmul(psR[:, 0, :], upper[:], flat, start=True, stop=True)
                pe.matmul(psR[:, 1, :], ones[:], flat, start=True, stop=True).then_inc(s["ranked"], 1)

            @block.vector
            def _(dve):
                k = Steps(dve, s["steps"])
                for i in range(NB):
                    ins = dve.max(best[:, i, :], logits[:, i, :])
                k.step(ins)
                for i in range(NB):
                    dve.max_index(index[:, i, :], best[:, i, :], logits[:, i, :])
                dve.tensor_tensor(shifted[:], logits[:], best[:, :, 0:1].to_broadcast([P, NB, NE]), ALU.subtract)\
                   .then_inc(s["shifted_done"], 1)
                dve.wait_ge(s["iota_done"], 1)
                k.step(dve.tensor_copy(iota[:], iota_i[:]))
                k.step(dve.tensor_copy(which[:], index[:, :, 0]))
                dve.tensor_tensor(hot[:], which[:].unsqueeze(2).to_broadcast([P, NB, NE]),
                                  iota[:, 0:NE].unsqueeze(1).to_broadcast([P, NB, NE]), ALU.is_equal).then_inc(s["hot_done"], 1)
                dve.wait_ge(s["exp_done"], 1)
                k.step(dve.tensor_reduce(prob[:], expd[:], AX.X, ALU.add))
                k.step(dve.reciprocal(prob[:], prob[:]))
                k.step(dve.tensor_scalar(prob[:], prob[:], gates[:, 2:3], None, ALU.mult))
                dve.wait_ge(s["ranked"], 1)
                three = lambda t: t.rearrange("p (b e) -> p b e", e=NE)
                k.step(dve.tensor_copy(tot[:], three(psR[:, 1, :])))
                incl = prefix_steps(dve, k, tot, pre, NB)
                k.step(dve.tensor_tensor(rank[:], three(psR[:, 0, :]), incl[:], ALU.add))
                k.step(dve.tensor_tensor(rank[:], rank[:], tot[:], ALU.subtract))
                k.step(dve.tensor_scalar(cnt_i[:], incl[:, NB - 1, :], float(P - 1), None, ALU.add))
                k.step(dve.tensor_scalar(cnt_i[:], cnt_i[:], 7, None, ALU.logical_shift_right))
                k.step(dve.tensor_copy(tiles[:], cnt_i[:]))
                end = prefix_steps(dve, k, tiles, ends, NE)
                k.step(dve.tensor_tensor(base[:], end[:], tiles[:], ALU.subtract))
                k.step(dve.tensor_scalar(base[:], base[:], float(P), None, ALU.mult))
                k.step(dve.tensor_tensor(rank[:], rank[:], base[:].unsqueeze(1).to_broadcast([P, NB, NE]), ALU.add))
                k.step(dve.tensor_tensor(rank[:], rank[:], hot[:], ALU.mult))
                k.step(dve.tensor_reduce(posf[:], rank[:], AX.X, ALU.add))
                k.step(dve.tensor_copy(pos[:], posf[:]))
                k.step(dve.tensor_tensor(after[:], iota[:].unsqueeze(2).to_broadcast([P, NT, NE]),
                                         end[:].unsqueeze(1).to_broadcast([P, NT, NE]), ALU.is_ge))
                k.step(dve.tensor_reduce(nown[:], after[:], AX.X, ALU.add))
                k.step(dve.tensor_scalar(owner[:], nown[:], float(NE - 1), None, ALU.min))


def shared_ternary(nc, sb, ps, sem, NB, D, KD, KF, SH, hT, w1t, w2t, s1, sh, n_sb, pos, xg, scattered):
    with ExitStack() as c:
        g = [sb(f"s0_g{i}", [P, KF, P], F32, c) for i in range(2)]
        gs = [[sb(f"s0_g{n}{i}", [P, KF, P], F32R, c) for n in ("hi", "lo")] for i in range(2)]
        psH = [ps(f"s0_psH{i}", [P, KF, P], F32, c) for i in range(2)]
        psY = [ps(f"s0_psY{i}", [P, D], F32, c) for i in range(2)]
        s = {n: sem(f"s0_{n}", c) for n in "up silu steps split down kept".split()}
        with nc.Block() as block:
            @block.gpsimd
            def _(pool):
                for i in range(NB):
                    pool.indirect_dma_start(xg, bass.IndirectOffsetOnAxis(ap=pos[:, i:i + 1], axis=0), n_sb[:, i, :], None)\
                        .then_inc(scattered, 16)

            @block.tensor
            def _(pe):
                def up(i, b, first=False):
                    if not first:
                        pe.wait_ge(s["silu"], i - 1)
                    for t in range(KF):
                        for n, (a, part) in enumerate([(a, part) for a in range(KD) for part in range(2)]):
                            ins = pe.matmul(psH[b][:, t, :], w1t[:, SH, a, t * P:(t + 1) * P], hT[part][:, a, i, :],
                                            start=(n == 0), stop=(n == 2 * KD - 1))
                    ins.then_inc(s["up"], 1)

                def down(i, b, first=False):
                    pe.wait_ge(s["split"], i + 1)
                    if not first:
                        pe.wait_ge(s["kept"], i - 1)
                    for n, (t, part) in enumerate([(t, part) for t in range(KF) for part in range(2)]):
                        ins = pe.matmul(psY[b][:], gs[b][part][:, t, :], w2t[:, SH, t, :], start=(n == 0), stop=(n == 2 * KF - 1))
                    ins.then_inc(s["down"], 1)

                up(0, 0, True)
                up(1, 1, True)
                down(0, 0, True)
                up(2, 0)
                down(1, 1, True)
                up(3, 1)
                with pe.Fori(1, NB // 2 - 1) as i:
                    for b in range(2):
                        down(i * 2 + b, b)
                        up(i * 2 + b + 2, b)
                for b in range(2):
                    down(NB - 2 + b, b)

            @block.scalar
            def _(act):
                def silu(i, b, first=False):
                    act.wait_ge(s["up"], i + 1)
                    if not first:
                        act.wait_ge(s["split"], i - 1)
                    for t in range(KF):
                        ins = act.activation(g[b][:, t, :], psH[b][:, t, :], ACT.Silu, scale=s1[:, SH, t:t + 1])
                    ins.then_inc(s["silu"], 1)

                def keep(i, b):
                    act.wait_ge(s["down"], i + 1)
                    act.activation(sh[:, i, :], psY[b][:], ACT.Copy).then_inc(s["kept"], 1)

                silu(0, 0, True)
                silu(1, 1, True)
                with act.Fori(0, NB // 2 - 1) as i:
                    for b in range(2):
                        keep(i * 2 + b, b)
                        silu(i * 2 + b + 2, b)
                for b in range(2):
                    keep(NB - 2 + b, b)

            @block.vector
            def _(dve):
                def split(i, b, first=False):
                    dve.wait_ge(s["silu"], i + 1)
                    if not first:
                        dve.wait_ge(s["down"], i - 1)
                    k = Steps(dve, s["steps"], i)
                    k.step(dve.tensor_copy(gs[b][0][:], g[b][:]))
                    dve.tensor_tensor(gs[b][1][:], g[b][:], gs[b][0][:].bitcast(F32), ALU.subtract).then_inc(s["split"], 1)

                split(0, 0, True)
                split(1, 1, True)
                with dve.Fori(1, NB // 2) as i:
                    for b in range(2):
                        split(i * 2 + b, b)


def expert_tiles(nc, sb, ps, sem, NB, NT, D, KD, KF, SH, x_sb, sh, s2, s1, w1t, w2t, gamma, beta, ident, owner,
                 xg, yg, n_sb, pos, prob, gates, scattered, x_stats):
    F = KF * P
    with ExitStack() as c:
        xin = [sb(f"e0_xin{i}", [P, D], F32, c) for i in range(2)]
        h = [sb(f"e0_h{i}", [P, KD, P], F32, c) for i in range(2)]
        hs = [[sb(f"e0_h{n}{i}", [P, KD, P], F32R, c) for n in ("hi", "lo")] for i in range(2)]
        u = [sb(f"e0_u{i}", [P, F], F32, c) for i in range(2)]
        g = [sb(f"e0_g{i}", [P, KF, P], F32, c) for i in range(2)]
        gs = [[sb(f"e0_g{n}{i}", [P, KF, P], F32R, c) for n in ("hi", "lo")] for i in range(2)]
        y = [sb(f"e0_y{i}", [P, D], F32, c) for i in range(2)]
        s2g = sb("e0_s2g", [P, D], F32, c)
        psA = [ps(f"e0_psA{i}", [P, KD, P], F32, c) for i in range(2)]
        psH = [ps(f"e0_psH{i}", [P, F], F32, c) for i in range(2)]
        psT = [ps(f"e0_psT{i}", [P, KF, P], F32, c) for i in range(2)]
        psY = [ps(f"e0_psY{i}", [P, D], F32, c) for i in range(2)]
        names = "in0 in1 turned scaled steps steps2 split up up_out turned2 silu split2 down y_done out0 out1 shared_in s2g".split()
        gathered = [sem(f"e0_gathered{i}", c) for i in range(NB)]
        s = {n: sem(f"e0_{n}", c) for n in names}
        x_in, y_out = [s["in0"], s["in1"]], [s["out0"], s["out1"]]

        with nc.Block() as block:
            @block.sync
            def _(sp):
                sp.wait_ge(scattered, 16 * NB)

                def load(j, b):
                    sp.dma_start(xin[b][:], xg.rearrange("(t p) d -> t p d", p=P)[j]).then_inc(x_in[b], 16)

                def store(j, b):
                    sp.wait_ge(s["y_done"], j + 1)
                    sp.dma_start(yg.rearrange("(t p) d -> t p d", p=P)[j], y[b][:]).then_inc(y_out[b], 16)

                for b in range(2):
                    load(b, b)
                with sp.Fori(1, NT // 2) as i:
                    for b in range(2):
                        sp.wait_ge(s["turned"], i * 2 + b - 1)
                        load(i * 2 + b, b)
                        store(i * 2 + b - 2, b)
                for b in range(2):
                    store(NT - 2 + b, b)

            @block.tensor
            def _(pe):
                def turn(j, i, b, first=False):
                    pe.wait_ge(x_in[b], i * 16 + 16)
                    if not first:
                        pe.wait_ge(s["scaled"], j - 1)
                    for a in range(KD):
                        ins = pe.transpose(psA[b][:, a, :], xin[b][:, a * P:(a + 1) * P], ident[:])
                    ins.then_inc(s["turned"], 1)

                def up(j, b, first=False):
                    e = pe.value_load(owner[0:1, bass.ds(j, 1)], min_val=0, max_val=SH - 1)
                    pe.wait_ge(s["split"], j + 1)
                    if not first:
                        pe.wait_ge(s["up_out"], j - 1)
                    for n, (a, part) in enumerate([(a, part) for a in range(KD) for part in range(2)]):
                        ins = pe.matmul(psH[b][:], hs[b][part][:, a, :], w1t[:, e, a, :], start=(n == 0), stop=(n == 2 * KD - 1))
                    ins.then_inc(s["up"], 1)

                def turn2(j, b, first=False):
                    pe.wait_ge(s["up_out"], j + 1)
                    if not first:
                        pe.wait_ge(s["silu"], j - 1)
                    for t in range(KF):
                        ins = pe.transpose(psT[b][:, t, :], u[b][:, t * P:(t + 1) * P], ident[:])
                    ins.then_inc(s["turned2"], 1)

                def down(j, b, first=False):
                    e = pe.value_load(owner[0:1, bass.ds(j, 1)], min_val=0, max_val=SH - 1)
                    pe.wait_ge(s["split2"], j + 1)
                    if not first:
                        pe.wait_ge(s["y_done"], j - 1)
                    for n, (t, part) in enumerate([(t, part) for t in range(KF) for part in range(2)]):
                        ins = pe.matmul(psY[b][:], gs[b][part][:, t, :], w2t[:, e, t, :], start=(n == 0), stop=(n == 2 * KF - 1))
                    ins.then_inc(s["down"], 1)

                def tile(j, i, b, first=False, second=False, third=False):
                    turn(j, i, b, first or second)
                    if not first:
                        turn2(j - 1, 1 - b, second or third)
                    up(j, b, first or second)
                    if not first:
                        down(j - 1, 1 - b, second or third)

                tile(0, 0, 0, first=True)
                tile(1, 0, 1, second=True)
                tile(2, 1, 0, third=True)
                tile(3, 1, 1)
                with pe.Fori(2, NT // 2) as i:
                    for b in range(2):
                        tile(i * 2 + b, i, b)
                turn2(NT - 1, 1)
                down(NT - 1, 1)

            @block.scalar
            def _(act):
                def scale(j, b, first=False):
                    act.wait_ge(s["turned"], j + 1)
                    if not first:
                        act.wait_ge(s["split"], j - 1)
                    for a in range(KD):
                        ins = act.activation(h[b][:, a, :], psA[b][:, a, :], ACT.Identity, bias=beta[:, a:a + 1],
                                             scale=gamma[:, a:a + 1])
                    ins.then_inc(s["scaled"], 1)

                def silu(j, b, first=False):
                    e = act.value_load(owner[0:1, bass.ds(j, 1)], min_val=0, max_val=SH - 1)
                    act.wait_ge(s["turned2"], j + 1)
                    if not first:
                        act.wait_ge(s["split2"], j - 1)
                    for t in range(KF):
                        ins = act.activation(g[b][:, t, :], psT[b][:, t, :], ACT.Silu, scale=s1[:, e, t:t + 1])
                    ins.then_inc(s["silu"], 1)

                scale(0, 0, True)
                scale(1, 1, True)
                silu(0, 0, True)
                scale(2, 0)
                silu(1, 1, True)
                with act.Fori(1, NT // 2 - 1) as i:
                    for b in range(2):
                        scale(i * 2 + b + 1, 1 - b)
                        silu(i * 2 + b, b)
                scale(NT - 1, 1)
                silu(NT - 2, 0)
                silu(NT - 1, 1)

            @block.vector
            def _(dve):
                dve.tensor_scalar(s2g[:], s2[:, SH, :], gates[:, 2:3], None, ALU.mult).then_inc(s["s2g"], 1)

                def split(j, b, first=False):
                    dve.wait_ge(s["scaled"], j + 1)
                    if not first:
                        dve.wait_ge(s["up"], j - 1)
                    k = Steps(dve, s["steps"], j)
                    k.step(dve.tensor_copy(hs[b][0][:], h[b][:]))
                    dve.tensor_tensor(hs[b][1][:], h[b][:], hs[b][0][:].bitcast(F32), ALU.subtract).then_inc(s["split"], 1)

                def up_out(j, b, first=False):
                    dve.wait_ge(s["up"], j + 1)
                    if not first:
                        dve.wait_ge(s["turned2"], j - 1)
                    dve.tensor_copy(u[b][:], psH[b][:]).then_inc(s["up_out"], 1)

                def split2(j, b, first=False):
                    dve.wait_ge(s["silu"], j + 1)
                    if not first:
                        dve.wait_ge(s["down"], j - 1)
                    k = Steps(dve, s["steps2"], j)
                    k.step(dve.tensor_copy(gs[b][0][:], g[b][:]))
                    dve.tensor_tensor(gs[b][1][:], g[b][:], gs[b][0][:].bitcast(F32), ALU.subtract).then_inc(s["split2"], 1)

                def out(j, stored, b, first=False):
                    e = dve.value_load(owner[0:1, bass.ds(j, 1)], min_val=0, max_val=SH - 1)
                    dve.wait_ge(s["down"], j + 1)
                    if not first:
                        dve.wait_ge(y_out[b], stored * 16)
                    dve.tensor_tensor(y[b][:], psY[b][:], s2[:, e, :], ALU.mult).then_inc(s["y_done"], 1)

                split(0, 0, True)
                up_out(0, 0, True)

                def tile(j, stored, b, first=False, second=False):
                    split(j, b, first)
                    split2(j - 1, 1 - b, first or second)
                    up_out(j, b, first)
                    out(j - 1, stored, 1 - b, first or second)

                tile(1, 0, 1, first=True)
                tile(2, 0, 0, second=True)
                tile(3, 1, 1)
                with dve.Fori(2, NT // 2) as i:
                    tile(i * 2, i - 1, 0)
                    tile(i * 2 + 1, i, 1)
                split2(NT - 1, 1)
                out(NT - 1, NT // 2 - 1, 1)
                for i in range(NB):
                    dve.wait_ge(gathered[i], 16)
                    dve.wait_ge(s["shared_in"], i * 2 + 2)
                    dve.scalar_tensor_tensor(out=x_sb[:, i, :], in0=n_sb[:, i, :], scalar=prob[:, i:i + 1],
                                             in1=x_sb[:, i, :], op0=ALU.mult, op1=ALU.add)

            @block.gpsimd
            def _(pool):
                pool.wait_ge(s["s2g"], 1)
                with pool.Fori(0, NB) as i:
                    pool.tensor_tensor(sh[:, i, :], sh[:, i, :], s2g[:], ALU.mult).then_inc(s["shared_in"], 1)
                    pool.wait_ge(s["shared_in"], i * 2 + 1)
                    pool.tensor_tensor(x_sb[:, i, :], x_sb[:, i, :], sh[:, i, :], ALU.add).then_inc(s["shared_in"], 1)
                for b in range(2):
                    pool.wait_ge(y_out[b], NT // 2 * 16)
                for i in range(NB):
                    pool.indirect_dma_start(n_sb[:, i, :], None, yg, bass.IndirectOffsetOnAxis(ap=pos[:, i:i + 1], axis=0))\
                        .then_inc(gathered[i], 16)


def at_least(eng, sem, value):
    if isinstance(value, int) and value <= 0:
        return
    eng.wait_ge(sem, value)


PARTS3 = ((0, 0), (0, 1), (1, 0))


def attention_1(nc, A, sb, ps, sem, NB, D, KD, x_sb, ctx_sb, ident, gates, x_mean, x_rstd, c_mean, c_rstd,
                x_stats, c_stats, nt):
    DH = 128
    NI = A["L1_xattn_Wq"].shape[1]
    NH = NI // DH
    NK = 2 * P
    scale = float(DH) ** -0.5
    with ExitStack() as c:
        wq = [sb(f"a1_wq{n}", [P, KD, NI], F32R, c) for n in ("hi", "lo")]
        wkv = [sb(f"a1_wkv{n}", [P, KD, 2 * NI], F32R, c) for n in ("hi", "lo")]
        wo = [sb(f"a1_wo{n}", [P, NH, D], F32R, c) for n in ("hi", "lo")]
        bq, bk = sb("a1_bq", [P, NH], F32, c), sb("a1_bk", [P, NH], F32, c)
        bv, bo = sb("a1_bv", [P, NI], F32, c), sb("a1_bo", [P, D], F32, c)
        gam, bet = sb("a1_gam", [P, 2, KD], F32, c), sb("a1_bet", [P, 2, KD], F32, c)

        with ExitStack() as r:
            rawq = sb("a1_rawq", [P, KD, NI], F32, r)
            rawkv = sb("a1_rawkv", [P, KD, 2 * NI], F32, r)
            rawo = sb("a1_rawo", [P, NH, D], F32, r)
            s = {n: sem(f"a1w_{n}", r) for n in "q_in kv_in o_in small_in scaled hi lo steps".split()}
            with nc.Block() as block:
                @block.sync
                def _(sp):
                    sp.dma_start(rawq[:], A["L1_xattn_Wq"].rearrange("(k p) n -> p k n", p=P)).then_inc(s["q_in"], 16)
                    sp.dma_start(rawkv[:], A["L1_xattn_Wkv"].rearrange("(k p) n -> p k n", p=P)).then_inc(s["kv_in"], 16)
                    sp.dma_start(rawo[:], A["L1_xattn_Wo"].rearrange("(h p) n -> p h n", p=P)).then_inc(s["o_in"], 16)
                    with nc.allow_non_contiguous_dma(reason="a few hundred small parameters"):
                        for dst, src in ((bq[:], A["L1_xattn_bq"].rearrange("(h p) -> p h", p=P)),
                                         (bk[:], A["L1_xattn_bkv"][0:NI].rearrange("(h p) -> p h", p=P)),
                                         (bv[:], A["L1_xattn_bkv"][NI:2 * NI].partition_broadcast(P)),
                                         (bo[:], A["L1_xattn_bo"].partition_broadcast(P)),
                                         (gam[:, 0, :], A["L1_xattn_gamma_media"].rearrange("(k p) -> p k", p=P)),
                                         (gam[:, 1, :], A["L1_xattn_gamma_lat"].rearrange("(k p) -> p k", p=P)),
                                         (bet[:, 0, :], A["L1_xattn_beta_media"].rearrange("(k p) -> p k", p=P)),
                                         (bet[:, 1, :], A["L1_xattn_beta_lat"].rearrange("(k p) -> p k", p=P))):
                            sp.dma_start(dst, src).then_inc(s["small_in"], 16)
                    sp.wait_ge(s["small_in"], 128)

                flat = lambda t: t.rearrange("p a n -> p (a n)")
                chunks = [(wq, rawq, 0)] + [(wkv, rawkv, n) for n in range(2)] + [(wo, rawo, 0)]

                @block.scalar
                def _(act):
                    act.wait_ge(s["q_in"], 16)
                    act.activation(rawq[:], rawq[:], ACT.Copy, scale=scale).then_inc(s["scaled"], 1)
                    act.wait_ge(s["scaled"], 1)
                    for n, (w, raw, part) in enumerate(chunks):
                        if n == 1:
                            act.wait_ge(s["kv_in"], 16)
                        if n == 3:
                            act.wait_ge(s["o_in"], 16)
                        cols = slice(2048 * part, 2048 * (part + 1))
                        act.activation(flat(w[0][:])[:, cols], flat(raw[:])[:, cols], ACT.Copy).then_inc(s["hi"], 1)

                @block.vector
                def _(dve):
                    for n, (w, raw, part) in enumerate(chunks):
                        cols = slice(2048 * part, 2048 * (part + 1))
                        dve.wait_ge(s["hi"], n + 1)
                        dve.tensor_tensor(flat(w[1][:])[:, cols], flat(raw[:])[:, cols], flat(w[0][:])[:, cols].bitcast(F32),
                                          ALU.subtract)
                    dve.wait_ge(s["small_in"], 128)
                    dve.tensor_scalar(bq[:], bq[:], scale, None, ALU.mult)
                    dve.tensor_scalar(bo[:], bo[:], gates[:, 1:2], None, ALU.mult)
                    k = Steps(dve, s["steps"])
                    for j in range(NB):
                        dve.bn_stats(x_stats[:, j, :], x_sb[:, j, :])
                    for j in range(NB):
                        ins = dve.bn_stats(c_stats[:, j, :], ctx_sb[:, j, :])
                    k.step(ins)
                    norm_steps(dve, k, x_stats, x_mean[:], x_rstd[:], [t[:] for t in nt], True)
                    norm_steps(dve, k, c_stats, c_mean[:], c_rstd[:], [t[:] for t in nt], False)

        normed = [sb(f"a1_n{n}", [P, D], F32, c) for n in ("media", "lat")]
        kvf = sb("a1_kvf", [P, KD, NK], F32, c)
        kv = [[sb(f"a1_kv{n}{i}", [P, KD, NK], F32R, c) for n in ("hi", "lo")] for i in range(2)]
        q = [sb(f"a1_q{n}", [P, NH, P], F32R, c) for n in ("hi", "lo")]
        k_ = [sb(f"a1_k{n}", [P, NH, NK], F32R, c) for n in ("hi", "lo")]
        vf = sb("a1_vf", [P, 512], F32, c)
        v = [sb(f"a1_v{n}", [P, 2, NI], F32R, c) for n in ("hi", "lo")]
        nmax, sums, rsum = (sb(f"a1_{n}", [P, NH], F32, c) for n in ("nmax", "sums", "rsum"))
        probs = sb("a1_probs", [P, NH, NK], F32, c)
        pT = [sb(f"a1_pT{n}", [P, NH, 2, P], F32R, c) for n in ("hi", "lo")]
        oT = [sb(f"a1_oT{n}", [P, NH, P], F32R, c) for n in ("hi", "lo")]
        psA = [ps(f"a1_psA{i}", [P, 3 * P], F32, c) for i in range(2)]
        psS = [ps(f"a1_psS{i}", [P, NK], F32, c) for i in range(2)]
        psT = ps("a1_psT", [P, 2, P], F32, c)
        psO = ps("a1_psO", [P, P], F32, c)
        psV = ps("a1_psV", [P, 512], F32, c)
        psY = ps("a1_psY", [P, D], F32, c)
        names = ("normed resid kv_turned kv_scaled kv_hi kv_lo qk_done qk_hi qk_lo s_done max_done exp_done rsum_done "
                 "p_done t_done pt_hi pt_lo pv_done o_hi o_lo v_done v_f v_hi v_lo y_done x_done").split()
        s = {n: sem(f"a1_{n}", c) for n in names}
        CHUNKS = {0: 0, 1: 1, 3: 2, 5: 3}

        def schedule(batch, finish, eng):
            batch(0, 0, True)
            batch(1, 1, True)
            with eng.Fori(1, NB // 2 - 1) as i:
                for par in range(2):
                    batch(i * 2 + par, par, True)
            batch(NB - 2, 0, True)
            batch(NB - 1, 1, False)
            finish()

        def exists(n):
            return not isinstance(n, int) or 0 <= n < NH * NB

        with nc.Block() as block:
            @block.tensor
            def _(pe):
                def turn_kv(b):
                    pe.wait_ge(s["normed"], b * 2 + 2)
                    at_least(pe, s["v_f"], b * 4)
                    for m in range(2):
                        for a in range(KD):
                            ins = pe.transpose(psV[:, (a * 2 + m) * P:(a * 2 + m + 1) * P], normed[m][:, a * P:(a + 1) * P], ident[:])
                    ins.then_inc(s["kv_turned"], 1)

                def project(n, b, h, par):
                    if h == 0:
                        pe.wait_ge(s["kv_lo"], b + 1)
                    at_least(pe, s["qk_lo"], n - 1)
                    for w, col, lo, width, at in ((wq, h, P, P, 0), (wkv, h, 0, NK, P)):
                        for m, (a, (x, y)) in enumerate([(a, xy) for a in range(KD) for xy in PARTS3]):
                            ins = pe.matmul(psA[h % 2][:, at:at + width], w[x][:, a, col * DH:(col + 1) * DH],
                                            kv[par][y][:, a, lo:lo + width], start=(m == 0), stop=(m == 3 * KD - 1))
                    ins.then_inc(s["qk_done"], 1)

                def values(b, ch, par):
                    half, kt = divmod(ch, 2)
                    at_least(pe, s["v_f"], b * 4 + ch)
                    if ch == 0:
                        pe.wait_ge(s["kv_scaled"], b + 1)
                    for m, (a, (x, y)) in enumerate([(a, xy) for a in range(KD) for xy in PARTS3]):
                        ins = pe.matmul(psV[:], kv[par][x][:, a, kt * P:(kt + 1) * P],
                                        wkv[y][:, a, NI + half * 512:NI + (half + 1) * 512], start=(m == 0), stop=(m == 3 * KD - 1))
                    ins.then_inc(s["v_done"], 1)

                def score(n, h):
                    pe.wait_ge(s["qk_lo"], n + 1)
                    at_least(pe, s["exp_done"], n - 1)
                    for m, (x, y) in enumerate(PARTS3):
                        ins = pe.matmul(psS[h % 2][:], q[x][:, h, :], k_[y][:, h, :], start=(m == 0), stop=(m == 2))
                    ins.then_inc(s["s_done"], 1)

                def turn(n, h):
                    pe.wait_ge(s["p_done"], n + 1)
                    at_least(pe, s["pt_lo"], n)
                    for kt in range(2):
                        ins = pe.transpose(psT[:, kt, :], probs[:, h, kt * P:(kt + 1) * P], ident[:])
                    ins.then_inc(s["t_done"], 1)

                def apply(n, b, h):
                    pe.wait_ge(s["pt_lo"], n + 1)
                    at_least(pe, s["o_lo"], n)
                    if h in (0, 4):
                        pe.wait_ge(s["v_lo"], b * 4 + (2 if h == 0 else 4))
                    for m, (kt, (x, y)) in enumerate([(kt, xy) for kt in range(2) for xy in PARTS3]):
                        ins = pe.matmul(psO[:], v[x][:, kt, h * DH:(h + 1) * DH], pT[y][:, h, kt, :], start=(m == 0), stop=(m == 5))
                    ins.then_inc(s["pv_done"], 1)

                def output(b):
                    pe.wait_ge(s["o_lo"], b * NH + NH)
                    at_least(pe, s["x_done"], b)
                    for m, (h, (x, y)) in enumerate([(h, xy) for h in range(NH) for xy in PARTS3]):
                        ins = pe.matmul(psY[:], oT[x][:, h, :], wo[y][:, h, :], start=(m == 0), stop=(m == 3 * NH - 1))
                    ins.then_inc(s["y_done"], 1)

                def later(b, h, lag):
                    return (b, h - lag) if h >= lag else (b - 1, h - lag + NH)

                def rest(b, h):
                    for lag, do in ((1, "s"), (3, "t"), (4, "a")):
                        bb, hh = later(b, h, lag)
                        n = bb * NH + hh
                        if do == "a" and h == 4 and exists((b - 1) * NH):
                            output(b - 1)
                        if not exists(n):
                            continue
                        if do == "s":
                            score(n, hh)
                        elif do == "t":
                            turn(n, hh)
                        else:
                            apply(n, bb, hh)

                def batch(b, par, more):
                    for h in range(NH):
                        project(b * NH + h, b, h, par)
                        if h in CHUNKS:
                            values(b, CHUNKS[h], par)
                        if h == 6 and more:
                            turn_kv(b + 1)
                        rest(b, h)

                def finish():
                    for h in range(5):
                        rest(NB, h)

                turn_kv(0)
                schedule(batch, finish, pe)

            @block.scalar
            def _(act):
                def scale_kv(b):
                    act.wait_ge(s["kv_turned"], b + 1)
                    at_least(act, s["kv_lo"], b)
                    for m in range(2):
                        for a in range(KD):
                            ins = act.activation(kvf[:, a, m * P:(m + 1) * P], psV[:, (a * 2 + m) * P:(a * 2 + m + 1) * P], ACT.Identity,
                                                 bias=bet[:, m, a:a + 1], scale=gam[:, m, a:a + 1])
                    ins.then_inc(s["kv_scaled"], 1)

                def project(n, h):
                    act.wait_ge(s["qk_done"], n + 1)
                    act.activation(q[0][:, h, :], psA[h % 2][:, 0:P], ACT.Identity, bias=bq[:, h:h + 1])
                    act.activation(k_[0][:, h, :], psA[h % 2][:, P:3 * P], ACT.Identity, bias=bk[:, h:h + 1]).then_inc(s["qk_hi"], 1)

                def exps(n, h):
                    act.wait_ge(s["max_done"], n + 1)
                    act.activation(probs[:, h, :], psS[h % 2][:], ACT.Exp, bias=nmax[:, h:h + 1],
                                   accum_out=sums[:, h:h + 1]).then_inc(s["exp_done"], 1)

                def turn(n, h):
                    act.wait_ge(s["t_done"], n + 1)
                    act.activation(pT[0][:, h, :, :], psT[:], ACT.Copy).then_inc(s["pt_hi"], 1)

                def apply(n, h):
                    act.wait_ge(s["pv_done"], n + 1)
                    act.activation(oT[0][:, h, :], psO[:], ACT.Copy).then_inc(s["o_hi"], 1)

                def values(b, ch):
                    half, kt = divmod(ch, 2)
                    act.wait_ge(s["v_f"], b * 4 + ch + 1)
                    act.activation(v[0][:, kt, half * 512:(half + 1) * 512], vf[:], ACT.Copy).then_inc(s["v_hi"], 1)

                def rest(b, h, lags):
                    for lag, do in lags:
                        bb, hh = (b, h - lag) if h >= lag else (b - 1, h - lag + NH)
                        if exists(bb * NH + hh):
                            do(bb * NH + hh, hh)

                def batch(b, par, more):
                    for h in range(NH):
                        rest(b, h, ((4, turn), (5, apply)))
                        if h - 1 in CHUNKS:
                            values(b, CHUNKS[h - 1])
                        rest(b, h, ((2, exps),))
                        if h == 7 and more:
                            scale_kv(b + 1)
                        project(b * NH + h, h)

                def finish():
                    for h in range(5):
                        rest(NB, h, ((4, turn), (5, apply), (2, exps)))

                scale_kv(0)
                schedule(batch, finish, act)

            @block.gpsimd
            def _(pool):
                with pool.Fori(0, NB) as i:
                    pool.wait_ge(s["normed"], i * 2 + 2)
                    pool.tensor_tensor(x_sb[:, i, :], x_sb[:, i, :], bo[:], ALU.add).then_inc(s["resid"], 1)

            @block.vector
            def _(dve):
                def norm(b):
                    at_least(dve, s["kv_turned"], b)
                    for m, (src, mean, rstd) in enumerate(((ctx_sb, c_mean, c_rstd), (x_sb, x_mean, x_rstd))):
                        at = b if isinstance(b, int) else bass.ds(b, 1)
                        one = slice(b, b + 1) if isinstance(b, int) else bass.ds(b, 1)
                        dve.tensor_scalar(normed[m][:], src[:, b, :], mean[:, one], rstd[:, one],
                                          ALU.subtract, ALU.mult).then_inc(s["normed"], 1)

                def split_kv(b, par):
                    dve.wait_ge(s["kv_scaled"], b + 1)
                    dve.tensor_copy(kv[par][0][:], kvf[:]).then_inc(s["kv_hi"], 1)
                    dve.wait_ge(s["kv_hi"], b + 1)
                    dve.tensor_tensor(kv[par][1][:], kvf[:], kv[par][0][:].bitcast(F32), ALU.subtract).then_inc(s["kv_lo"], 1)

                def project(n, h):
                    dve.wait_ge(s["qk_hi"], n + 1)
                    dve.scalar_tensor_tensor(out=q[1][:, h, :], in0=psA[h % 2][:, 0:P], scalar=bq[:, h:h + 1],
                                             in1=q[0][:, h, :].bitcast(F32), op0=ALU.add, op1=ALU.subtract)
                    dve.scalar_tensor_tensor(out=k_[1][:, h, :], in0=psA[h % 2][:, P:3 * P], scalar=bk[:, h:h + 1],
                                             in1=k_[0][:, h, :].bitcast(F32), op0=ALU.add, op1=ALU.subtract).then_inc(s["qk_lo"], 1)

                def values(b, ch):
                    half, kt = divmod(ch, 2)
                    dve.wait_ge(s["v_done"], b * 4 + ch + 1)
                    at_least(dve, s["v_lo"], b * 4 + ch)
                    cols = slice(half * 512, (half + 1) * 512)
                    dve.tensor_tensor(vf[:], psV[:], bv[:, cols], ALU.add).then_inc(s["v_f"], 1)

                def values_lo(b, ch):
                    half, kt = divmod(ch, 2)
                    cols = slice(half * 512, (half + 1) * 512)
                    dve.wait_ge(s["v_hi"], b * 4 + ch + 1)
                    dve.tensor_tensor(v[1][:, kt, cols], vf[:], v[0][:, kt, cols].bitcast(F32), ALU.subtract).then_inc(s["v_lo"], 1)

                def maximum(n, h):
                    dve.wait_ge(s["s_done"], n + 1)
                    dve.tensor_reduce(nmax[:, h:h + 1], psS[h % 2][:], AX.X, ALU.max, negate=True).then_inc(s["max_done"], 1)

                def normalize(n, h):
                    dve.wait_ge(s["exp_done"], n + 1)
                    dve.reciprocal(rsum[:, h:h + 1], sums[:, h:h + 1]).then_inc(s["rsum_done"], 1)
                    dve.wait_ge(s["rsum_done"], n + 1)
                    dve.tensor_scalar(probs[:, h, :], probs[:, h, :], rsum[:, h:h + 1], None, ALU.mult).then_inc(s["p_done"], 1)

                def turn(n, h):
                    dve.wait_ge(s["pt_hi"], n + 1)
                    dve.tensor_tensor(pT[1][:, h, :, :], psT[:], pT[0][:, h, :, :].bitcast(F32), ALU.subtract).then_inc(s["pt_lo"], 1)

                def apply(n, h):
                    dve.wait_ge(s["o_hi"], n + 1)
                    dve.tensor_tensor(oT[1][:, h, :], psO[:], oT[0][:, h, :].bitcast(F32), ALU.subtract).then_inc(s["o_lo"], 1)

                def residual(b):
                    dve.wait_ge(s["y_done"], b + 1)
                    dve.wait_ge(s["resid"], b + 1)
                    dve.scalar_tensor_tensor(out=x_sb[:, b, :], in0=psY[:], scalar=gates[:, 1:2], in1=x_sb[:, b, :],
                                             op0=ALU.mult, op1=ALU.add).then_inc(s["x_done"], 1)

                def steps(b, h, lags):
                    for lag, do in lags:
                        bb, hh = (b, h - lag) if h >= lag else (b - 1, h - lag + NH)
                        if exists(bb * NH + hh):
                            do(bb * NH + hh, hh)

                def batch(b, par, more):
                    for h in range(NH):
                        steps(b, h, ((2, maximum), (4, turn), (5, apply)))
                        if h - 1 in CHUNKS:
                            values_lo(b, CHUNKS[h - 1])
                        steps(b, h, ((2, normalize),))
                        if h == 2 and more:
                            norm(b + 1)
                        if h == 5 and exists((b - 1) * NH):
                            residual(b - 1)
                        if h == 7 and more:
                            split_kv(b + 1, 1 - par)
                        project(b * NH + h, h)
                        if h in CHUNKS:
                            values(b, CHUNKS[h])

                def finish():
                    for h in range(5):
                        steps(NB, h, ((2, maximum), (4, turn), (5, apply), (2, normalize)))
                    residual(NB - 1)

                norm(0)
                split_kv(0, 0)
                schedule(batch, finish, dve)


def mixture_1(nc, A, sb, ps, sem, NB, D, KD, x_sb, ctx_sb, ident, gates, x_mean, x_rstd, c_mean, c_rstd,
              x_stats, c_stats, nt):
    NE, _, F = A["fc1_T"].shape
    FS = A["sh1_T"].shape[1]
    NTOK = NB * P
    CAP = -(-(-(-NTOK * 2 // NE) * 5) // 4)
    NSLOT = NE * CAP
    xg = nc.dram_tensor("m1_sorted", (NSLOT + 2 * NTOK, D), F32, kind="Internal").ap()
    yg = nc.dram_tensor("m1_expert_out", (NSLOT + P, D), F32, kind="Internal").ap()
    KS = FS // P
    with ExitStack() as c:
        n_sb = sb("m1_n", [P, NB, D], F32, c)
        sh = sb("m1_shared", [P, NB, D], F32, c)
        b2s = sb("m1_b2s", [P, D], F32, c)
        into = [sb(f"m1_into{i}", [P, NB], U32, c) for i in range(2)]
        back = [sb(f"m1_back{i}", [P, NB], U32, c) for i in range(2)]
        wk = [sb(f"m1_wk{i}", [P, NB], F32, c) for i in range(2)]
        ones = sb("m1_ones", [P, P], F32, c)
        upper = sb("m1_upper", [P, P], F32, c)
        scattered = sem("m1_scattered", c)
        with ExitStack() as t:
            w1 = [sb(f"m1_ws1{n}", [P, KD, FS], F32R, t) for n in ("hi", "lo")]
            w2 = [sb(f"m1_ws2{n}", [P, KS, D], F32R, t) for n in ("hi", "lo")]
            b1 = sb("m1_bs1", [P, KS], F32, t)
            logits = sb("m1_logits", [P, NB, NE], F32, t)
            proj = sb("m1_proj", [P, KD, NE], F32, t)
            pb, eb = sb("m1_pb", [P, NE], F32, t), sb("m1_eb", [P, NE], F32, t)
            shared_weights(nc, A, sb, ps, sem, D, KD, KS, FS, w1, w2, b1, b2s, proj, pb, eb, ones, upper, gates, xg, yg, NSLOT, x_sb)
            hT = [sb(f"m1_hT{n}", [P, KD, NB, P], F32R, t) for n in ("hi", "lo")]
            token_norms(nc, sb, ps, sem, NB, D, KD, x_sb, ident, x_mean, x_rstd, x_stats, nt, n_sb, hT,
                        logits, proj, None, None, NE, "m1", False)
            wmat, cur, hots, ws = top2(nc, sb, ps, sem, NB, NE, logits, pb, eb, t)
            shared_gelu(nc, sb, ps, sem, 0, NB // 2, D, KD, KS, hT, w1, w2, b1, sh, gates, "a",
                        search=(NB, NE, CAP, wmat, cur, ones))
            places(nc, sb, ps, sem, NB, NE, CAP, NSLOT, NTOK, wmat, cur, hots, ws, into, back, wk, ones, upper, gates)
            shared_gelu(nc, sb, ps, sem, NB // 2, NB, D, KD, KS, hT, w1, w2, b1, sh, gates, "b",
                        scatter=(into, n_sb, xg, scattered, NB))
        experts_gelu(nc, A, sb, ps, sem, NB, NE, CAP, D, KD, F, x_sb, sh, b2s, ident, xg, yg, n_sb, back, wk, scattered)


def shared_weights(nc, A, sb, ps, sem, D, KD, KS, FS, w1, w2, b1, b2s, proj, pb, eb, ones, upper, gates, xg, yg, NSLOT, x_sb):
    with ExitStack() as c:
        raw1 = sb("d_raw1", [P, KD, FS], F32, c)
        raw2 = sb("d_raw2", [P, KS, D], F32, c)
        zeros = sb("d_zeros", [P, D], F32, c)
        s = {n: sem(f"d_{n}", c) for n in "w1_in w2_in small_in hi lo const_done zero_out".split()}
        flat = lambda t: t.rearrange("p a n -> p (a n)")
        with nc.Block() as block:
            @block.sync
            def _(sp):
                sp.dma_start(raw1[:], A["sh1_T"].rearrange("(k p) f -> p k f", p=P)).then_inc(s["w1_in"], 16)
                sp.dma_start(raw2[:], A["sh2_T"].rearrange("(k p) d -> p k d", p=P)).then_inc(s["w2_in"], 16)
                with nc.allow_non_contiguous_dma(reason="a few hundred small parameters"):
                    for dst, src in ((b1[:], A["L1_ffn_sh1_b"].rearrange("(k p) -> p k", p=P)),
                                     (b2s[:], A["L1_ffn_sh2_b"].partition_broadcast(P)),
                                     (proj[:], A["proj_T"].rearrange("(k p) e -> p k e", p=P)),
                                     (pb[:], A["L1_ffn_proj_b"].partition_broadcast(P)),
                                     (eb[:], A["L1_ffn_expert_bias"].partition_broadcast(P))):
                        sp.dma_start(dst, src).then_inc(s["small_in"], 16)
                sp.wait_ge(s["const_done"], 2)
                sp.dma_start(xg[0:NSLOT].rearrange("(t p) d -> p t d", p=P), zeros[:].unsqueeze(1).to_broadcast([P, NSLOT // P, D]))\
                  .then_inc(s["zero_out"], 16)
                sp.dma_start(yg[NSLOT:NSLOT + P], zeros[:]).then_inc(s["zero_out"], 16)
                sp.wait_ge(s["zero_out"], 32)
                sp.wait_ge(s["small_in"], 80)

            @block.gpsimd
            def _(pool):
                pool.memset(zeros[:], 0.0).then_inc(s["const_done"], 1)
                pool.memset(ones[:], 1.0).then_inc(s["const_done"], 1)
                pool.wait_ge(s["const_done"], 2)
                pool.affine_select(out=upper[:], in_=ones[:], compare_op=ALU.is_gt, fill=0.0, base=0,
                                   pattern=[[1, P]], channel_multiplier=-1).then_inc(s["const_done"], 1)

            @block.scalar
            def _(act):
                act.wait_ge(s["w1_in"], 16)
                act.activation(flat(w1[0][:]), flat(raw1[:]), ACT.Copy).then_inc(s["hi"], 1)
                act.wait_ge(s["w2_in"], 16)
                act.activation(flat(w2[0][:]), flat(raw2[:]), ACT.Copy).then_inc(s["hi"], 1)

            @block.vector
            def _(dve):
                for n, (w, raw) in enumerate(((w1, raw1), (w2, raw2))):
                    dve.wait_ge(s["hi"], n + 1)
                    dve.tensor_tensor(flat(w[1][:]), flat(raw[:]), flat(w[0][:]).bitcast(F32), ALU.subtract)
                dve.wait_ge(s["small_in"], 80)
                dve.tensor_scalar(b2s[:], b2s[:], gates[:, 3:4], None, ALU.mult)


def top2(nc, sb, ps, sem, NB, NE, logits, pb, eb, c):
    wmat = sb("r1_wmat", [P, NB, NE], F32, c)
    hots = [sb(f"r1_hot{i}", [P, NB, NE], F32, c) for i in range(2)]
    ws = [sb(f"r1_w{i}", [P, NB], F32, c) for i in range(2)]
    cur = sb("r1_cur", [P, NE], I32, c)
    with ExitStack() as t:
        z = sb("r1_z", [P, NB, NE], F32, t)
        sg = sb("r1_sg", [P, NB, NE], F32, t)
        best = sb("r1_best", [P, NB, 8], F32, t)
        index = sb("r1_index", [P, NB, 8], U32, t)
        which = sb("r1_which", [P, 2, NB], F32, t)
        iota_i = sb("r1_iota_i", [P, NE], I32, t)
        iota = sb("r1_iota", [P, NE], F32, t)
        tmp = sb("r1_tmp", [P, NB, NE], F32, t)
        total = sb("r1_total", [P, NB], F32, t)
        s = {n: sem(f"r1_{n}", t) for n in "steps iota_done biased sigmoid".split()}
        wide = lambda a: a.unsqueeze(2).to_broadcast([P, NB, NE])
        with nc.Block() as block:
            @block.gpsimd
            def _(pool):
                pool.iota(iota_i[:], pattern=[[1, NE]], base=0, channel_multiplier=0).then_inc(s["iota_done"], 1)

            @block.scalar
            def _(act):
                act.wait_ge(s["biased"], 1)
                act.activation(sg[:], z[:], ACT.Sigmoid).then_inc(s["sigmoid"], 1)

            @block.vector
            def _(dve):
                k = Steps(dve, s["steps"])
                dve.tensor_tensor(z[:], logits[:], pb[:].unsqueeze(1).to_broadcast([P, NB, NE]), ALU.add).then_inc(s["biased"], 1)
                dve.memset(cur[:], 0)
                dve.wait_ge(s["iota_done"], 1)
                k.step(dve.tensor_copy(iota[:], iota_i[:]))
                dve.wait_ge(s["sigmoid"], 1)
                k.step(dve.tensor_tensor(sg[:], sg[:], eb[:].unsqueeze(1).to_broadcast([P, NB, NE]), ALU.add))
                k.step(dve.tensor_scalar(sg[:], sg[:], 1e-12, None, ALU.max))
                for i in range(NB):
                    ins = dve.max(best[:, i, :], sg[:, i, :])
                k.step(ins)
                for i in range(NB):
                    ins = dve.max_index(index[:, i, :], best[:, i, :], sg[:, i, :])
                k.step(ins)
                for n in range(2):
                    ins = dve.tensor_copy(which[:, n, :], index[:, :, n])
                k.step(ins)
                k.step(dve.tensor_tensor(total[:], best[:, :, 0], best[:, :, 1], ALU.add))
                k.step(dve.reciprocal(total[:], total[:]))
                for n in range(2):
                    dve.tensor_tensor(ws[n][:], best[:, :, n], total[:], ALU.mult)
                    ins = dve.tensor_tensor(hots[n][:], wide(which[:, n, :]), iota[:].unsqueeze(1).to_broadcast([P, NB, NE]),
                                            ALU.is_equal)
                k.step(ins)
                dve.tensor_tensor(wmat[:], hots[0][:], wide(ws[0][:]), ALU.mult)
                k.step(dve.tensor_tensor(tmp[:], hots[1][:], wide(ws[1][:]), ALU.mult))
                dve.tensor_tensor(wmat[:], wmat[:], tmp[:], ALU.add)
    return wmat, cur, hots, ws


def shared_gelu(nc, sb, ps, sem, first_tile, end_tile, D, KD, KS, hT, w1, w2, b1, sh, gates, tag, search=None, scatter=None):
    PAIRS = (end_tile - first_tile) // 2
    NQ = KS // 2
    with ExitStack() as c:
        g = [sb(f"s1{tag}_g{i}", [P, 2, 2 * P], F32, c) for i in range(2)]
        gs = [[sb(f"s1{tag}_g{n}{i}", [P, KS, 2 * P], F32R, c) for n in ("hi", "lo")] for i in range(2)]
        psH = [ps(f"s1{tag}_psH{i}", [P, 2, 2 * P], F32, c) for i in range(NQ)]
        psY = [ps(f"s1{tag}_psY{i}", [P, D], F32, c) for i in range(2)]
        s = {n: sem(f"s1{tag}_{n}", c) for n in "up gelu g_hi g_lo down kept start counted count_out found".split()}
        if search:
            NB, NE, CAP, wmat, cur, ones = search
            ROUNDS, CANDS = 4, 3
            assert PAIRS * ROUNDS * 2 >= 31
            bits = sb("s1_bits", [P, CANDS, NE], I32, c)
            cand = sb("s1_cand", [P, CANDS, NE], I32, c)
            pass_ = sb("s1_pass", [P, CANDS, NE], F32, c)
            take = sb("s1_take", [P, NE], I32, c)
            over = sb("s1_over", [P, CANDS * NE, NB], F32, c)
            count = sb("s1_count", [P, CANDS * NE], F32, c)
            psC = ps("s1_psC", [P, CANDS, NE], F32, c)
        with nc.Block() as block:
            if scatter:
                @block.gpsimd
                def _(pool):
                    into, n_sb, xg, scattered, NB = scatter
                    for i in range(NB):
                        for n in range(2):
                            pool.indirect_dma_start(xg, bass.IndirectOffsetOnAxis(ap=into[n][:, i:i + 1], axis=0), n_sb[:, i, :], None)\
                                .then_inc(scattered, 16)

            @block.tensor
            def _(pe):
                def up(i, q):
                    at_least(pe, s["gelu"], (i - 1) * NQ + q + 1)
                    tiles = slice(first_tile + 2 * i, first_tile + 2 * i + 2)
                    for j in range(2):
                        t = 2 * q + j
                        for m, (a, (x, y)) in enumerate([(a, xy) for a in range(KD) for xy in PARTS3]):
                            ins = pe.matmul(psH[q][:, j, :], w1[x][:, a, t * P:(t + 1) * P],
                                            hT[y][:, a, tiles, :].rearrange("p b t -> p (b t)"), start=(m == 0), stop=(m == 3 * KD - 1))
                    ins.then_inc(s["up"], 1)

                def down(i, j):
                    pe.wait_ge(s["g_lo"], i * NQ + NQ)
                    at_least(pe, s["kept"], (i - 1) * 2 + j + 1)
                    for m, (t, (x, y)) in enumerate([(t, xy) for t in range(KS) for xy in PARTS3]):
                        ins = pe.matmul(psY[j][:], gs[i % 2][x][:, t, j * P:(j + 1) * P], w2[y][:, t, :], start=(m == 0), stop=(m == 3 * KS - 1))
                    ins.then_inc(s["down"], 1)

                def tally(i, r):
                    if search:
                        pe.wait_ge(s["counted"], i * ROUNDS + r + 1)
                        pe.matmul(psC[:].rearrange("p c e -> p (c e)"), ones[:], count[:], start=True, stop=True).then_inc(s["count_out"], 1)

                for q in range(NQ):
                    up(0, q)
                for i in range(PAIRS):
                    for q in range(NQ):
                        if i + 1 < PAIRS:
                            up(i + 1, q)
                        if q in (0, 2):
                            tally(i, q // 2)
                    down(i, 0)
                    tally(i, 2)
                    down(i, 1)
                    tally(i, 3)

            @block.scalar
            def _(act):
                def gelu(i, q):
                    act.wait_ge(s["up"], i * NQ + q + 1)
                    at_least(act, s["g_lo"], i * NQ + q - 1)
                    at_least(act, s["down"], (i - 1) * 2)
                    for j in range(2):
                        t = 2 * q + j
                        ins = act.activation(g[q % 2][:, j, :], psH[q][:, j, :], ACT.Gelu, bias=b1[:, t:t + 1])
                    ins.then_inc(s["gelu"], 1)
                    act.wait_ge(s["gelu"], i * NQ + q + 1)
                    act.activation(gs[i % 2][0][:, 2 * q:2 * q + 2, :], g[q % 2][:], ACT.Copy).then_inc(s["g_hi"], 1)

                def keep(i, j):
                    act.wait_ge(s["down"], i * 2 + j + 1)
                    act.activation(sh[:, first_tile + 2 * i + j, :], psY[j][:], ACT.Copy, scale=gates[:, 3:4]).then_inc(s["kept"], 1)

                for i in range(PAIRS + 1):
                    for q in range(NQ):
                        if i < PAIRS:
                            gelu(i, q)
                        if i > 0 and q == 1:
                            keep(i - 1, 0)
                    if i > 0:
                        keep(i - 1, 1)

            @block.vector
            def _(dve):
                def split(i, q):
                    dve.wait_ge(s["g_hi"], i * NQ + q + 1)
                    dve.tensor_tensor(gs[i % 2][1][:, 2 * q:2 * q + 2, :], g[q % 2][:], gs[i % 2][0][:, 2 * q:2 * q + 2, :].bitcast(F32),
                                      ALU.subtract).then_inc(s["g_lo"], 1)

                STEPS = 5

                def count_over(i, r):
                    if not search:
                        return
                    k = Steps(dve, s["found"], (i * ROUNDS + r) * STEPS)
                    k.step(dve.tensor_tensor(over[:].rearrange("p (c e) b -> p c b e", e=NE),
                                             wmat[:].unsqueeze(1).to_broadcast([P, CANDS, NB, NE]),
                                             cand[:].bitcast(F32).unsqueeze(2).to_broadcast([P, CANDS, NB, NE]), ALU.is_ge))
                    dve.tensor_reduce(count[:], over[:], AX.X, ALU.add).then_inc(s["counted"], 1)

                def raise_bar(i, r):
                    if not search:
                        return
                    k = Steps(dve, s["found"], (i * ROUNDS + r) * STEPS + 1)
                    dve.wait_ge(s["count_out"], i * ROUNDS + r + 1)
                    k.step(dve.scalar_tensor_tensor(out=pass_[:], in0=psC[:], scalar=float(CAP), in1=bits[:],
                                                    op0=ALU.is_ge, op1=ALU.mult))
                    dve.tensor_scalar(bits[:], bits[:], 2, None, ALU.logical_shift_right)
                    k.step(dve.tensor_reduce(take[:], pass_[:].rearrange("p c e -> p e c"), AX.X, ALU.max))
                    k.step(dve.tensor_tensor(cur[:], cur[:], take[:], ALU.bitwise_or))
                    k.step(dve.tensor_tensor(cand[:], bits[:], cur[:].unsqueeze(1).to_broadcast([P, CANDS, NE]), ALU.bitwise_or))
                    assert k.n == STEPS - 1

                if search:
                    k = Steps(dve, s["start"])
                    for n in range(CANDS):
                        ins = dve.memset(bits[:, n, :], (n + 1) << 29)
                    k.step(ins)
                    k.step(dve.tensor_copy(cand[:], bits[:]))
                for q in range(NQ):
                    split(0, q)
                for i in range(PAIRS):
                    more = i + 1 < PAIRS
                    count_over(i, 0)
                    raise_bar(i, 0)
                    if more:
                        split(i + 1, 0)
                    count_over(i, 1)
                    if more:
                        split(i + 1, 1)
                    raise_bar(i, 1)
                    if more:
                        split(i + 1, 2)
                    count_over(i, 2)
                    if more:
                        split(i + 1, 3)
                    raise_bar(i, 2)
                    count_over(i, 3)
                    raise_bar(i, 3)


def places(nc, sb, ps, sem, NB, NE, CAP, NSLOT, NTOK, wmat, cur, hots, ws, into, back, wk, ones, upper, gates):
    with ExitStack() as c:
        over = sb("p1_over", [P, NB, NE], F32, c)
        equal = sb("p1_equal", [P, NB, NE], F32, c)
        tmp = sb("p1_tmp", [P, NB, NE], F32, c)
        tot = sb("p1_tot", [P, NB, NE], F32, c)
        pre = [sb(f"p1_pre{i}", [P, NB, NE], F32, c) for i in range(2)]
        rank = sb("p1_rank", [P, NB, NE], F32, c)
        kept = sb("p1_kept", [P, NB, NE], F32, c)
        nover = sb("p1_nover", [P, NE], F32, c)
        room = sb("p1_room", [P, NE], F32, c)
        first_i = sb("p1_first_i", [P, NE], I32, c)
        first = sb("p1_first", [P, NE], F32, c)
        token_i = sb("p1_token_i", [P, NB], I32, c)
        token = sb("p1_token", [P, NB], F32, c)
        at, has, lost = (sb(f"p1_{n}", [P, NB], F32, c) for n in ("at", "has", "lost"))
        psR = ps("p1_ps", [P, 3, NB * NE], F32, c)
        psK = ps("p1_psK", [P, 2, NB * NE], F32, c)
        s = {n: sem(f"p1_{n}", c) for n in "steps iota_done marked ranked kept_done ranked2".split()}
        flat = lambda t: t[:].rearrange("p b e -> p (b e)")
        three = lambda t: t.rearrange("p (b e) -> p b e", e=NE)
        wide = lambda a: a.unsqueeze(1).to_broadcast([P, NB, NE])
        with nc.Block() as block:
            @block.gpsimd
            def _(pool):
                pool.iota(first_i[:], pattern=[[CAP, NE]], base=0, channel_multiplier=0).then_inc(s["iota_done"], 1)
                pool.iota(token_i[:], pattern=[[P, NB]], base=NSLOT, channel_multiplier=1).then_inc(s["iota_done"], 1)

            @block.tensor
            def _(pe):
                pe.wait_ge(s["marked"], 1)
                pe.matmul(psR[:, 0, :], upper[:], flat(equal), start=True, stop=True)
                pe.matmul(psR[:, 1, :], ones[:], flat(equal), start=True, stop=True)
                pe.matmul(psR[:, 2, :], ones[:], flat(over), start=True, stop=True).then_inc(s["ranked"], 1)
                pe.wait_ge(s["kept_done"], 1)
                pe.matmul(psK[:, 0, :], upper[:], flat(kept), start=True, stop=True)
                pe.matmul(psK[:, 1, :], ones[:], flat(kept), start=True, stop=True).then_inc(s["ranked2"], 1)

            @block.vector
            def _(dve):
                k = Steps(dve, s["steps"])
                bar = cur[:].bitcast(F32)
                dve.tensor_tensor(over[:], wmat[:], wide(bar), ALU.is_gt)
                k.step(dve.tensor_tensor(tmp[:], wmat[:], wide(bar), ALU.is_equal))
                dve.scalar_tensor_tensor(out=equal[:], in0=wmat[:], scalar=0.0, in1=tmp[:], op0=ALU.is_gt, op1=ALU.mult)\
                   .then_inc(s["marked"], 1)
                dve.wait_ge(s["iota_done"], 2)
                dve.tensor_copy(first[:], first_i[:])
                k.step(dve.tensor_copy(token[:], token_i[:]))

                def before(psX):
                    k.step(dve.tensor_copy(tot[:], three(psX[:, 1, :])))
                    incl = prefix_steps(dve, k, tot, pre, NB)
                    k.step(dve.tensor_tensor(rank[:], three(psX[:, 0, :]), incl[:], ALU.add))
                    k.step(dve.tensor_tensor(rank[:], rank[:], tot[:], ALU.subtract))

                dve.wait_ge(s["ranked"], 1)
                before(psR)
                k.step(dve.tensor_reduce(nover[:], psR[:, 2, :].rearrange("p (b e) -> p e b", e=NE), AX.X, ALU.add))
                k.step(dve.tensor_scalar(room[:], nover[:], -1.0, float(CAP), ALU.mult, ALU.add))
                k.step(dve.tensor_tensor(rank[:], rank[:], wide(room[:]), ALU.is_lt))
                k.step(dve.tensor_tensor(rank[:], rank[:], equal[:], ALU.mult))
                k.step(dve.tensor_tensor(kept[:], rank[:], over[:], ALU.add))
                dve.tensor_copy(tmp[:], kept[:]).then_inc(s["kept_done"], 1)
                dve.wait_ge(s["ranked2"], 1)
                before(psK)
                k.step(dve.tensor_tensor(rank[:], rank[:], wide(first[:]), ALU.add))
                k.step(dve.tensor_tensor(rank[:], rank[:], kept[:], ALU.mult))
                for n in range(2):
                    k.step(dve.tensor_tensor(tmp[:], hots[n][:], rank[:], ALU.mult))
                    k.step(dve.tensor_reduce(at[:], tmp[:], AX.X, ALU.add))
                    k.step(dve.tensor_tensor(tmp[:], hots[n][:], kept[:], ALU.mult))
                    k.step(dve.tensor_reduce(has[:], tmp[:], AX.X, ALU.add))
                    k.step(dve.tensor_scalar(lost[:], has[:], -1.0, 1.0, ALU.mult, ALU.add))
                    k.step(dve.scalar_tensor_tensor(out=back[n][:], in0=lost[:], scalar=float(NSLOT), in1=at[:],
                                                    op0=ALU.mult, op1=ALU.add))
                    k.step(dve.scalar_tensor_tensor(out=lost[:], in0=token[:], scalar=float(n * NTOK), in1=lost[:],
                                                    op0=ALU.add, op1=ALU.mult))
                    k.step(dve.tensor_tensor(into[n][:], lost[:], at[:], ALU.add))
                    k.step(dve.tensor_tensor(wk[n][:], ws[n][:], has[:], ALU.mult))
                    k.step(dve.tensor_scalar(wk[n][:], wk[n][:], gates[:, 3:4], None, ALU.mult))


def experts_gelu(nc, A, sb, ps, sem, NB, NE, CAP, D, KD, F, x_sb, sh, b2s, ident, xg, yg, n_sb, back, wk, scattered):
    KF, NT, HALF = F // P, CAP // P, CAP // 2
    assert CAP % P == 0 and HALF <= 512 and KD * F == KF * D
    with ExitStack() as c:
        raw = [sb(f"x1_raw{i}", [P, 2, KD * F], F32, c) for i in range(2)]
        w1 = [[sb(f"x1_w1{n}{i}", [P, KD, F], F32R, c) for n in ("hi", "lo")] for i in range(2)]
        w2 = [[sb(f"x1_w2{n}{i}", [P, KF, D], F32R, c) for n in ("hi", "lo")] for i in range(2)]
        b1 = sb("x1_b1", [P, NE, KF], F32, c)
        b1e = [sb(f"x1_b1e{i}", [P, KF], F32, c) for i in range(2)]
        b2 = sb("x1_b2", [P, NE, D], F32, c)
        xin = [sb(f"x1_xin{i}", [P, NT, D], F32, c) for i in range(2)]
        xT = [sb(f"x1_xT{n}", [P, KD, CAP], F32R, c) for n in ("hi", "lo")]
        g = sb("x1_g", [P, KF, CAP], F32, c)
        gs = [sb(f"x1_g{n}", [P, KF, CAP], F32R, c) for n in ("hi", "lo")]
        y = [sb(f"x1_y{i}", [P, D], F32, c) for i in range(2)]
        psX = [ps(f"x1_psX{i}", [P, KD, P], F32, c) for i in range(2)]
        psH = [ps(f"x1_psH{i}", [P, HALF], F32, c) for i in range(4)]
        psY = [ps(f"x1_psY{i}", [P, D], F32, c) for i in range(2)]
        names = ("w_in0 w_in1 b_in x_in0 x_in1 turned xt_hi xt_lo w_hi w_lo up gelu g_hi g_lo down y_done y_out0 y_out1 "
                 "x_gated x_biased combined").split()
        s = {n: sem(f"x1_{n}", c) for n in names}
        w_in, x_in, y_out = [s["w_in0"], s["w_in1"]], [s["x_in0"], s["x_in1"]], [s["y_out0"], s["y_out1"]]
        xg_t = xg[0:NE * CAP].rearrange("(e t p) d -> e p t d", p=P, t=NT)
        yg_t = yg[0:NE * CAP].rearrange("(e t p) d -> e t p d", p=P, t=NT)
        NC = 2 * KF
        chunk = lambda m: (m % KF, m // KF)
        gathered = [[sem(f"x1_gathered{n}_{i}", c) for i in range(NB)] for n in range(2)]

        flat = lambda t: t.rearrange("p a n -> p (a n)")
        parts_of = lambda b: ((w1[b], raw[b][:, 0, :]), (w2[b], raw[b][:, 1, :]))

        with nc.Block() as block:
            @block.sync
            def _(sp):
                def load_w(e, b):
                    sp.dma_start(raw[b][:, 0, :].rearrange("p (k f) -> p k f", k=KD), A["fc1_T"][e].rearrange("(k p) f -> p k f", p=P))\
                      .then_inc(w_in[b], 16)
                    sp.dma_start(raw[b][:, 1, :].rearrange("p (k d) -> p k d", k=KF), A["fc2_T"][e].rearrange("(k p) d -> p k d", p=P))\
                      .then_inc(w_in[b], 16)

                def load_x(e, b):
                    sp.dma_start(xin[b][:], xg_t[e]).then_inc(x_in[b], 16)

                load_w(0, 0)
                load_w(1, 1)
                with nc.allow_non_contiguous_dma(reason="a few thousand small parameters"):
                    sp.dma_start(b1[:], A["L1_ffn_fc1_b"].rearrange("e (k p) -> p e k", p=P)).then_inc(s["b_in"], 16)
                    sp.dma_start(b2[:], A["L1_ffn_fc2_b"].partition_broadcast(P)).then_inc(s["b_in"], 16)
                sp.wait_ge(scattered, 2 * NB * 16)
                load_x(0, 0)
                load_x(1, 1)

                def stores(e):
                    for t in range(NT):
                        b = (e_par * NT + t) % 2
                        sp.wait_ge(s["y_done"], e * NT + t + 1)
                        sp.dma_start(yg_t[e, t], y[b][:]).then_inc(y_out[b], 16)

                with sp.Fori(0, NE // 2 - 1) as i:
                    for e_par in range(2):
                        sp.wait_ge(s["w_lo"], i * 2 + e_par + 1)
                        load_w(i * 2 + e_par + 2, e_par)
                        sp.wait_ge(s["turned"], (i * 2 + e_par + 1) * NT)
                        load_x(i * 2 + e_par + 2, e_par)
                        stores(i * 2 + e_par)
                for e_par in range(2):
                    stores(NE - 2 + e_par)

            @block.tensor
            def _(pe):
                def turn(e, b, pair, t):
                    if t == 0:
                        pe.wait_ge(x_in[b], pair * 16 + 16)
                    at_least(pe, s["xt_lo"], e * NT + t - 1)
                    for a in range(KD):
                        ins = pe.transpose(psX[(b * NT + t) % 2][:, a, :], xin[b][:, t, a * P:(a + 1) * P], ident[:])
                    ins.then_inc(s["turned"], 1)

                def up(e, b):
                    pe.wait_ge(s["w_lo"], e + 1)
                    pe.wait_ge(s["xt_lo"], e * NT + NT)
                    for m in range(NC):
                        f, half = chunk(m)
                        at_least(pe, s["gelu"], e * NC + m - 3)
                        rows = slice(half * HALF, (half + 1) * HALF)
                        for n, (a, (x, y_)) in enumerate([(a, xy) for a in range(KD) for xy in PARTS3]):
                            ins = pe.matmul(psH[m % 4][:], w1[b][x][:, a, f * P:(f + 1) * P], xT[y_][:, a, rows],
                                            start=(n == 0), stop=(n == 3 * KD - 1))
                        ins.then_inc(s["up"], 1)

                def down(e, b, t):
                    if t == 0:
                        pe.wait_ge(s["g_lo"], e * NC + KF)
                    if t == HALF // P:
                        pe.wait_ge(s["g_lo"], e * NC + NC)
                    at_least(pe, s["y_done"], e * NT + t - 1)
                    for n, (f, (x, y_)) in enumerate([(f, xy) for f in range(KF) for xy in PARTS3]):
                        ins = pe.matmul(psY[(b * NT + t) % 2][:], gs[x][:, f, t * P:(t + 1) * P], w2[b][y_][:, f, :],
                                        start=(n == 0), stop=(n == 3 * KF - 1))
                    ins.then_inc(s["down"], 1)

                def expert(e, b, pair, more=True):
                    up(e, b)
                    for t in range(NT):
                        if more:
                            turn(e + 1, 1 - b, pair + b, t)
                        down(e, b, t)

                for t in range(NT):
                    turn(0, 0, 0, t)
                expert(0, 0, 0)
                expert(1, 1, 0)
                with pe.Fori(1, NE // 2 - 1) as i:
                    for b in range(2):
                        expert(i * 2 + b, b, i)
                expert(NE - 2, 0, NE // 2 - 1)
                expert(NE - 1, 1, NE // 2 - 1, more=False)

            @block.scalar
            def _(act):
                def weights(e, b, pair):
                    act.wait_ge(w_in[b], pair * 32 + 32)
                    at_least(act, s["down"], (e - 1) * NT)
                    at_least(act, s["gelu"], (e - 1) * NC)
                    act.activation(b1e[b][:], b1[:, e, :], ACT.Copy)
                    for w, r in parts_of(b):
                        act.activation(flat(w[0][:]), r, ACT.Copy).then_inc(s["w_hi"], 1)

                def turn(e, b):
                    at_least(act, s["up"], e * NC)
                    for t in range(NT):
                        act.wait_ge(s["turned"], e * NT + t + 1)
                        act.activation(xT[0][:, :, t * P:(t + 1) * P], psX[(b * NT + t) % 2][:], ACT.Copy).then_inc(s["xt_hi"], 1)

                def gelu(e, b):
                    act.wait_ge(s["w_hi"], e * 2 + 2)
                    for m in range(NC):
                        f, half = chunk(m)
                        act.wait_ge(s["up"], e * NC + m + 1)
                        at_least(act, s["g_lo"], e * NC + m - NC + 1)
                        act.activation(g[:, f, half * HALF:(half + 1) * HALF], psH[m % 4][:], ACT.Gelu, bias=b1e[b][:, f:f + 1])\
                           .then_inc(s["gelu"], 1)

                def expert(e, b, pair, more=True):
                    gelu(e, b)
                    if more:
                        turn(e + 1, 1 - b)
                        if not (isinstance(e, int) and e == NE - 2):
                            weights(e + 2, b, pair + 1)

                act.wait_ge(s["b_in"], 32)
                weights(0, 0, 0)
                weights(1, 1, 0)
                turn(0, 0)
                expert(0, 0, 0)
                expert(1, 1, 0)
                with act.Fori(1, NE // 2 - 1) as i:
                    for b in range(2):
                        expert(i * 2 + b, b, i)
                expert(NE - 2, 0, NE // 2 - 1)
                expert(NE - 1, 1, NE // 2 - 1, more=False)

            @block.gpsimd
            def _(pool):
                def weights(e, b):
                    for n, (w, r) in enumerate(parts_of(b)):
                        pool.wait_ge(s["w_hi"], e * 2 + n + 1)
                        ins = pool.tensor_tensor(flat(w[1][:]), r, flat(w[0][:]).bitcast(F32), ALU.subtract)
                    ins.then_inc(s["w_lo"], 1)

                def residual(i):
                    pool.tensor_tensor(x_sb[:, i, :], x_sb[:, i, :], b2s[:], ALU.add).then_inc(s["x_biased"], 1)
                    pool.wait_ge(s["x_biased"], i + 1)
                    pool.tensor_tensor(x_sb[:, i, :], x_sb[:, i, :], sh[:, i, :], ALU.add).then_inc(s["x_gated"], 1)

                with pool.Fori(0, NE // 2) as i:
                    for b in range(2):
                        weights(i * 2 + b, b)
                        for n in range(NB // NE):
                            residual((i * 2 + b) * (NB // NE) + n)
                for b in range(2):
                    pool.wait_ge(y_out[b], NE * NT // 2 * 16)
                pool.wait_ge(s["x_gated"], NB)
                for i in range(NB):
                    for n, dst in enumerate((n_sb, sh)):
                        pool.indirect_dma_start(dst[:, i, :], None, yg, bass.IndirectOffsetOnAxis(ap=back[n][:, i:i + 1], axis=0))\
                            .then_inc(gathered[n][i], 16)

            @block.vector
            def _(dve):
                def turn(e, b, t):
                    at_least(dve, s["up"], e * NC)
                    cols = slice(t * P, (t + 1) * P)
                    dve.wait_ge(s["xt_hi"], e * NT + t + 1)
                    dve.tensor_tensor(xT[1][:, :, cols], psX[(b * NT + t) % 2][:], xT[0][:, :, cols].bitcast(F32), ALU.subtract)\
                       .then_inc(s["xt_lo"], 1)

                def split(e, b):
                    at_least(dve, s["down"], e * NT)
                    for m in range(NC):
                        f, half = chunk(m)
                        rows = slice(half * HALF, (half + 1) * HALF)
                        dve.wait_ge(s["gelu"], e * NC + m + 1)
                        dve.tensor_copy(gs[0][:, f, rows], g[:, f, rows]).then_inc(s["g_hi"], 1)
                        dve.wait_ge(s["g_hi"], e * NC + m + 1)
                        dve.tensor_tensor(gs[1][:, f, rows], g[:, f, rows], gs[0][:, f, rows].bitcast(F32), ALU.subtract)\
                           .then_inc(s["g_lo"], 1)

                def out(e, b, pair, t):
                    yb = (b * NT + t) % 2
                    dve.wait_ge(s["down"], e * NT + t + 1)
                    at_least(dve, y_out[yb], (pair * NT + (b * NT + t) // 2) * 16)
                    dve.tensor_tensor(y[yb][:], psY[yb][:], b2[:, e, :], ALU.add).then_inc(s["y_done"], 1)

                def expert(e, b, pair, more=True):
                    split(e, b)
                    for t in range(NT):
                        if more:
                            turn(e + 1, 1 - b, t)
                        out(e, b, pair, t)

                dve.wait_ge(s["b_in"], 32)
                for t in range(NT):
                    turn(0, 0, t)
                expert(0, 0, 0)
                expert(1, 1, 0)
                with dve.Fori(1, NE // 2 - 1) as i:
                    for b in range(2):
                        expert(i * 2 + b, b, i)
                expert(NE - 2, 0, NE // 2 - 1)
                expert(NE - 1, 1, NE // 2 - 1, more=False)
                for i in range(NB):
                    for n, src in enumerate((n_sb, sh)):
                        dve.wait_ge(gathered[n][i], 16)
                        dve.wait_ge(s["x_gated"], i + 1)
                        ins = dve.scalar_tensor_tensor(out=x_sb[:, i, :], in0=src[:, i, :], scalar=wk[n][:, i:i + 1],
                                                       in1=x_sb[:, i, :], op0=ALU.mult, op1=ALU.add)
                        ins.then_inc(s["combined"], 1)
                        dve.wait_ge(s["combined"], i * 2 + n + 1)


def laid_out(inputs):
    import numpy as np

    a = {k: np.ascontiguousarray(v) for k, v in inputs.items()}
    wo = a["L0_xattn_Wo"]
    a["L0_xattn_Wo"] = np.ascontiguousarray(wo.reshape(2, 4, 2, 16, -1).transpose(1, 0, 2, 3, 4).reshape(wo.shape))
    a["router_T"] = np.ascontiguousarray(a["L0_ffn_router_w"].T)
    a["proj_T"] = np.ascontiguousarray(a["L1_ffn_proj_w"].T)
    a["sh1_T"] = np.ascontiguousarray(a["L1_ffn_sh1_w"].T)
    a["sh2_T"] = np.ascontiguousarray(a["L1_ffn_sh2_w"].T)
    a["fc1_T"] = np.ascontiguousarray(a["L1_ffn_fc1_w"].transpose(0, 2, 1))
    a["fc2_T"] = np.ascontiguousarray(a["L1_ffn_fc2_w"].transpose(0, 2, 1))
    for k in ("L0_ffn_router_w", "L1_ffn_proj_w", "L1_ffn_sh1_w", "L1_ffn_sh2_w", "L1_ffn_fc1_w", "L1_ffn_fc2_w"):
        del a[k]
    return a


def kernel(**inputs):
    import concourse.bacc as bacc
    from concourse.bass_utils import run_bass_kernel_spmd

    nc = bacc.Bacc("TRN2", target_bir_lowering=False, num_devices=1)
    arrays = {f"in_{k}": v for k, v in laid_out(inputs).items()}
    A = {k[3:]: nc.dram_tensor(k, v.shape, mybir.dt.from_np(v.dtype), kind="ExternalInput").ap() for k, v in arrays.items()}
    out = nc.dram_tensor("out", arrays["in_x"].shape, F32, kind="ExternalOutput").ap()
    program(nc, A, out)
    return run_bass_kernel_spmd(nc, [arrays], core_ids=[0]).results[0]["out"]
```

```python
from contextlib import ExitStack

import concourse.bass as bass
from concourse import mybir

F32 = mybir.dt.float32
F32R = mybir.dt.float32r
BF16 = mybir.dt.bfloat16
I32 = mybir.dt.int32
U32 = mybir.dt.uint32
ALU = mybir.AluOpType
ACT = mybir.ActivationFunctionType
AX = mybir.AxisListType

P = 128
LN_EPS = 1e-5


PARTS3 = ((0, 0), (0, 1), (1, 0))


def at_least(eng, sem, value):
    if isinstance(value, int) and value <= 0:
        return
    eng.wait_ge(sem, value)


def recycle(nc):
    used = sorted(x for x in nc.released_uncleared_semaphores)
    with nc.Block() as block:
        @block.gpsimd
        def _(pool):
            start = 0
            for n in range(1, len(used) + 1):
                if n == len(used) or used[n] != used[n - 1] + 1:
                    pool.sem_clear(range(used[start], used[n - 1] + 1))
                    start = n


class Steps:

    def __init__(self, eng, sem, base=0):
        self.eng, self.sem, self.base, self.n = eng, sem, base, 0

    def step(self, ins):
        ins.then_inc(self.sem, 1)
        self.n += 1
        self.eng.wait_ge(self.sem, self.base + self.n)


def rsqrt_steps(dve, s, y, v, a, b):
    vi, ai = v.bitcast(I32), a.bitcast(I32)
    s.step(dve.tensor_scalar(ai, vi, 1, None, ALU.logical_shift_right))
    s.step(dve.tensor_scalar(y.bitcast(I32), ai, -1.0, float(0x5F3759DF), ALU.mult, ALU.add))
    for _ in range(4):
        s.step(dve.tensor_tensor(a, y, y, ALU.mult))
        s.step(dve.tensor_tensor(b, a, v, ALU.mult))
        s.step(dve.tensor_scalar(a, b, -0.5, 1.5, ALU.mult, ALU.add))
        s.step(dve.tensor_tensor(y, y, a, ALU.mult))


def norm_steps(dve, s, stats, mean, rstd, tmp, twice):
    a, b, v = tmp
    s.step(dve.tensor_tensor(mean, stats[:, :, 1], stats[:, :, 4], ALU.add))
    s.step(dve.tensor_scalar(mean, mean, 0.5, None, ALU.mult))
    s.step(dve.tensor_tensor(a, stats[:, :, 1], stats[:, :, 4], ALU.subtract))
    s.step(dve.scalar_tensor_tensor(out=b, in0=a, scalar=0.25, in1=a, op0=ALU.mult, op1=ALU.mult))
    s.step(dve.tensor_tensor(a, stats[:, :, 2], stats[:, :, 5], ALU.add))
    s.step(dve.scalar_tensor_tensor(out=v, in0=a, scalar=1.0 / 256, in1=b, op0=ALU.mult, op1=ALU.add))
    s.step(dve.tensor_scalar(a, v, LN_EPS, None, ALU.add))
    if not twice:
        s.step(dve.tensor_copy(v, a))
        rsqrt_steps(dve, s, rstd, v, a, b)
        return
    s.step(dve.scalar_tensor_tensor(out=v, in0=a, scalar=LN_EPS, in1=v, op0=ALU.mult, op1=ALU.add))
    rsqrt_steps(dve, s, rstd, v, a, b)


def program(nc, A, out):
    NB, S, D = A["x"].shape
    assert S == P and D == 256
    KD = D // P
    ctx = ExitStack()

    def sb(name, shape, dt=F32, where=ctx):
        return where.enter_context(nc.sbuf_tensor(name, shape, dt))

    def ps(name, shape, dt=F32, where=ctx):
        return where.enter_context(nc.psum_tensor(name, shape, dt))

    def sem(name, where=ctx):
        return where.enter_context(nc.semaphore(name))

    with ctx:
        x_sb = sb("x_sb", [P, NB, D])
        ctx_sb = sb("ctx_sb", [P, NB, D])
        ident = sb("ident", [P, P])
        gates = sb("gates", [P, 4])
        x_mean, x_rstd = sb("x_mean", [P, NB]), sb("x_rstd", [P, NB])
        c_mean, c_rstd = sb("c_mean", [P, NB]), sb("c_rstd", [P, NB])
        x_stats, c_stats = sb("x_stats", [P, NB, 6]), sb("c_stats", [P, NB, 6])
        nt = [sb(f"norm_tmp{i}", [P, NB]) for i in range(3)]
        g = dict(nc=nc, A=A, sb=sb, ps=ps, sem=sem, NB=NB, D=D, KD=KD, x_sb=x_sb, ctx_sb=ctx_sb, ident=ident,
                 gates=gates, x_mean=x_mean, x_rstd=x_rstd, c_mean=c_mean, c_rstd=c_rstd,
                 x_stats=x_stats, c_stats=c_stats, nt=nt)
        attention_0(**g)
        mixture_0(**g)
        attention_1(**g)
        recycle(nc)
        mixture_1(**g)
        out_done = sem("out_done")
        with nc.Block() as block:
            @block.sync
            def _(sp):
                sp.dma_start(out.rearrange("b p d -> p b d"), x_sb[:]).then_inc(out_done, 16)
                sp.wait_ge(out_done, 16)


def attention_0(nc, A, sb, ps, sem, NB, D, KD, x_sb, ctx_sb, ident, gates, x_mean, x_rstd, c_mean, c_rstd,
                x_stats, c_stats, nt):
    NH = 16
    HD = D // NH
    NG = 4
    with ExitStack() as c:
        W = {n: sb(f"a0_w{n}", [P, KD, D], F32, c) for n in "qkvo"}
        bq, bk = sb("a0_bq", [P, KD], F32, c), sb("a0_bk", [P, KD], F32, c)
        bv, bo = sb("a0_bv", [P, D], F32, c), sb("a0_bo", [P, D], F32, c)
        pidx = sb("a0_pidx", [P, 1], I32, c)
        mask = sb("a0_mask", [P, 2], F32, c)
        cst = sb("a0_cst", [P, D], F32, c)
        xn = sb("a0_xn", [P, D], F32, c)
        xcT = sb("a0_xcT", [P, 4, P], F32, c)
        q = [sb(f"a0_q{n}", [P, 2, P], F32R, c) for n in ("hi", "lo")]
        kT = sb("a0_kT", [P, 2, P], F32, c)
        km = [sb(f"a0_km{n}", [P, 2, 2, P], F32R, c) for n in ("hi", "lo")]
        v = sb("a0_v", [P, NB, D], F32, c)
        nmax = sb("a0_nmax", [P, NH], F32, c)
        probs = sb("a0_probs", [P, NH, P], F32, c)
        sums, rsum = sb("a0_sums", [P, NH], F32, c), sb("a0_rsum", [P, NH], F32, c)
        pT = sb("a0_pT", [P, NH, P], F32, c)
        vpad = sb("a0_vpad", [P, NH, P], F32, c)
        oT = sb("a0_oT", [P, 2, P], F32, c)
        psS = [ps(f"a0_psS{j}", [P, NG, P], F32, c) for j in range(NG)]
        psT = [ps(f"a0_psT{j}", [P, NG, P], F32, c) for j in range(2)]
        psM0 = ps("a0_psM0", [P, 512], F32, c)
        psM1 = ps("a0_psM1", [P, 512], F32, c)
        names = ("x_in0 x_in1 x_in2 x_in3 c_in0 c_in1 w_in small_in gates_done dve_steps ident_zero ident_done pidx_done "
                 "bo_done xn_done cst_done resid_done tx_done txc_done qk_done v_done q_hi q_lo km_hi km_lo kT_done vs_done "
                 "s_done max_done exp_done rsum_done p_done t_done tcA_done tcV_done vpad_zero vpad_done pv_done oTc_done y_done "
                 "x_done").split()
        s = {n: sem(f"a0_{n}", c) for n in names}
        XPARTS, CFIRST = 4, 4


        with nc.Block() as block:
            @block.sync
            def _(sp):
                part = NB // XPARTS
                for n in range(XPARTS):
                    sp.dma_start(x_sb[:, n * part:(n + 1) * part, :], A["x"][n * part:(n + 1) * part].rearrange("b p d -> p b d"))\
                      .then_inc(s[f"x_in{n}"], 16)
                for n, key in (("q", "Wq"), ("k", "Wk"), ("v", "Wv"), ("o", "Wo")):
                    sp.dma_start(W[n][:], A["L0_xattn_" + key].rearrange("(k p) n -> p k n", p=P)).then_inc(s["w_in"], 16)
                sp.dma_start(ctx_sb[:, 0:CFIRST, :], A["ctx_1024"][0:CFIRST].rearrange("b p d -> p b d")).then_inc(s["c_in0"], 16)
                sp.dma_start(ctx_sb[:, CFIRST:NB, :], A["ctx_1024"][CFIRST:NB].rearrange("b p d -> p b d")).then_inc(s["c_in1"], 16)

            @block.gpsimd
            def _(pool):
                pool.memset(ident[:], 0.0).then_inc(s["ident_zero"], 1)
                pool.iota(pidx[:], pattern=[[0, 1]], base=0, channel_multiplier=1).then_inc(s["pidx_done"], 1)
                pool.wait_ge(s["ident_zero"], 1)
                pool.affine_select(out=ident[:], in_=ident[:], compare_op=ALU.not_equal, fill=1.0, base=0,
                                   pattern=[[-1, P]], channel_multiplier=1).then_inc(s["ident_done"], 1)

                def stage_context(i, first):
                    if not first:
                        pool.wait_ge(s["tx_done"], i)
                    pool.tensor_copy(cst[:], ctx_sb[:, i, :]).then_inc(s["cst_done"], 1)

                def residual(i):
                    pool.wait_ge(s["xn_done"], i + 1)
                    pool.tensor_tensor(x_sb[:, i, :], x_sb[:, i, :], bo[:], ALU.add).then_inc(s["resid_done"], 1)

                def pad_values(i):
                    pool.wait_ge(s["vs_done"], i + 1)
                    at_least(pool, s["pv_done"], i)
                    for m in range(2):
                        own = vpad[:, 8 * m:8 * m + 8, :].rearrange("p h (g d) -> p (h g) d", d=HD)[:, 0::9, :]
                        ins = pool.tensor_copy(own, v[:, i, m * P:(m + 1) * P].rearrange("p (h d) -> p h d", d=HD))
                    ins.then_inc(s["vpad_done"], 1)

                pool.memset(vpad[:], 0.0).then_inc(s["vpad_zero"], 1)
                pool.wait_ge(s["c_in0"], 16)
                stage_context(0, True)
                pool.wait_ge(s["bo_done"], 1)
                pool.wait_ge(s["c_in1"], 16)
                pool.wait_ge(s["vpad_zero"], 1)
                stage_context(1, False)
                pad_values(0)
                residual(0)
                with pool.Fori(2, NB) as i:
                    stage_context(i, False)
                    pad_values(i - 1)
                    residual(i - 1)
                pad_values(NB - 1)
                residual(NB - 1)

            @block.scalar
            def _(act):
                for dst, src in ((bq[:], A["L0_xattn_bq"].rearrange("(k p) -> p k", p=P)),
                                 (bk[:], A["L0_xattn_bk"].rearrange("(k p) -> p k", p=P)),
                                 (bv[:], A["L0_xattn_bv"].partition_broadcast(P)),
                                 (bo[:], A["L0_xattn_bo"].partition_broadcast(P)),
                                 (gates[:, 0:2], A["g_xattn"].partition_broadcast(P)),
                                 (gates[:, 2:4], A["g_ffn"].partition_broadcast(P))):
                    with nc.allow_non_contiguous_dma(reason="a few hundred small parameters"):
                        act.dma_start(dst, src).then_inc(s["small_in"], 16)
                act.wait_ge(s["small_in"], 96)
                act.activation(gates[:], gates[:], ACT.Tanh).then_inc(s["gates_done"], 1)

                def front(i):
                    act.wait_ge(s["tx_done"], i + 1)
                    act.activation(xcT[:], psT[1][:], ACT.Copy).then_inc(s["txc_done"], 1)

                def copy(i, gr):
                    act.wait_ge(s["t_done"], i * 4 + gr + 1)
                    act.activation(pT[:, 4 * gr:4 * gr + 4, :], psT[0][:], ACT.Copy).then_inc(s["tcA_done"], 1)

                def project(i):
                    act.wait_ge(s["qk_done"], i + 1)
                    for m in range(2):
                        ins = act.activation(q[0][:, m, :], psM1[:, m * P:(m + 1) * P], ACT.Identity, bias=bq[:, m:m + 1])
                    ins.then_inc(s["q_hi"], 1)
                    at_least(act, s["km_lo"], i)
                    for m in range(2):
                        ins = act.activation(kT[:, m, :], psM1[:, (2 + m) * P:(3 + m) * P], ACT.Identity, bias=bk[:, m:m + 1])
                    ins.then_inc(s["kT_done"], 1)
                    act.wait_ge(s["kT_done"], i + 1)
                    for par in range(2):
                        ins = act.activation(km[0][:, :, par, :], kT[:], ACT.Copy, scale=mask[:, par:par + 1])
                    ins.then_inc(s["km_hi"], 1)

                def exps(i, j):
                    act.wait_ge(s["max_done"], i * 4 + j + 1)
                    for slot in range(NG):
                        n = 4 * j + slot
                        act.activation(probs[:, n, :], psS[j][:, slot, :], ACT.Exp, bias=nmax[:, n:n + 1],
                                       accum_out=sums[:, n:n + 1]).then_inc(s["exp_done"], 1)

                def heads_out(i):
                    act.wait_ge(s["pv_done"], i + 1)
                    act.activation(oT[:], psM0[:, D:2 * D].rearrange("p (a t) -> p a t", a=2), ACT.Copy).then_inc(s["oTc_done"], 1)

                def tile(i, first=False, last=False):
                    exps(i, 0)
                    if not last:
                        front(i + 1)
                    for j in range(1, 4):
                        exps(i, j)
                    if not first:
                        heads_out(i - 1)
                    copy(i, 0)
                    if not last:
                        project(i + 1)
                    copy(i, 2)

                front(0)
                project(0)
                tile(0, first=True)
                with act.Fori(1, NB - 1) as i:
                    tile(i)
                tile(NB - 1, last=True)
                heads_out(NB - 1)

            @block.vector
            def _(dve):
                k = Steps(dve, s["dve_steps"])
                dve.wait_ge(s["pidx_done"], 1)
                k.step(dve.tensor_scalar(pidx[:], pidx[:], 16, None, ALU.bitwise_and))
                k.step(dve.tensor_scalar(mask[:, 1:2], pidx[:], 1.0 / 64, None, ALU.mult))
                k.step(dve.tensor_scalar(mask[:, 0:1], mask[:, 1:2], -1.0, 0.25, ALU.mult, ALU.add))
                for n in range(XPARTS):
                    dve.wait_ge(s[f"x_in{n}"], 16)
                    for j in range(n * NB // XPARTS, (n + 1) * NB // XPARTS):
                        ins = dve.bn_stats(x_stats[:, j, :], x_sb[:, j, :])
                k.step(ins)
                norm_steps(dve, k, x_stats, x_mean[:], x_rstd[:], [t[:] for t in nt], False)
                dve.wait_ge(s["gates_done"], 1)
                dve.tensor_scalar(bo[:], bo[:], gates[:, 0:1], None, ALU.mult).then_inc(s["bo_done"], 1)

                def normed(i):
                    at_least(dve, s["tx_done"], i)
                    at = slice(i, i + 1) if isinstance(i, int) else bass.ds(i, 1)
                    dve.tensor_scalar(xn[:], x_sb[:, i, :], x_mean[:, at], x_rstd[:, at],
                                      ALU.subtract, ALU.mult).then_inc(s["xn_done"], 1)

                def copy(i, gr):
                    dve.wait_ge(s["t_done"], i * 4 + gr + 1)
                    dve.tensor_copy(pT[:, 4 * gr:4 * gr + 4, :], psT[1][:]).then_inc(s["tcV_done"], 1)

                def queries(i):
                    dve.wait_ge(s["kT_done"], i + 1)
                    for m in range(2):
                        ins = dve.scalar_tensor_tensor(out=q[1][:, m, :], in0=psM1[:, m * P:(m + 1) * P], scalar=bq[:, m:m + 1],
                                                       in1=q[0][:, m, :].bitcast(F32), op0=ALU.add, op1=ALU.subtract)
                    ins.then_inc(s["q_lo"], 1)

                def keys(i):
                    dve.wait_ge(s["km_hi"], i + 1)
                    for par in range(2):
                        ins = dve.scalar_tensor_tensor(out=km[1][:, :, par, :], in0=kT[:], scalar=mask[:, par:par + 1],
                                                       in1=km[0][:, :, par, :].bitcast(F32), op0=ALU.mult, op1=ALU.subtract)
                    ins.then_inc(s["km_lo"], 1)

                def values(i):
                    dve.wait_ge(s["v_done"], i + 1)
                    dve.tensor_tensor(v[:, i, :], psM0[:, 0:D], bv[:], ALU.add).then_inc(s["vs_done"], 1)

                def normalize(i, j):
                    dve.wait_ge(s["exp_done"], i * 16 + 4 * j + 4)
                    own = slice(4 * j, 4 * j + 4)
                    dve.reciprocal(rsum[:, own], sums[:, own]).then_inc(s["rsum_done"], 1)
                    dve.wait_ge(s["rsum_done"], i * 4 + j + 1)
                    dve.tensor_tensor(probs[:, own, :], probs[:, own, :], rsum[:, own].unsqueeze(2).to_broadcast([P, NG, P]),
                                      ALU.mult).then_inc(s["p_done"], 1)

                def maximum(i, j):
                    dve.wait_ge(s["s_done"], i * 4 + j + 1)
                    dve.tensor_reduce(nmax[:, 4 * j:4 * j + 4], psS[j][:], AX.X, ALU.max, negate=True)\
                       .then_inc(s["max_done"], 1)

                def residual(i):
                    dve.wait_ge(s["y_done"], i + 1)
                    dve.wait_ge(s["resid_done"], i + 1)
                    dve.scalar_tensor_tensor(out=x_sb[:, i, :], in0=psM0[:, D:2 * D], scalar=gates[:, 0:1],
                                             in1=x_sb[:, i, :], op0=ALU.mult, op1=ALU.add).then_inc(s["x_done"], 1)

                def statistics(i):
                    dve.wait_ge(s["x_done"], i + 1)
                    dve.bn_stats(x_stats[:, i, :], x_sb[:, i, :])

                def tile(i, first=False, ahead=2):
                    for j in range(4):
                        maximum(i, j)
                    normalize(i, 0)
                    if ahead > 1:
                        normed(i + 2)
                    for j in range(1, 4):
                        normalize(i, j)
                    copy(i, 1)
                    if ahead > 0:
                        queries(i + 1)
                        values(i + 1)
                        keys(i + 1)
                    copy(i, 3)
                    dve.bn_stats(c_stats[:, i, :], ctx_sb[:, i, :])
                    if not first:
                        residual(i - 1)
                        statistics(i - 1)

                normed(0)
                normed(1)
                queries(0)
                values(0)
                keys(0)
                tile(0, first=True)
                with dve.Fori(1, NB - 2) as i:
                    tile(i)
                tile(NB - 2, ahead=1)
                tile(NB - 1, ahead=0)
                residual(NB - 1)
                statistics(NB - 1)

            @block.tensor
            def _(pe):
                def turn_in(i):
                    pe.wait_ge(s["xn_done"], i + 1)
                    pe.wait_ge(s["cst_done"], i + 1)
                    at_least(pe, s["tcV_done"], (i - 1) * 2)
                    for a in range(KD):
                        pe.transpose(psT[1][:, a, :], xn[:, a * P:(a + 1) * P], ident[:])
                    for a in range(KD):
                        ins = pe.transpose(psT[1][:, 2 + a, :], cst[:, a * P:(a + 1) * P], ident[:])
                    ins.then_inc(s["tx_done"], 1)

                def turn_probs(i, gr):
                    pe.wait_ge(s["p_done"], i * 4 + gr + 1)
                    if gr == 2:
                        pe.wait_ge(s["tcA_done"], i * 2 + 1)
                    if gr == 3:
                        pe.wait_ge(s["tcV_done"], i * 2 + 1)
                    for h in range(4):
                        ins = pe.transpose(psT[gr % 2][:, h, :], probs[:, 4 * gr + h, :], ident[:])
                    ins.then_inc(s["t_done"], 1)

                def value(i):
                    at_least(pe, s["vs_done"], i)
                    at_least(pe, s["oTc_done"], i - 1)
                    for a in range(KD):
                        ins = pe.matmul(psM0[:, 0:D], xcT[:, 2 + a, :], W["v"][:, a, :], start=(a == 0), stop=(a == KD - 1))
                    ins.then_inc(s["v_done"], 1)

                def project(i):
                    pe.wait_ge(s["txc_done"], i + 1)
                    for b, (w, src) in enumerate((("q", 0), ("q", 0), ("k", 2), ("k", 2))):
                        for a in range(KD):
                            m = b % 2
                            ins = pe.matmul(psM1[:, b * P:(b + 1) * P], W[w][:, a, m * P:(m + 1) * P], xcT[:, src + a, :],
                                            start=(a == 0), stop=(a == KD - 1))
                    ins.then_inc(s["qk_done"], 1)

                def weigh(i):
                    at_least(pe, s["x_done"], i)
                    pe.wait_ge(s["vpad_done"], i + 1)
                    pe.wait_ge(s["tcA_done"], i * 2 + 2)
                    pe.wait_ge(s["tcV_done"], i * 2 + 2)
                    for m in range(2):
                        for n in range(8):
                            j, parity = divmod(n, 2)
                            ins = pe.matmul(psM0[:, D + m * P:D + (m + 1) * P], vpad[:, 8 * m + n, :], pT[:, 4 * j + 2 * m + parity, :],
                                            start=(n == 0), stop=(n == 7))
                    ins.then_inc(s["pv_done"], 1)

                def scores(i):
                    pe.wait_ge(s["q_lo"], i + 1)
                    pe.wait_ge(s["km_lo"], i + 1)
                    for m in range(2):
                        for j in range(4):
                            r = slice(32 * j, 32 * j + 32)
                            for n, (x, y) in enumerate(PARTS3):
                                ins = pe.matmul(psS[j][:, 2 * m:2 * m + 2, :].rearrange("p a t -> p (a t)"), q[x][r, m, :],
                                                km[y][r, m, :, :].rearrange("p a t -> p (a t)"), start=(n == 0), stop=(n == 2))
                            if m == 1:
                                ins.then_inc(s["s_done"], 1)

                def output(i, last=False):
                    pe.wait_ge(s["oTc_done"], i + 1)
                    if not last:
                        pe.wait_ge(s["vs_done"], i + 3)
                    for a in range(KD):
                        ins = pe.matmul(psM0[:, D:2 * D], oT[:, a, :], W["o"][:, a, :], start=(a == 0), stop=(a == KD - 1))
                    ins.then_inc(s["y_done"], 1)

                def tile(i, first=False, last=False):
                    scores(i)
                    if not last:
                        turn_in(i + 1)
                    if not first:
                        weigh(i - 1)
                    turn_probs(i, 0)
                    turn_probs(i, 1)
                    if not last:
                        project(i + 1)
                        value(i + 1)
                    turn_probs(i, 2)
                    turn_probs(i, 3)
                    if not first:
                        output(i - 1, last)

                pe.wait_ge(s["ident_done"], 1)
                pe.wait_ge(s["w_in"], 64)
                turn_in(0)
                project(0)
                value(0)
                tile(0, first=True)
                with pe.Fori(1, NB - 1) as i:
                    tile(i)
                tile(NB - 1, last=True)
                weigh(NB - 1)
                output(NB - 1, True)


def prefix_steps(dve, s, src, bufs, n):
    a, b = src, bufs[0]
    shift, turn = 1, 0
    while shift < n:
        dve.tensor_copy(b[:, 0:shift], a[:, 0:shift])
        s.step(dve.tensor_tensor(b[:, shift:n], a[:, shift:n], a[:, 0:n - shift], ALU.add))
        turn += 1
        a, b = b, bufs[turn % 2]
        shift *= 2
    return a


def mixture_0(nc, A, sb, ps, sem, NB, D, KD, x_sb, ctx_sb, ident, gates, x_mean, x_rstd, c_mean, c_rstd,
              x_stats, c_stats, nt):
    NE = A["L0_ffn_expert_w1"].shape[0]
    F = A["L0_ffn_expert_w1"].shape[1]
    KF = F // P
    NT = NB + NE
    SH = NE
    xg = nc.dram_tensor("m0_sorted", (NT * P, D), F32, kind="Internal").ap()
    yg = nc.dram_tensor("m0_expert_out", (NT * P, D), F32, kind="Internal").ap()
    with ExitStack() as c:
        w1t = sb("m0_w1t", [P, NE + 1, KD, F], F32R, c)
        w2t = sb("m0_w2t", [P, NE + 1, KF, D], F32R, c)
        s1 = sb("m0_s1", [P, NE + 1, KF], F32, c)
        s2 = sb("m0_s2", [P, NE + 1, D], F32, c)
        logits = sb("m0_logits", [P, NB, NE], F32, c)
        prob = sb("m0_prob", [P, NB], F32, c)
        pos = sb("m0_pos", [P, NB], U32, c)
        owner = sb("m0_owner", [P, NT], I32, c)
        gamma, beta = sb("m0_gamma", [P, KD], F32, c), sb("m0_beta", [P, KD], F32, c)
        router = sb("m0_router", [P, KD, NE], F32, c)
        zeros = sb("m0_zeros", [P, D], F32, c)
        ones = sb("m0_ones", [P, P], F32, c)
        upper = sb("m0_upper", [P, P], F32, c)
        scattered = sem("m0_scattered", c)
        ternary_weights(nc, A, sb, ps, sem, NE, F, KF, KD, D, w1t, w2t, s1, s2, ident, ones, zeros, xg,
                        gamma, beta, router, upper)
        n_sb = sb("m0_n", [P, NB, D], F32, c)
        sh = sb("m0_shared", [P, NB, D], F32, c)
        with ExitStack() as turned:
            hT = [sb(f"m0_hT{n}", [P, KD, NB, P], F32R, turned) for n in ("hi", "lo")]
            token_norms(nc, sb, ps, sem, NB, D, KD, x_sb, ident, x_mean, x_rstd, x_stats, nt, n_sb, hT,
                        logits, router, gamma, beta, NE, "m0", True)
            route_top1(nc, sb, ps, sem, NB, NE, NT, D, logits, prob, pos, owner, ones, upper, gates)
            shared_ternary(nc, sb, ps, sem, NB, D, KD, KF, SH, hT, w1t, w2t, s1, sh, n_sb, pos, xg, scattered)
        expert_tiles(nc, sb, ps, sem, NB, NT, D, KD, KF, SH, x_sb, sh, s2, s1, w1t, w2t, gamma, beta, ident, owner,
                     xg, yg, n_sb, pos, prob, gates, scattered, x_stats)


def ternary_weights(nc, A, sb, ps, sem, NE, F, KF, KD, D, w1t, w2t, s1, s2, ident, ones, zeros, xg,
                    gamma, beta, router, upper):
    with ExitStack() as c:
        raw1 = [sb(f"t_raw1_{i}", [P, KF, D], F32, c) for i in range(2)]
        raw2 = [sb(f"t_raw2_{i}", [P, KD, F], F32, c) for i in range(2)]
        identb = sb("t_identb", [P, P], BF16, c)
        sums = [sb(f"t_sums{i}", [P, KF + KD], F32, c) for i in range(2)]
        mag = sb("t_mag", [P, KF + KD], F32, c)
        thr, nthr = sb("t_thr", [P, KF + KD], F32, c), sb("t_nthr", [P, KF + KD], F32, c)
        neg = sb("t_neg", [P, KF * D + KD * F], BF16, c)
        unused = sb("t_unused", [P, KF * D + KD * F], BF16, c)
        tern = sb("t_tern", [P, KF * D + KD * F], BF16, c)
        diag = sb("t_diag", [P, KD, P], F32, c)
        psA = [ps(f"t_ps{i}", [P, 8, P], BF16, c) for i in range(2)]
        psB = ps("t_psB", [P, D], F32, c)
        names = ("const_done upper_zero raw0 raw1 small_in zero_out steps sum_done mag_done diag_done tern_done turned1 turned2 spread "
                 "w1_done w2_done").split()
        s = {n: sem(f"t_{n}", c) for n in names}
        raw_in = [s["raw0"], s["raw1"]]

        def source(e):
            if isinstance(e, int) and e == NE:
                return A["L0_ffn_shared_w1"], A["L0_ffn_shared_w2"]
            return A["L0_ffn_expert_w1"][e], A["L0_ffn_expert_w2"][e]

        def loads_of(n, buf):
            return (n - buf) * 16 + 32

        with nc.Block() as block:
            @block.sync
            def _(sp):
                with nc.allow_non_contiguous_dma(reason="a few hundred small parameters"):
                    sp.dma_start(gamma[:], A["L0_ffn_ln_gamma"].rearrange("(k p) -> p k", p=P)).then_inc(s["small_in"], 16)
                    sp.dma_start(beta[:], A["L0_ffn_ln_beta"].rearrange("(k p) -> p k", p=P)).then_inc(s["small_in"], 16)
                    sp.dma_start(router[:], A["router_T"].rearrange("(k p) e -> p k e", p=P)).then_inc(s["small_in"], 16)

                def load(e, buf):
                    a, b = source(e)
                    sp.dma_start(raw1[buf][:], a.rearrange("(t p) d -> p t d", p=P)).then_inc(raw_in[buf], 16)
                    sp.dma_start(raw2[buf][:], b.rearrange("(t p) f -> p t f", p=P)).then_inc(raw_in[buf], 16)

                load(NE, 0)
                load(0, 1)
                sp.wait_ge(s["const_done"], 2)
                sp.dma_start(xg.rearrange("(t p) d -> p t d", p=P), zeros[:].unsqueeze(1).to_broadcast([P, xg.shape[0] // P, D]))\
                  .then_inc(s["zero_out"], 16)
                with sp.Fori(0, NE // 2 - 1) as i:
                    for half in range(2):
                        sp.wait_ge(s["tern_done"], i * 2 + half + 1)
                        load(i * 2 + half + 1, half)
                sp.wait_ge(s["tern_done"], NE - 1)
                load(NE - 1, 0)
                sp.wait_ge(s["zero_out"], 16)
                sp.wait_ge(s["small_in"], 48)

            @block.gpsimd
            def _(pool):
                pool.memset(zeros[:], 0.0).then_inc(s["const_done"], 1)
                pool.memset(ones[:], 1.0).then_inc(s["const_done"], 1)
                pool.wait_ge(s["const_done"], 2)
                pool.affine_select(out=upper[:], in_=ones[:], compare_op=ALU.is_gt, fill=0.0, base=0,
                                   pattern=[[1, P]], channel_multiplier=-1).then_inc(s["const_done"], 1)

                def spread(n, e):
                    pool.wait_ge(s["mag_done"], n + 1)
                    at_least(pool, s["spread"], n)
                    for t in range(KD):
                        pool.tensor_tensor(diag[:, t, :], ident[:], mag[:, KF + t:KF + t + 1].to_broadcast([P, P]), ALU.mult)
                    pool.tensor_copy(s1[:, e, :], mag[:, 0:KF]).then_inc(s["diag_done"], 1)

                spread(0, NE)
                with pool.Fori(1, NE + 1) as n:
                    spread(n, n - 1)

            @block.vector
            def _(dve):
                dve.tensor_copy(identb[:], ident[:]).then_inc(s["steps"], 1)
                per = 3

                def signs(n, e, buf, first=False):
                    k = Steps(dve, s["steps"], 1 + n * per)
                    dve.wait_ge(s["sum_done"], n + 1)
                    if not first:
                        dve.wait_ge(s["diag_done"], n)
                    dve.tensor_scalar(mag[:, 0:KF], sums[buf][:, 0:KF], 1.0 / D, 1e-5, ALU.mult, ALU.max)
                    dve.tensor_scalar(mag[:, KF:], sums[buf][:, KF:], 1.0 / F, 1e-5, ALU.mult, ALU.max).then_inc(s["mag_done"], 1)
                    dve.wait_ge(s["mag_done"], n + 1)
                    dve.tensor_scalar(thr[:], mag[:], 0.5, None, ALU.mult)
                    k.step(dve.tensor_scalar(nthr[:], mag[:], -0.5, None, ALU.mult))
                    rows = [(raw1[buf][:, t, :], t * D, D) for t in range(KF)] + \
                           [(raw2[buf][:, t, :], KF * D + t * F, F) for t in range(KD)]
                    for t, (w, at, width) in enumerate(rows):
                        ins = dve.tensor_scalar(neg[:, at:at + width], w, nthr[:, t:t + 1], None, ALU.is_lt)
                    k.step(ins)
                    if not first:
                        dve.wait_ge(s["turned2"], n)
                    for t, (w, at, width) in enumerate(rows):
                        ins = dve.scalar_tensor_tensor(out=tern[:, at:at + width], in0=w, scalar=thr[:, t:t + 1],
                                                       in1=neg[:, at:at + width], op0=ALU.is_gt, op1=ALU.subtract)
                    ins.then_inc(s["tern_done"], 1)
                    dve.wait_ge(s["spread"], n + 1)
                    k.step(dve.tensor_copy(s2[:, e, :], psB[:]))
                    assert k.n == per

                signs(0, NE, 0, True)
                with dve.Fori(0, NE // 2) as i:
                    signs(i * 2 + 1, i * 2, 1)
                    signs(i * 2 + 2, i * 2 + 1, 0)

            @block.tensor
            def _(pe):
                pe.wait_ge(s["const_done"], 3)

                def turn(n, first=False):
                    pe.wait_ge(s["tern_done"], n + 1)
                    if not first:
                        pe.wait_ge(s["w1_done"], n)
                    for a in range(KD):
                        for t in range(KF):
                            ins = pe.transpose(psA[0][:, a * KF + t, :], tern[:, t * D + a * P:t * D + (a + 1) * P], identb[:])
                    ins.then_inc(s["turned1"], 1)
                    if not first:
                        pe.wait_ge(s["w2_done"], n)
                    for a in range(KF):
                        for t in range(KD):
                            at = KF * D + t * F + a * P
                            ins = pe.transpose(psA[1][:, a * KD + t, :], tern[:, at:at + P], identb[:])
                    ins.then_inc(s["turned2"], 1)

                def spread(n, first=False):
                    pe.wait_ge(s["diag_done"], n + 1)
                    if not first:
                        pe.wait_ge(s["steps"], 1 + n * 3)
                    for t in range(KD):
                        ins = pe.matmul(psB[:, t * P:(t + 1) * P], ones[:], diag[:, t, :], start=True, stop=True)
                    ins.then_inc(s["spread"], 1)

                spread(0, True)
                turn(0, True)
                with pe.Fori(1, NE + 1) as n:
                    spread(n)
                    turn(n)

            @block.scalar
            def _(act):
                def keep(n, e):
                    act.wait_ge(s["turned1"], n + 1)
                    act.activation(w1t[:, e, :, :].rearrange("p k f -> p (k f)"), psA[0][:].rearrange("p a t -> p (a t)"),
                                   ACT.Copy).then_inc(s["w1_done"], 1)
                    act.wait_ge(s["turned2"], n + 1)
                    act.activation(w2t[:, e, :, :].rearrange("p k f -> p (k f)"), psA[1][:].rearrange("p a t -> p (a t)"),
                                   ACT.Copy).then_inc(s["w2_done"], 1)

                def magnitudes(n, buf):
                    act.wait_ge(raw_in[buf], loads_of(n, buf))
                    at_least(act, s["mag_done"], n - 1)
                    at_least(act, s["sum_done"], n)
                    for t in range(KF):
                        act.activation(unused[:, t * D:(t + 1) * D], raw1[buf][:, t, :], ACT.Abs, accum_out=sums[buf][:, t:t + 1])
                    for t in range(KD):
                        ins = act.activation(unused[:, KF * D + t * F:KF * D + (t + 1) * F], raw2[buf][:, t, :], ACT.Abs, accum_out=sums[buf][:, KF + t:KF + t + 1])
                    ins.then_inc(s["sum_done"], 1)

                magnitudes(0, 0)
                magnitudes(1, 1)
                keep(0, NE)
                with act.Fori(1, NE // 2) as i:
                    magnitudes(i * 2, 0)
                    keep(i * 2 - 1, i * 2 - 2)
                    magnitudes(i * 2 + 1, 1)
                    keep(i * 2, i * 2 - 1)
                magnitudes(NE, 0)
                keep(NE - 1, NE - 2)
                keep(NE, NE - 1)


def token_norms(nc, sb, ps, sem, NB, D, KD, x_sb, ident, x_mean, x_rstd, x_stats, nt, n_sb, hT,
                logits, router, gamma, beta, NE, tag, twice):
    with ExitStack() as c:
        n_t = [sb(f"{tag}_nt{i}", [P, D], F32, c) for i in range(2)]
        h = [sb(f"{tag}_h{i}", [P, KD, P], F32, c) for i in range(2)]
        psT = [ps(f"{tag}_psN{i}", [P, KD, P], F32, c) for i in range(2)]
        psL = [ps(f"{tag}_psL{i}", [P, NE], F32, c) for i in range(2)]
        s = {n: sem(f"{tag}_n_{n}", c) for n in ("steps normed kept turned scaled split scored logits_out".split())}
        with nc.Block() as block:
            @block.vector
            def _(dve):
                k = Steps(dve, s["steps"])
                norm_steps(dve, k, x_stats, x_mean[:], x_rstd[:], [t[:] for t in nt], twice)
                base = k.n

                def norm(i, b, first=False):
                    if not first:
                        dve.wait_ge(s["turned"], i - 1)
                        dve.wait_ge(s["kept"], i - 1)
                    dve.tensor_scalar(n_t[b][:], x_sb[:, i, :], x_mean[:, bass.ds(i, 1)], x_rstd[:, bass.ds(i, 1)],
                                      ALU.subtract, ALU.mult).then_inc(s["normed"], 1)

                def split(i, b):
                    dve.wait_ge(s["scaled"], i + 1)
                    k = Steps(dve, s["steps"], base + i)
                    k.step(dve.tensor_copy(hT[0][:, :, i, :], h[b][:]))
                    dve.tensor_tensor(hT[1][:, :, i, :], h[b][:], hT[0][:, :, i, :].bitcast(F32), ALU.subtract)\
                       .then_inc(s["split"], 1)

                def keep_logits(i, b):
                    dve.wait_ge(s["scored"], i + 1)
                    dve.tensor_copy(logits[:, i, :], psL[b][:]).then_inc(s["logits_out"], 1)

                norm(0, 0, True)
                norm(1, 1, True)
                for b in range(2):
                    split(b, b)
                    norm(b + 2, b)
                    if b == 1:
                        keep_logits(0, 0)
                with dve.Fori(1, NB // 2 - 1) as i:
                    for b in range(2):
                        split(i * 2 + b, b)
                        norm(i * 2 + b + 2, b)
                        keep_logits(i * 2 + b - 1, 1 - b)
                for b in range(2):
                    split(NB - 2 + b, b)
                    keep_logits(NB - 3 + b, 1 - b)
                keep_logits(NB - 1, 1)

            @block.gpsimd
            def _(pool):
                with pool.Fori(0, NB // 2) as i:
                    for b in range(2):
                        pool.wait_ge(s["normed"], i * 2 + b + 1)
                        pool.tensor_copy(n_sb[:, i * 2 + b, :], n_t[b][:]).then_inc(s["kept"], 1)

            @block.tensor
            def _(pe):
                def turn(i, b, first=False):
                    pe.wait_ge(s["normed"], i + 1)
                    if not first:
                        pe.wait_ge(s["scaled"], i - 1)
                    for a in range(KD):
                        ins = pe.transpose(psT[b][:, a, :], n_t[b][:, a * P:(a + 1) * P], ident[:])
                    ins.then_inc(s["turned"], 1)

                def score(i, b, first=False):
                    pe.wait_ge(s["scaled"], i + 1)
                    if not first:
                        pe.wait_ge(s["logits_out"], i - 1)
                    for a in range(KD):
                        ins = pe.matmul(psL[b][:], h[b][:, a, :], router[:, a, :], start=(a == 0), stop=(a == KD - 1))
                    ins.then_inc(s["scored"], 1)

                turn(0, 0, True)
                turn(1, 1, True)
                score(0, 0, True)
                turn(2, 0)
                score(1, 1, True)
                turn(3, 1)
                with pe.Fori(1, NB // 2 - 1) as i:
                    for b in range(2):
                        score(i * 2 + b, b)
                        turn(i * 2 + b + 2, b)
                for b in range(2):
                    score(NB - 2 + b, b)

            @block.scalar
            def _(act):
                def scale(i, b, first=False):
                    act.wait_ge(s["turned"], i + 1)
                    if not first:
                        act.wait_ge(s["scored"], i - 1)
                        act.wait_ge(s["split"], i - 1)
                    if gamma is None:
                        act.activation(h[b][:], psT[b][:], ACT.Copy).then_inc(s["scaled"], 1)
                        return
                    for a in range(KD):
                        ins = act.activation(h[b][:, a, :], psT[b][:, a, :], ACT.Identity, bias=beta[:, a:a + 1],
                                             scale=gamma[:, a:a + 1])
                    ins.then_inc(s["scaled"], 1)

                scale(0, 0, True)
                scale(1, 1, True)
                with act.Fori(1, NB // 2) as i:
                    for b in range(2):
                        scale(i * 2 + b, b)


def route_top1(nc, sb, ps, sem, NB, NE, NT, D, logits, prob, pos, owner, ones, upper, gates):
    with ExitStack() as c:
        best = sb("r0_best", [P, NB, 8], F32, c)
        index = sb("r0_index", [P, NB, 8], U32, c)
        shifted = sb("r0_shifted", [P, NB, NE], F32, c)
        expd = sb("r0_exp", [P, NB, NE], F32, c)
        which = sb("r0_which", [P, NB], F32, c)
        iota_i = sb("r0_iota_i", [P, NT], I32, c)
        iota = sb("r0_iota", [P, NT], F32, c)
        hot = sb("r0_hot", [P, NB, NE], F32, c)
        rank = sb("r0_rank", [P, NB, NE], F32, c)
        tot = sb("r0_tot", [P, NB, NE], F32, c)
        pre = [sb(f"r0_pre{i}", [P, NB, NE], F32, c) for i in range(2)]
        cnt_i = sb("r0_cnt_i", [P, NE], I32, c)
        tiles = sb("r0_tiles", [P, NE], F32, c)
        ends = [sb(f"r0_ends{i}", [P, NE], F32, c) for i in range(2)]
        base = sb("r0_base", [P, NE], F32, c)
        after = sb("r0_after", [P, NT, NE], F32, c)
        nown = sb("r0_nown", [P, NT], F32, c)
        posf = sb("r0_posf", [P, NB], F32, c)
        psR = ps("r0_ps", [P, 2, NB * NE], F32, c)
        s = {n: sem(f"r0_{n}", c) for n in "steps iota_done shifted_done exp_done hot_done ranked".split()}

        with nc.Block() as block:
            @block.gpsimd
            def _(pool):
                pool.iota(iota_i[:], pattern=[[1, NT]], base=0, channel_multiplier=0).then_inc(s["iota_done"], 1)

            @block.scalar
            def _(act):
                act.wait_ge(s["shifted_done"], 1)
                act.activation(expd[:], shifted[:], ACT.Exp).then_inc(s["exp_done"], 1)

            @block.tensor
            def _(pe):
                pe.wait_ge(s["hot_done"], 1)
                flat = hot[:].rearrange("p b e -> p (b e)")
                pe.matmul(psR[:, 0, :], upper[:], flat, start=True, stop=True)
                pe.matmul(psR[:, 1, :], ones[:], flat, start=True, stop=True).then_inc(s["ranked"], 1)

            @block.vector
            def _(dve):
                k = Steps(dve, s["steps"])
                for i in range(NB):
                    ins = dve.max(best[:, i, :], logits[:, i, :])
                k.step(ins)
                for i in range(NB):
                    dve.max_index(index[:, i, :], best[:, i, :], logits[:, i, :])
                dve.tensor_tensor(shifted[:], logits[:], best[:, :, 0:1].to_broadcast([P, NB, NE]), ALU.subtract)\
                   .then_inc(s["shifted_done"], 1)
                dve.wait_ge(s["iota_done"], 1)
                k.step(dve.tensor_copy(iota[:], iota_i[:]))
                k.step(dve.tensor_copy(which[:], index[:, :, 0]))
                dve.tensor_tensor(hot[:], which[:].unsqueeze(2).to_broadcast([P, NB, NE]),
                                  iota[:, 0:NE].unsqueeze(1).to_broadcast([P, NB, NE]), ALU.is_equal).then_inc(s["hot_done"], 1)
                dve.wait_ge(s["exp_done"], 1)
                k.step(dve.tensor_reduce(prob[:], expd[:], AX.X, ALU.add))
                k.step(dve.reciprocal(prob[:], prob[:]))
                k.step(dve.tensor_scalar(prob[:], prob[:], gates[:, 2:3], None, ALU.mult))
                dve.wait_ge(s["ranked"], 1)
                three = lambda t: t.rearrange("p (b e) -> p b e", e=NE)
                k.step(dve.tensor_copy(tot[:], three(psR[:, 1, :])))
                incl = prefix_steps(dve, k, tot, pre, NB)
                k.step(dve.tensor_tensor(rank[:], three(psR[:, 0, :]), incl[:], ALU.add))
                k.step(dve.tensor_tensor(rank[:], rank[:], tot[:], ALU.subtract))
                k.step(dve.tensor_scalar(cnt_i[:], incl[:, NB - 1, :], float(P - 1), None, ALU.add))
                k.step(dve.tensor_scalar(cnt_i[:], cnt_i[:], 7, None, ALU.logical_shift_right))
                k.step(dve.tensor_copy(tiles[:], cnt_i[:]))
                end = prefix_steps(dve, k, tiles, ends, NE)
                k.step(dve.tensor_tensor(base[:], end[:], tiles[:], ALU.subtract))
                k.step(dve.tensor_scalar(base[:], base[:], float(P), None, ALU.mult))
                k.step(dve.tensor_tensor(rank[:], rank[:], base[:].unsqueeze(1).to_broadcast([P, NB, NE]), ALU.add))
                k.step(dve.tensor_tensor(rank[:], rank[:], hot[:], ALU.mult))
                k.step(dve.tensor_reduce(posf[:], rank[:], AX.X, ALU.add))
                k.step(dve.tensor_copy(pos[:], posf[:]))
                k.step(dve.tensor_tensor(after[:], iota[:].unsqueeze(2).to_broadcast([P, NT, NE]),
                                         end[:].unsqueeze(1).to_broadcast([P, NT, NE]), ALU.is_ge))
                k.step(dve.tensor_reduce(nown[:], after[:], AX.X, ALU.add))
                k.step(dve.tensor_scalar(owner[:], nown[:], float(NE - 1), None, ALU.min))


def shared_ternary(nc, sb, ps, sem, NB, D, KD, KF, SH, hT, w1t, w2t, s1, sh, n_sb, pos, xg, scattered):
    with ExitStack() as c:
        g = [sb(f"s0_g{i}", [P, KF, P], F32, c) for i in range(2)]
        gs = [[sb(f"s0_g{n}{i}", [P, KF, P], F32R, c) for n in ("hi", "lo")] for i in range(2)]
        psH = [ps(f"s0_psH{i}", [P, KF, P], F32, c) for i in range(2)]
        psY = [ps(f"s0_psY{i}", [P, D], F32, c) for i in range(2)]
        s = {n: sem(f"s0_{n}", c) for n in "up silu steps split down kept".split()}
        with nc.Block() as block:
            @block.gpsimd
            def _(pool):
                for i in range(NB):
                    pool.indirect_dma_start(xg, bass.IndirectOffsetOnAxis(ap=pos[:, i:i + 1], axis=0), n_sb[:, i, :], None)\
                        .then_inc(scattered, 16)

            @block.tensor
            def _(pe):
                def up(i, b, first=False):
                    if not first:
                        pe.wait_ge(s["silu"], i - 1)
                    for t in range(KF):
                        for n, (a, part) in enumerate([(a, part) for a in range(KD) for part in range(2)]):
                            ins = pe.matmul(psH[b][:, t, :], w1t[:, SH, a, t * P:(t + 1) * P], hT[part][:, a, i, :],
                                            start=(n == 0), stop=(n == 2 * KD - 1))
                    ins.then_inc(s["up"], 1)

                def down(i, b, first=False):
                    pe.wait_ge(s["split"], i + 1)
                    if not first:
                        pe.wait_ge(s["kept"], i - 1)
                    for n, (t, part) in enumerate([(t, part) for t in range(KF) for part in range(2)]):
                        ins = pe.matmul(psY[b][:], gs[b][part][:, t, :], w2t[:, SH, t, :], start=(n == 0), stop=(n == 2 * KF - 1))
                    ins.then_inc(s["down"], 1)

                up(0, 0, True)
                up(1, 1, True)
                down(0, 0, True)
                up(2, 0)
                down(1, 1, True)
                up(3, 1)
                with pe.Fori(1, NB // 2 - 1) as i:
                    for b in range(2):
                        down(i * 2 + b, b)
                        up(i * 2 + b + 2, b)
                for b in range(2):
                    down(NB - 2 + b, b)

            @block.scalar
            def _(act):
                def silu(i, b, first=False):
                    act.wait_ge(s["up"], i + 1)
                    if not first:
                        act.wait_ge(s["split"], i - 1)
                    for t in range(KF):
                        ins = act.activation(g[b][:, t, :], psH[b][:, t, :], ACT.Silu, scale=s1[:, SH, t:t + 1])
                    ins.then_inc(s["silu"], 1)

                def keep(i, b):
                    act.wait_ge(s["down"], i + 1)
                    act.activation(sh[:, i, :], psY[b][:], ACT.Copy).then_inc(s["kept"], 1)

                silu(0, 0, True)
                silu(1, 1, True)
                with act.Fori(0, NB // 2 - 1) as i:
                    for b in range(2):
                        keep(i * 2 + b, b)
                        silu(i * 2 + b + 2, b)
                for b in range(2):
                    keep(NB - 2 + b, b)

            @block.vector
            def _(dve):
                def split(i, b, first=False):
                    dve.wait_ge(s["silu"], i + 1)
                    if not first:
                        dve.wait_ge(s["down"], i - 1)
                    k = Steps(dve, s["steps"], i)
                    k.step(dve.tensor_copy(gs[b][0][:], g[b][:]))
                    dve.tensor_tensor(gs[b][1][:], g[b][:], gs[b][0][:].bitcast(F32), ALU.subtract).then_inc(s["split"], 1)

                split(0, 0, True)
                split(1, 1, True)
                with dve.Fori(1, NB // 2) as i:
                    for b in range(2):
                        split(i * 2 + b, b)


def expert_tiles(nc, sb, ps, sem, NB, NT, D, KD, KF, SH, x_sb, sh, s2, s1, w1t, w2t, gamma, beta, ident, owner,
                 xg, yg, n_sb, pos, prob, gates, scattered, x_stats):
    F = KF * P
    with ExitStack() as c:
        xin = [sb(f"e0_xin{i}", [P, D], F32, c) for i in range(2)]
        h = [sb(f"e0_h{i}", [P, KD, P], F32, c) for i in range(2)]
        hs = [[sb(f"e0_h{n}{i}", [P, KD, P], F32R, c) for n in ("hi", "lo")] for i in range(2)]
        u = [sb(f"e0_u{i}", [P, F], F32, c) for i in range(2)]
        g = [sb(f"e0_g{i}", [P, KF, P], F32, c) for i in range(2)]
        gs = [[sb(f"e0_g{n}{i}", [P, KF, P], F32R, c) for n in ("hi", "lo")] for i in range(2)]
        y = [sb(f"e0_y{i}", [P, D], F32, c) for i in range(2)]
        s2g = sb("e0_s2g", [P, D], F32, c)
        psA = [ps(f"e0_psA{i}", [P, KD, P], F32, c) for i in range(2)]
        psH = [ps(f"e0_psH{i}", [P, F], F32, c) for i in range(2)]
        psT = [ps(f"e0_psT{i}", [P, KF, P], F32, c) for i in range(2)]
        psY = [ps(f"e0_psY{i}", [P, D], F32, c) for i in range(2)]
        names = "in0 in1 turned scaled steps steps2 split up up_out turned2 silu split2 down y_done out0 out1 shared_in s2g combined".split()
        gathered = [sem(f"e0_gathered{i}", c) for i in range(NB)]
        s = {n: sem(f"e0_{n}", c) for n in names}
        x_in, y_out = [s["in0"], s["in1"]], [s["out0"], s["out1"]]

        LAG_UP, LAG_TURN2, LAG_DOWN, LAG_OUT = 2, 4, 6, 7
        PEEL = 10

        def steps(eng, step):
            for t in range(PEEL):
                step(t, t // 2, t % 2)
            with eng.Fori(PEEL // 2, NT // 2) as i:
                for b in range(2):
                    step(i * 2 + b, i, b)
            for t in range(NT, NT + LAG_OUT):
                step(t, t // 2, t % 2)

        def tile_at(t, i, b, lag):
            if isinstance(t, int) and not 0 <= t - lag < NT:
                return None
            buf = (b - lag) % 2
            return t - lag, i + (b - lag - buf) // 2, buf

        with nc.Block() as block:
            @block.sync
            def _(sp):
                sp.wait_ge(scattered, 16 * NB)

                def load(j, b):
                    sp.dma_start(xin[b][:], xg.rearrange("(t p) d -> t p d", p=P)[j]).then_inc(x_in[b], 16)

                def store(j, b):
                    sp.wait_ge(s["y_done"], j + 1)
                    sp.dma_start(yg.rearrange("(t p) d -> t p d", p=P)[j], y[b][:]).then_inc(y_out[b], 16)

                def step(t, i, b):
                    if tile_at(t, i, b, LAG_OUT):
                        store(t - LAG_OUT, 1 - b)
                    if isinstance(t, int) and (t == 0 or t + 1 >= NT):
                        return
                    sp.wait_ge(s["turned"], t)
                    load(t + 1, 1 - b)

                for b in range(2):
                    load(b, b)
                for t in range(PEEL):
                    step(t, t // 2, t % 2)
                with sp.Fori(PEEL // 2, NT // 2 - 1) as i:
                    for b in range(2):
                        step(i * 2 + b, i, b)
                for t in range(NT - 2, NT + LAG_OUT):
                    step(t, t // 2, t % 2)

            @block.tensor
            def _(pe):
                def turn(j, i, b):
                    pe.wait_ge(x_in[b], i * 16 + 16)
                    at_least(pe, s["scaled"], j - 1)
                    for a in range(KD):
                        ins = pe.transpose(psA[b][:, a, :], xin[b][:, a * P:(a + 1) * P], ident[:])
                    ins.then_inc(s["turned"], 1)

                def up(j, i, b):
                    e = pe.value_load(owner[0:1, bass.ds(j, 1)], min_val=0, max_val=SH - 1)
                    pe.wait_ge(s["split"], j + 1)
                    at_least(pe, s["up_out"], j - 1)
                    for n, (a, part) in enumerate([(a, part) for a in range(KD) for part in range(2)]):
                        ins = pe.matmul(psH[b][:], hs[b][part][:, a, :], w1t[:, e, a, :], start=(n == 0), stop=(n == 2 * KD - 1))
                    ins.then_inc(s["up"], 1)

                def turn2(j, i, b):
                    pe.wait_ge(s["up_out"], j + 1)
                    at_least(pe, s["silu"], j - 1)
                    for t in range(KF):
                        ins = pe.transpose(psT[b][:, t, :], u[b][:, t * P:(t + 1) * P], ident[:])
                    ins.then_inc(s["turned2"], 1)

                def down(j, i, b):
                    e = pe.value_load(owner[0:1, bass.ds(j, 1)], min_val=0, max_val=SH - 1)
                    pe.wait_ge(s["split2"], j + 1)
                    at_least(pe, s["y_done"], j - 1)
                    for n, (t, part) in enumerate([(t, part) for t in range(KF) for part in range(2)]):
                        ins = pe.matmul(psY[b][:], gs[b][part][:, t, :], w2t[:, e, t, :], start=(n == 0), stop=(n == 2 * KF - 1))
                    ins.then_inc(s["down"], 1)

                def step(t, i, b):
                    for lag, do in ((0, turn), (LAG_TURN2, turn2), (LAG_UP, up), (LAG_DOWN, down)):
                        at = tile_at(t, i, b, lag)
                        if at:
                            do(*at)

                steps(pe, step)

            @block.scalar
            def _(act):
                def scale(j, i, b):
                    act.wait_ge(s["turned"], j + 1)
                    at_least(act, s["split"], j - 1)
                    for a in range(KD):
                        ins = act.activation(h[b][:, a, :], psA[b][:, a, :], ACT.Identity, bias=beta[:, a:a + 1],
                                             scale=gamma[:, a:a + 1])
                    ins.then_inc(s["scaled"], 1)

                def silu(j, i, b):
                    e = act.value_load(owner[0:1, bass.ds(j, 1)], min_val=0, max_val=SH - 1)
                    act.wait_ge(s["turned2"], j + 1)
                    at_least(act, s["split2"], j - 1)
                    for t in range(KF):
                        ins = act.activation(g[b][:, t, :], psT[b][:, t, :], ACT.Silu, scale=s1[:, e, t:t + 1])
                    ins.then_inc(s["silu"], 1)

                def step(t, i, b):
                    for lag, do in ((0, scale), (LAG_TURN2, silu)):
                        at = tile_at(t, i, b, lag)
                        if at:
                            do(*at)

                steps(act, step)

            @block.vector
            def _(dve):
                dve.tensor_scalar(s2g[:], s2[:, SH, :], gates[:, 2:3], None, ALU.mult).then_inc(s["s2g"], 1)

                def split(j, i, b):
                    dve.wait_ge(s["scaled"], j + 1)
                    at_least(dve, s["up"], j - 1)
                    k = Steps(dve, s["steps"], j)
                    k.step(dve.tensor_copy(hs[b][0][:], h[b][:]))
                    dve.tensor_tensor(hs[b][1][:], h[b][:], hs[b][0][:].bitcast(F32), ALU.subtract).then_inc(s["split"], 1)

                def up_out(j, i, b):
                    dve.wait_ge(s["up"], j + 1)
                    at_least(dve, s["turned2"], j - 1)
                    dve.tensor_copy(u[b][:], psH[b][:]).then_inc(s["up_out"], 1)

                def split2(j, i, b):
                    dve.wait_ge(s["silu"], j + 1)
                    at_least(dve, s["down"], j - 1)
                    k = Steps(dve, s["steps2"], j)
                    k.step(dve.tensor_copy(gs[b][0][:], g[b][:]))
                    dve.tensor_tensor(gs[b][1][:], g[b][:], gs[b][0][:].bitcast(F32), ALU.subtract).then_inc(s["split2"], 1)

                def out(j, i, b):
                    e = dve.value_load(owner[0:1, bass.ds(j, 1)], min_val=0, max_val=SH - 1)
                    dve.wait_ge(s["down"], j + 1)
                    at_least(dve, y_out[b], i * 16)
                    dve.tensor_tensor(y[b][:], psY[b][:], s2[:, e, :], ALU.mult).then_inc(s["y_done"], 1)

                def step(t, i, b):
                    for lag, do in ((LAG_OUT, out), (LAG_UP + 1, up_out), (LAG_TURN2 + 1, split2), (1, split)):
                        at = tile_at(t, i, b, lag)
                        if at:
                            do(*at)

                steps(dve, step)
                for i in range(NB):
                    dve.wait_ge(gathered[i], 16)
                    dve.wait_ge(s["shared_in"], i * 2 + 2)
                    dve.scalar_tensor_tensor(out=x_sb[:, i, :], in0=n_sb[:, i, :], scalar=prob[:, i:i + 1],
                                             in1=x_sb[:, i, :], op0=ALU.mult, op1=ALU.add).then_inc(s["combined"], 1)
                    if i > 0:
                        dve.wait_ge(s["combined"], i)
                        dve.bn_stats(x_stats[:, i - 1, :], x_sb[:, i - 1, :])
                dve.wait_ge(s["combined"], NB)
                dve.bn_stats(x_stats[:, NB - 1, :], x_sb[:, NB - 1, :])

            @block.gpsimd
            def _(pool):
                pool.wait_ge(s["s2g"], 1)
                with pool.Fori(0, NB) as i:
                    pool.tensor_tensor(sh[:, i, :], sh[:, i, :], s2g[:], ALU.mult).then_inc(s["shared_in"], 1)
                    pool.wait_ge(s["shared_in"], i * 2 + 1)
                    pool.tensor_tensor(x_sb[:, i, :], x_sb[:, i, :], sh[:, i, :], ALU.add).then_inc(s["shared_in"], 1)
                for b in range(2):
                    pool.wait_ge(y_out[b], NT // 2 * 16)
                for i in range(NB):
                    pool.indirect_dma_start(n_sb[:, i, :], None, yg, bass.IndirectOffsetOnAxis(ap=pos[:, i:i + 1], axis=0))\
                        .then_inc(gathered[i], 16)


def attention_1(nc, A, sb, ps, sem, NB, D, KD, x_sb, ctx_sb, ident, gates, x_mean, x_rstd, c_mean, c_rstd,
                x_stats, c_stats, nt):
    DH = 128
    NI = A["L1_xattn_Wq"].shape[1]
    NH = NI // DH
    NK = 2 * P
    scale = float(DH) ** -0.5
    with ExitStack() as c:
        wq = [sb(f"a1_wq{n}", [P, KD, NI], F32R, c) for n in ("hi", "lo")]
        wkv = [sb(f"a1_wkv{n}", [P, KD, 2 * NI], F32R, c) for n in ("hi", "lo")]
        wo = [sb(f"a1_wo{n}", [P, NH, D], F32R, c) for n in ("hi", "lo")]
        bq, bk = sb("a1_bq", [P, NH], F32, c), sb("a1_bk", [P, NH], F32, c)
        bv, bo = sb("a1_bv", [P, NI], F32, c), sb("a1_bo", [P, D], F32, c)
        gam, bet = sb("a1_gam", [P, 2, KD], F32, c), sb("a1_bet", [P, 2, KD], F32, c)

        with ExitStack() as r:
            rawq = sb("a1_rawq", [P, KD, NI], F32, r)
            rawkv = sb("a1_rawkv", [P, KD, 2 * NI], F32, r)
            rawo = sb("a1_rawo", [P, NH, D], F32, r)
            s = {n: sem(f"a1w_{n}", r) for n in "q_in kv_in o_in small_in scaled hi lo steps".split()}
            with nc.Block() as block:
                @block.sync
                def _(sp):
                    sp.dma_start(rawq[:], A["L1_xattn_Wq"].rearrange("(k p) n -> p k n", p=P)).then_inc(s["q_in"], 16)
                    sp.dma_start(rawkv[:], A["L1_xattn_Wkv"].rearrange("(k p) n -> p k n", p=P)).then_inc(s["kv_in"], 16)
                    sp.dma_start(rawo[:], A["L1_xattn_Wo"].rearrange("(h p) n -> p h n", p=P)).then_inc(s["o_in"], 16)
                    with nc.allow_non_contiguous_dma(reason="a few hundred small parameters"):
                        for dst, src in ((bq[:], A["L1_xattn_bq"].rearrange("(h p) -> p h", p=P)),
                                         (bk[:], A["L1_xattn_bkv"][0:NI].rearrange("(h p) -> p h", p=P)),
                                         (bv[:], A["L1_xattn_bkv"][NI:2 * NI].partition_broadcast(P)),
                                         (bo[:], A["L1_xattn_bo"].partition_broadcast(P)),
                                         (gam[:, 0, :], A["L1_xattn_gamma_media"].rearrange("(k p) -> p k", p=P)),
                                         (gam[:, 1, :], A["L1_xattn_gamma_lat"].rearrange("(k p) -> p k", p=P)),
                                         (bet[:, 0, :], A["L1_xattn_beta_media"].rearrange("(k p) -> p k", p=P)),
                                         (bet[:, 1, :], A["L1_xattn_beta_lat"].rearrange("(k p) -> p k", p=P))):
                            sp.dma_start(dst, src).then_inc(s["small_in"], 16)
                    sp.wait_ge(s["small_in"], 128)

                flat = lambda t: t.rearrange("p a n -> p (a n)")
                chunks = [(wq, rawq, 0)] + [(wkv, rawkv, n) for n in range(2)] + [(wo, rawo, 0)]

                @block.scalar
                def _(act):
                    act.wait_ge(s["q_in"], 16)
                    act.activation(rawq[:], rawq[:], ACT.Copy, scale=scale).then_inc(s["scaled"], 1)
                    act.wait_ge(s["scaled"], 1)
                    for n, (w, raw, part) in enumerate(chunks):
                        if n == 1:
                            act.wait_ge(s["kv_in"], 16)
                        if n == 3:
                            act.wait_ge(s["o_in"], 16)
                        cols = slice(2048 * part, 2048 * (part + 1))
                        act.activation(flat(w[0][:])[:, cols], flat(raw[:])[:, cols], ACT.Copy).then_inc(s["hi"], 1)

                @block.vector
                def _(dve):
                    for n, (w, raw, part) in enumerate(chunks):
                        cols = slice(2048 * part, 2048 * (part + 1))
                        dve.wait_ge(s["hi"], n + 1)
                        dve.tensor_tensor(flat(w[1][:])[:, cols], flat(raw[:])[:, cols], flat(w[0][:])[:, cols].bitcast(F32),
                                          ALU.subtract)
                    dve.wait_ge(s["small_in"], 128)
                    dve.tensor_scalar(bq[:], bq[:], scale, None, ALU.mult)
                    dve.tensor_scalar(bo[:], bo[:], gates[:, 1:2], None, ALU.mult)
                    k = Steps(dve, s["steps"])
                    norm_steps(dve, k, x_stats, x_mean[:], x_rstd[:], [t[:] for t in nt], True)
                    norm_steps(dve, k, c_stats, c_mean[:], c_rstd[:], [t[:] for t in nt], False)

        normed = [sb(f"a1_n{n}", [P, D], F32, c) for n in ("media", "lat")]
        kvf = sb("a1_kvf", [P, KD, NK], F32, c)
        kv = [[sb(f"a1_kv{n}{i}", [P, KD, NK], F32R, c) for n in ("hi", "lo")] for i in range(2)]
        q = [sb(f"a1_q{n}", [P, NH, P], F32R, c) for n in ("hi", "lo")]
        k_ = [sb(f"a1_k{n}", [P, NH, NK], F32R, c) for n in ("hi", "lo")]
        vf = sb("a1_vf", [P, 512], F32, c)
        v = [sb(f"a1_v{n}", [P, 2, NI], F32R, c) for n in ("hi", "lo")]
        nmax, sums, rsum = (sb(f"a1_{n}", [P, NH], F32, c) for n in ("nmax", "sums", "rsum"))
        probs = sb("a1_probs", [P, NH, NK], F32, c)
        pT = [sb(f"a1_pT{n}", [P, NH, 2, P], F32R, c) for n in ("hi", "lo")]
        oT = [sb(f"a1_oT{n}", [P, NH, P], F32R, c) for n in ("hi", "lo")]
        psA = [ps(f"a1_psA{i}", [P, 3 * P], F32, c) for i in range(2)]
        psS = [ps(f"a1_psS{i}", [P, NK], F32, c) for i in range(2)]
        psT = ps("a1_psT", [P, 2, P], F32, c)
        psO = ps("a1_psO", [P, P], F32, c)
        psV = ps("a1_psV", [P, 512], F32, c)
        psY = ps("a1_psY", [P, D], F32, c)
        names = ("normed resid kv_turned kv_scaled kv_hi kv_lo qk_done qk_hi qk_lo s_done max_done exp_done rsum_done "
                 "p_done t_done pt_hi pt_lo pv_done o_hi o_lo v_done v_f v_hi v_lo y_done x_done").split()
        s = {n: sem(f"a1_{n}", c) for n in names}
        CHUNKS = {0: 0, 1: 1, 3: 2, 5: 3}

        def schedule(batch, finish, eng):
            batch(0, 0, True)
            batch(1, 1, True)
            with eng.Fori(1, NB // 2 - 1) as i:
                for par in range(2):
                    batch(i * 2 + par, par, True)
            batch(NB - 2, 0, True)
            batch(NB - 1, 1, False)
            finish()

        def exists(n):
            return not isinstance(n, int) or 0 <= n < NH * NB

        with nc.Block() as block:
            @block.tensor
            def _(pe):
                def turn_kv(b):
                    pe.wait_ge(s["normed"], b * 2 + 2)
                    at_least(pe, s["v_f"], b * 4)
                    for m in range(2):
                        for a in range(KD):
                            ins = pe.transpose(psV[:, (a * 2 + m) * P:(a * 2 + m + 1) * P], normed[m][:, a * P:(a + 1) * P], ident[:])
                    ins.then_inc(s["kv_turned"], 1)

                def project(n, b, h, par):
                    if h == 0:
                        pe.wait_ge(s["kv_lo"], b + 1)
                    at_least(pe, s["qk_lo"], n - 1)
                    for w, col, lo, width, at in ((wq, h, P, P, 0), (wkv, h, 0, NK, P)):
                        for m, (a, (x, y)) in enumerate([(a, xy) for a in range(KD) for xy in PARTS3]):
                            ins = pe.matmul(psA[h % 2][:, at:at + width], w[x][:, a, col * DH:(col + 1) * DH],
                                            kv[par][y][:, a, lo:lo + width], start=(m == 0), stop=(m == 3 * KD - 1))
                    ins.then_inc(s["qk_done"], 1)

                def values(b, ch, par):
                    half, kt = divmod(ch, 2)
                    at_least(pe, s["v_f"], b * 4 + ch)
                    if ch == 0:
                        pe.wait_ge(s["kv_scaled"], b + 1)
                    for m, (a, (x, y)) in enumerate([(a, xy) for a in range(KD) for xy in PARTS3]):
                        ins = pe.matmul(psV[:], kv[par][x][:, a, kt * P:(kt + 1) * P],
                                        wkv[y][:, a, NI + half * 512:NI + (half + 1) * 512], start=(m == 0), stop=(m == 3 * KD - 1))
                    ins.then_inc(s["v_done"], 1)

                def score(n, h):
                    pe.wait_ge(s["qk_lo"], n + 1)
                    at_least(pe, s["exp_done"], n - 1)
                    for m, (x, y) in enumerate(PARTS3):
                        ins = pe.matmul(psS[h % 2][:], q[x][:, h, :], k_[y][:, h, :], start=(m == 0), stop=(m == 2))
                    ins.then_inc(s["s_done"], 1)

                def turn(n, h):
                    pe.wait_ge(s["p_done"], n + 1)
                    at_least(pe, s["pt_lo"], n)
                    for kt in range(2):
                        ins = pe.transpose(psT[:, kt, :], probs[:, h, kt * P:(kt + 1) * P], ident[:])
                    ins.then_inc(s["t_done"], 1)

                def apply(n, b, h):
                    pe.wait_ge(s["pt_lo"], n + 1)
                    at_least(pe, s["o_lo"], n)
                    if h in (0, 4):
                        pe.wait_ge(s["v_lo"], b * 4 + (2 if h == 0 else 4))
                    for m, (kt, (x, y)) in enumerate([(kt, xy) for kt in range(2) for xy in PARTS3]):
                        ins = pe.matmul(psO[:], v[x][:, kt, h * DH:(h + 1) * DH], pT[y][:, h, kt, :], start=(m == 0), stop=(m == 5))
                    ins.then_inc(s["pv_done"], 1)

                def output(b):
                    pe.wait_ge(s["o_lo"], b * NH + NH)
                    at_least(pe, s["x_done"], b)
                    for m, (h, (x, y)) in enumerate([(h, xy) for h in range(NH) for xy in PARTS3]):
                        ins = pe.matmul(psY[:], oT[x][:, h, :], wo[y][:, h, :], start=(m == 0), stop=(m == 3 * NH - 1))
                    ins.then_inc(s["y_done"], 1)

                def later(b, h, lag):
                    return (b, h - lag) if h >= lag else (b - 1, h - lag + NH)

                def rest(b, h):
                    for lag, do in ((1, "s"), (3, "t"), (4, "a")):
                        bb, hh = later(b, h, lag)
                        n = bb * NH + hh
                        if do == "a" and h == 4 and exists((b - 1) * NH):
                            output(b - 1)
                        if not exists(n):
                            continue
                        if do == "s":
                            score(n, hh)
                        elif do == "t":
                            turn(n, hh)
                        else:
                            apply(n, bb, hh)

                def batch(b, par, more):
                    for h in range(NH):
                        project(b * NH + h, b, h, par)
                        if h in CHUNKS:
                            values(b, CHUNKS[h], par)
                        if h == 6 and more:
                            turn_kv(b + 1)
                        rest(b, h)

                def finish():
                    for h in range(5):
                        rest(NB, h)

                turn_kv(0)
                schedule(batch, finish, pe)

            @block.scalar
            def _(act):
                def scale_kv(b):
                    act.wait_ge(s["kv_turned"], b + 1)
                    at_least(act, s["kv_lo"], b)
                    for m in range(2):
                        for a in range(KD):
                            ins = act.activation(kvf[:, a, m * P:(m + 1) * P], psV[:, (a * 2 + m) * P:(a * 2 + m + 1) * P], ACT.Identity,
                                                 bias=bet[:, m, a:a + 1], scale=gam[:, m, a:a + 1])
                    ins.then_inc(s["kv_scaled"], 1)

                def project(n, h):
                    act.wait_ge(s["qk_done"], n + 1)
                    act.activation(q[0][:, h, :], psA[h % 2][:, 0:P], ACT.Identity, bias=bq[:, h:h + 1])
                    act.activation(k_[0][:, h, :], psA[h % 2][:, P:3 * P], ACT.Identity, bias=bk[:, h:h + 1]).then_inc(s["qk_hi"], 1)

                def exps(n, h):
                    act.wait_ge(s["max_done"], n + 1)
                    act.activation(probs[:, h, :], psS[h % 2][:], ACT.Exp, bias=nmax[:, h:h + 1],
                                   accum_out=sums[:, h:h + 1]).then_inc(s["exp_done"], 1)

                def turn(n, h):
                    act.wait_ge(s["t_done"], n + 1)
                    act.activation(pT[0][:, h, :, :], psT[:], ACT.Copy).then_inc(s["pt_hi"], 1)

                def apply(n, h):
                    act.wait_ge(s["pv_done"], n + 1)
                    act.activation(oT[0][:, h, :], psO[:], ACT.Copy).then_inc(s["o_hi"], 1)

                def values(b, ch):
                    half, kt = divmod(ch, 2)
                    act.wait_ge(s["v_f"], b * 4 + ch + 1)
                    act.activation(v[0][:, kt, half * 512:(half + 1) * 512], vf[:], ACT.Copy).then_inc(s["v_hi"], 1)

                def rest(b, h, lags):
                    for lag, do in lags:
                        bb, hh = (b, h - lag) if h >= lag else (b - 1, h - lag + NH)
                        if exists(bb * NH + hh):
                            do(bb * NH + hh, hh)

                def batch(b, par, more):
                    for h in range(NH):
                        rest(b, h, ((4, turn), (5, apply)))
                        if h - 1 in CHUNKS:
                            values(b, CHUNKS[h - 1])
                        rest(b, h, ((2, exps),))
                        if h == 7 and more:
                            scale_kv(b + 1)
                        project(b * NH + h, h)

                def finish():
                    for h in range(5):
                        rest(NB, h, ((4, turn), (5, apply), (2, exps)))

                scale_kv(0)
                schedule(batch, finish, act)

            @block.gpsimd
            def _(pool):
                with pool.Fori(0, NB) as i:
                    pool.wait_ge(s["normed"], i * 2 + 2)
                    pool.tensor_tensor(x_sb[:, i, :], x_sb[:, i, :], bo[:], ALU.add).then_inc(s["resid"], 1)

            @block.vector
            def _(dve):
                def norm(b):
                    at_least(dve, s["kv_turned"], b)
                    for m, (src, mean, rstd) in enumerate(((ctx_sb, c_mean, c_rstd), (x_sb, x_mean, x_rstd))):
                        at = b if isinstance(b, int) else bass.ds(b, 1)
                        one = slice(b, b + 1) if isinstance(b, int) else bass.ds(b, 1)
                        dve.tensor_scalar(normed[m][:], src[:, b, :], mean[:, one], rstd[:, one],
                                          ALU.subtract, ALU.mult).then_inc(s["normed"], 1)

                def split_kv(b, par):
                    dve.wait_ge(s["kv_scaled"], b + 1)
                    dve.tensor_copy(kv[par][0][:], kvf[:]).then_inc(s["kv_hi"], 1)
                    dve.wait_ge(s["kv_hi"], b + 1)
                    dve.tensor_tensor(kv[par][1][:], kvf[:], kv[par][0][:].bitcast(F32), ALU.subtract).then_inc(s["kv_lo"], 1)

                def project(n, h):
                    dve.wait_ge(s["qk_hi"], n + 1)
                    dve.scalar_tensor_tensor(out=q[1][:, h, :], in0=psA[h % 2][:, 0:P], scalar=bq[:, h:h + 1],
                                             in1=q[0][:, h, :].bitcast(F32), op0=ALU.add, op1=ALU.subtract)
                    dve.scalar_tensor_tensor(out=k_[1][:, h, :], in0=psA[h % 2][:, P:3 * P], scalar=bk[:, h:h + 1],
                                             in1=k_[0][:, h, :].bitcast(F32), op0=ALU.add, op1=ALU.subtract).then_inc(s["qk_lo"], 1)

                def values(b, ch):
                    half, kt = divmod(ch, 2)
                    dve.wait_ge(s["v_done"], b * 4 + ch + 1)
                    at_least(dve, s["v_lo"], b * 4 + ch)
                    cols = slice(half * 512, (half + 1) * 512)
                    dve.tensor_tensor(vf[:], psV[:], bv[:, cols], ALU.add).then_inc(s["v_f"], 1)

                def values_lo(b, ch):
                    half, kt = divmod(ch, 2)
                    cols = slice(half * 512, (half + 1) * 512)
                    dve.wait_ge(s["v_hi"], b * 4 + ch + 1)
                    dve.tensor_tensor(v[1][:, kt, cols], vf[:], v[0][:, kt, cols].bitcast(F32), ALU.subtract).then_inc(s["v_lo"], 1)

                def maximum(n, h):
                    dve.wait_ge(s["s_done"], n + 1)
                    dve.tensor_reduce(nmax[:, h:h + 1], psS[h % 2][:], AX.X, ALU.max, negate=True).then_inc(s["max_done"], 1)

                def normalize(n, h):
                    dve.wait_ge(s["exp_done"], n + 1)
                    dve.reciprocal(rsum[:, h:h + 1], sums[:, h:h + 1]).then_inc(s["rsum_done"], 1)
                    dve.wait_ge(s["rsum_done"], n + 1)
                    dve.tensor_scalar(probs[:, h, :], probs[:, h, :], rsum[:, h:h + 1], None, ALU.mult).then_inc(s["p_done"], 1)

                def turn(n, h):
                    dve.wait_ge(s["pt_hi"], n + 1)
                    dve.tensor_tensor(pT[1][:, h, :, :], psT[:], pT[0][:, h, :, :].bitcast(F32), ALU.subtract).then_inc(s["pt_lo"], 1)

                def apply(n, h):
                    dve.wait_ge(s["o_hi"], n + 1)
                    dve.tensor_tensor(oT[1][:, h, :], psO[:], oT[0][:, h, :].bitcast(F32), ALU.subtract).then_inc(s["o_lo"], 1)

                def residual(b):
                    dve.wait_ge(s["y_done"], b + 1)
                    dve.wait_ge(s["resid"], b + 1)
                    dve.scalar_tensor_tensor(out=x_sb[:, b, :], in0=psY[:], scalar=gates[:, 1:2], in1=x_sb[:, b, :],
                                             op0=ALU.mult, op1=ALU.add).then_inc(s["x_done"], 1)

                def statistics(b):
                    dve.wait_ge(s["x_done"], b + 1)
                    dve.bn_stats(x_stats[:, b, :], x_sb[:, b, :])

                def steps(b, h, lags):
                    for lag, do in lags:
                        bb, hh = (b, h - lag) if h >= lag else (b - 1, h - lag + NH)
                        if exists(bb * NH + hh):
                            do(bb * NH + hh, hh)

                def batch(b, par, more):
                    for h in range(NH):
                        steps(b, h, ((2, maximum), (4, turn), (5, apply)))
                        if h - 1 in CHUNKS:
                            values_lo(b, CHUNKS[h - 1])
                        steps(b, h, ((2, normalize),))
                        if h == 2 and more:
                            norm(b + 1)
                        if h == 5 and exists((b - 1) * NH):
                            residual(b - 1)
                        if h == 6 and exists((b - 1) * NH):
                            statistics(b - 1)
                        if h == 7 and more:
                            split_kv(b + 1, 1 - par)
                        project(b * NH + h, h)
                        if h in CHUNKS:
                            values(b, CHUNKS[h])

                def finish():
                    for h in range(5):
                        steps(NB, h, ((2, maximum), (4, turn), (5, apply), (2, normalize)))
                    residual(NB - 1)
                    statistics(NB - 1)

                norm(0)
                split_kv(0, 0)
                schedule(batch, finish, dve)


def mixture_1(nc, A, sb, ps, sem, NB, D, KD, x_sb, ctx_sb, ident, gates, x_mean, x_rstd, c_mean, c_rstd,
              x_stats, c_stats, nt):
    NE, _, F = A["fc1_T"].shape
    FS = A["sh1_T"].shape[1]
    NTOK = NB * P
    CAP = -(-(-(-NTOK * 2 // NE) * 5) // 4)
    NSLOT = NE * CAP
    xg = nc.dram_tensor("m1_sorted", (NSLOT + 2 * NTOK, D), F32, kind="Internal").ap()
    yg = nc.dram_tensor("m1_expert_out", (NSLOT + P, D), F32, kind="Internal").ap()
    KS = FS // P
    with ExitStack() as c:
        n_sb = sb("m1_n", [P, NB, D], F32, c)
        sh = sb("m1_shared", [P, NB, D], F32, c)
        b2s = sb("m1_b2s", [P, D], F32, c)
        into = [sb(f"m1_into{i}", [P, NB], U32, c) for i in range(2)]
        back = [sb(f"m1_back{i}", [P, NB], U32, c) for i in range(2)]
        wk = [sb(f"m1_wk{i}", [P, NB], F32, c) for i in range(2)]
        ones = sb("m1_ones", [P, P], F32, c)
        upper = sb("m1_upper", [P, P], F32, c)
        scattered = sem("m1_scattered", c)
        with ExitStack() as t:
            w1 = [sb(f"m1_ws1{n}", [P, KD, FS], F32R, t) for n in ("hi", "lo")]
            w2 = [sb(f"m1_ws2{n}", [P, KS, D], F32R, t) for n in ("hi", "lo")]
            b1 = sb("m1_bs1", [P, KS], F32, t)
            logits = sb("m1_logits", [P, NB, NE], F32, t)
            proj = sb("m1_proj", [P, KD, NE], F32, t)
            pb, eb = sb("m1_pb", [P, NE], F32, t), sb("m1_eb", [P, NE], F32, t)
            shared_weights(nc, A, sb, ps, sem, D, KD, KS, FS, w1, w2, b1, b2s, proj, pb, eb, ones, upper, gates, xg, yg, NSLOT, x_sb)
            hT = [sb(f"m1_hT{n}", [P, KD, NB, P], F32R, t) for n in ("hi", "lo")]
            token_norms(nc, sb, ps, sem, NB, D, KD, x_sb, ident, x_mean, x_rstd, x_stats, nt, n_sb, hT,
                        logits, proj, None, None, NE, "m1", False)
            wmat, cur, hots, ws = top2(nc, sb, ps, sem, NB, NE, logits, pb, eb, t)
            shared_gelu(nc, sb, ps, sem, 0, NB // 2, D, KD, KS, hT, w1, w2, b1, sh, gates, "a",
                        search=(NB, NE, CAP, wmat, cur, ones))
            places(nc, sb, ps, sem, NB, NE, CAP, NSLOT, NTOK, wmat, cur, hots, ws, into, back, wk, ones, upper, gates)
            shared_gelu(nc, sb, ps, sem, NB // 2, NB, D, KD, KS, hT, w1, w2, b1, sh, gates, "b",
                        scatter=(into, n_sb, xg, scattered, NB))
        experts_gelu(nc, A, sb, ps, sem, NB, NE, CAP, D, KD, F, x_sb, sh, b2s, ident, xg, yg, n_sb, back, wk, scattered)


def shared_weights(nc, A, sb, ps, sem, D, KD, KS, FS, w1, w2, b1, b2s, proj, pb, eb, ones, upper, gates, xg, yg, NSLOT, x_sb):
    with ExitStack() as c:
        raw1 = sb("d_raw1", [P, KD, FS], F32, c)
        raw2 = sb("d_raw2", [P, KS, D], F32, c)
        zeros = sb("d_zeros", [P, D], F32, c)
        s = {n: sem(f"d_{n}", c) for n in "w1_in w2_in small_in hi lo const_done zero_out".split()}
        flat = lambda t: t.rearrange("p a n -> p (a n)")
        with nc.Block() as block:
            @block.sync
            def _(sp):
                sp.dma_start(raw1[:], A["sh1_T"].rearrange("(k p) f -> p k f", p=P)).then_inc(s["w1_in"], 16)
                sp.dma_start(raw2[:], A["sh2_T"].rearrange("(k p) d -> p k d", p=P)).then_inc(s["w2_in"], 16)
                with nc.allow_non_contiguous_dma(reason="a few hundred small parameters"):
                    for dst, src in ((b1[:], A["L1_ffn_sh1_b"].rearrange("(k p) -> p k", p=P)),
                                     (b2s[:], A["L1_ffn_sh2_b"].partition_broadcast(P)),
                                     (proj[:], A["proj_T"].rearrange("(k p) e -> p k e", p=P)),
                                     (pb[:], A["L1_ffn_proj_b"].partition_broadcast(P)),
                                     (eb[:], A["L1_ffn_expert_bias"].partition_broadcast(P))):
                        sp.dma_start(dst, src).then_inc(s["small_in"], 16)
                sp.wait_ge(s["const_done"], 2)
                sp.dma_start(xg[0:NSLOT].rearrange("(t p) d -> p t d", p=P), zeros[:].unsqueeze(1).to_broadcast([P, NSLOT // P, D]))\
                  .then_inc(s["zero_out"], 16)
                sp.dma_start(yg[NSLOT:NSLOT + P], zeros[:]).then_inc(s["zero_out"], 16)
                sp.wait_ge(s["zero_out"], 32)
                sp.wait_ge(s["small_in"], 80)

            @block.gpsimd
            def _(pool):
                pool.memset(zeros[:], 0.0).then_inc(s["const_done"], 1)
                pool.memset(ones[:], 1.0).then_inc(s["const_done"], 1)
                pool.wait_ge(s["const_done"], 2)
                pool.affine_select(out=upper[:], in_=ones[:], compare_op=ALU.is_gt, fill=0.0, base=0,
                                   pattern=[[1, P]], channel_multiplier=-1).then_inc(s["const_done"], 1)

            @block.scalar
            def _(act):
                act.wait_ge(s["w1_in"], 16)
                act.activation(flat(w1[0][:]), flat(raw1[:]), ACT.Copy).then_inc(s["hi"], 1)
                act.wait_ge(s["w2_in"], 16)
                act.activation(flat(w2[0][:]), flat(raw2[:]), ACT.Copy).then_inc(s["hi"], 1)

            @block.vector
            def _(dve):
                for n, (w, raw) in enumerate(((w1, raw1), (w2, raw2))):
                    dve.wait_ge(s["hi"], n + 1)
                    dve.tensor_tensor(flat(w[1][:]), flat(raw[:]), flat(w[0][:]).bitcast(F32), ALU.subtract)
                dve.wait_ge(s["small_in"], 80)
                dve.tensor_scalar(b2s[:], b2s[:], gates[:, 3:4], None, ALU.mult)


def top2(nc, sb, ps, sem, NB, NE, logits, pb, eb, c):
    wmat = sb("r1_wmat", [P, NB, NE], F32, c)
    hots = [sb(f"r1_hot{i}", [P, NB, NE], F32, c) for i in range(2)]
    ws = [sb(f"r1_w{i}", [P, NB], F32, c) for i in range(2)]
    cur = sb("r1_cur", [P, NE], I32, c)
    with ExitStack() as t:
        z = sb("r1_z", [P, NB, NE], F32, t)
        sg = sb("r1_sg", [P, NB, NE], F32, t)
        best = sb("r1_best", [P, NB, 8], F32, t)
        index = sb("r1_index", [P, NB, 8], U32, t)
        which = sb("r1_which", [P, 2, NB], F32, t)
        iota_i = sb("r1_iota_i", [P, NE], I32, t)
        iota = sb("r1_iota", [P, NE], F32, t)
        tmp = sb("r1_tmp", [P, NB, NE], F32, t)
        total = sb("r1_total", [P, NB], F32, t)
        s = {n: sem(f"r1_{n}", t) for n in "steps iota_done biased sigmoid".split()}
        wide = lambda a: a.unsqueeze(2).to_broadcast([P, NB, NE])
        with nc.Block() as block:
            @block.gpsimd
            def _(pool):
                pool.iota(iota_i[:], pattern=[[1, NE]], base=0, channel_multiplier=0).then_inc(s["iota_done"], 1)

            @block.scalar
            def _(act):
                act.wait_ge(s["biased"], 1)
                act.activation(sg[:], z[:], ACT.Sigmoid).then_inc(s["sigmoid"], 1)

            @block.vector
            def _(dve):
                k = Steps(dve, s["steps"])
                dve.tensor_tensor(z[:], logits[:], pb[:].unsqueeze(1).to_broadcast([P, NB, NE]), ALU.add).then_inc(s["biased"], 1)
                dve.memset(cur[:], 0)
                dve.wait_ge(s["iota_done"], 1)
                k.step(dve.tensor_copy(iota[:], iota_i[:]))
                dve.wait_ge(s["sigmoid"], 1)
                k.step(dve.tensor_tensor(sg[:], sg[:], eb[:].unsqueeze(1).to_broadcast([P, NB, NE]), ALU.add))
                k.step(dve.tensor_scalar(sg[:], sg[:], 1e-12, None, ALU.max))
                for i in range(NB):
                    ins = dve.max(best[:, i, :], sg[:, i, :])
                k.step(ins)
                for i in range(NB):
                    ins = dve.max_index(index[:, i, :], best[:, i, :], sg[:, i, :])
                k.step(ins)
                for n in range(2):
                    ins = dve.tensor_copy(which[:, n, :], index[:, :, n])
                k.step(ins)
                k.step(dve.tensor_tensor(total[:], best[:, :, 0], best[:, :, 1], ALU.add))
                k.step(dve.reciprocal(total[:], total[:]))
                for n in range(2):
                    dve.tensor_tensor(ws[n][:], best[:, :, n], total[:], ALU.mult)
                    ins = dve.tensor_tensor(hots[n][:], wide(which[:, n, :]), iota[:].unsqueeze(1).to_broadcast([P, NB, NE]),
                                            ALU.is_equal)
                k.step(ins)
                dve.tensor_tensor(wmat[:], hots[0][:], wide(ws[0][:]), ALU.mult)
                k.step(dve.tensor_tensor(tmp[:], hots[1][:], wide(ws[1][:]), ALU.mult))
                dve.tensor_tensor(wmat[:], wmat[:], tmp[:], ALU.add)
    return wmat, cur, hots, ws


def shared_gelu(nc, sb, ps, sem, first_tile, end_tile, D, KD, KS, hT, w1, w2, b1, sh, gates, tag, search=None, scatter=None):
    PAIRS = (end_tile - first_tile) // 2
    NQ = KS // 2
    with ExitStack() as c:
        g = [sb(f"s1{tag}_g{i}", [P, 2, 2 * P], F32, c) for i in range(2)]
        gs = [[sb(f"s1{tag}_g{n}{i}", [P, KS, 2 * P], F32R, c) for n in ("hi", "lo")] for i in range(2)]
        psH = [ps(f"s1{tag}_psH{i}", [P, 2, 2 * P], F32, c) for i in range(NQ)]
        psY = [ps(f"s1{tag}_psY{i}", [P, D], F32, c) for i in range(2)]
        s = {n: sem(f"s1{tag}_{n}", c) for n in "up gelu g_hi g_lo down kept start counted count_out found".split()}
        if search:
            NB, NE, CAP, wmat, cur, ones = search
            ROUNDS, CANDS = 4, 3
            assert PAIRS * ROUNDS * 2 >= 31
            bits = sb("s1_bits", [P, CANDS, NE], I32, c)
            cand = sb("s1_cand", [P, CANDS, NE], I32, c)
            pass_ = sb("s1_pass", [P, CANDS, NE], F32, c)
            take = sb("s1_take", [P, NE], I32, c)
            over = sb("s1_over", [P, CANDS * NE, NB], F32, c)
            count = sb("s1_count", [P, CANDS * NE], F32, c)
            psC = ps("s1_psC", [P, CANDS, NE], F32, c)
        with nc.Block() as block:
            if scatter:
                @block.gpsimd
                def _(pool):
                    into, n_sb, xg, scattered, NB = scatter
                    for i in range(NB):
                        for n in range(2):
                            pool.indirect_dma_start(xg, bass.IndirectOffsetOnAxis(ap=into[n][:, i:i + 1], axis=0), n_sb[:, i, :], None)\
                                .then_inc(scattered, 16)

            @block.tensor
            def _(pe):
                def up(i, q):
                    at_least(pe, s["gelu"], (i - 1) * NQ + q + 1)
                    tiles = slice(first_tile + 2 * i, first_tile + 2 * i + 2)
                    for j in range(2):
                        t = 2 * q + j
                        for m, (a, (x, y)) in enumerate([(a, xy) for a in range(KD) for xy in PARTS3]):
                            ins = pe.matmul(psH[q][:, j, :], w1[x][:, a, t * P:(t + 1) * P],
                                            hT[y][:, a, tiles, :].rearrange("p b t -> p (b t)"), start=(m == 0), stop=(m == 3 * KD - 1))
                    ins.then_inc(s["up"], 1)

                def down(i, j):
                    pe.wait_ge(s["g_lo"], i * NQ + NQ)
                    at_least(pe, s["kept"], (i - 1) * 2 + j + 1)
                    for m, (t, (x, y)) in enumerate([(t, xy) for t in range(KS) for xy in PARTS3]):
                        ins = pe.matmul(psY[j][:], gs[i % 2][x][:, t, j * P:(j + 1) * P], w2[y][:, t, :], start=(m == 0), stop=(m == 3 * KS - 1))
                    ins.then_inc(s["down"], 1)

                def tally(i, r):
                    if search:
                        pe.wait_ge(s["counted"], i * ROUNDS + r + 1)
                        pe.matmul(psC[:].rearrange("p c e -> p (c e)"), ones[:], count[:], start=True, stop=True).then_inc(s["count_out"], 1)

                for q in range(NQ):
                    up(0, q)
                for i in range(PAIRS):
                    for q in range(NQ):
                        if i + 1 < PAIRS:
                            up(i + 1, q)
                        if q in (0, 2):
                            tally(i, q // 2)
                    down(i, 0)
                    tally(i, 2)
                    down(i, 1)
                    tally(i, 3)

            @block.scalar
            def _(act):
                def gelu(i, q):
                    act.wait_ge(s["up"], i * NQ + q + 1)
                    at_least(act, s["g_lo"], i * NQ + q - 1)
                    at_least(act, s["down"], (i - 1) * 2)
                    for j in range(2):
                        t = 2 * q + j
                        ins = act.activation(g[q % 2][:, j, :], psH[q][:, j, :], ACT.Gelu, bias=b1[:, t:t + 1])
                    ins.then_inc(s["gelu"], 1)
                    act.wait_ge(s["gelu"], i * NQ + q + 1)
                    act.activation(gs[i % 2][0][:, 2 * q:2 * q + 2, :], g[q % 2][:], ACT.Copy).then_inc(s["g_hi"], 1)

                def keep(i, j):
                    act.wait_ge(s["down"], i * 2 + j + 1)
                    act.activation(sh[:, first_tile + 2 * i + j, :], psY[j][:], ACT.Copy, scale=gates[:, 3:4]).then_inc(s["kept"], 1)

                for i in range(PAIRS + 1):
                    for q in range(NQ):
                        if i < PAIRS:
                            gelu(i, q)
                        if i > 0 and q == 1:
                            keep(i - 1, 0)
                    if i > 0:
                        keep(i - 1, 1)

            @block.vector
            def _(dve):
                def split(i, q):
                    dve.wait_ge(s["g_hi"], i * NQ + q + 1)
                    dve.tensor_tensor(gs[i % 2][1][:, 2 * q:2 * q + 2, :], g[q % 2][:], gs[i % 2][0][:, 2 * q:2 * q + 2, :].bitcast(F32),
                                      ALU.subtract).then_inc(s["g_lo"], 1)

                STEPS = 5

                def count_over(i, r):
                    if not search:
                        return
                    k = Steps(dve, s["found"], (i * ROUNDS + r) * STEPS)
                    k.step(dve.tensor_tensor(over[:].rearrange("p (c e) b -> p c b e", e=NE),
                                             wmat[:].unsqueeze(1).to_broadcast([P, CANDS, NB, NE]),
                                             cand[:].bitcast(F32).unsqueeze(2).to_broadcast([P, CANDS, NB, NE]), ALU.is_ge))
                    dve.tensor_reduce(count[:], over[:], AX.X, ALU.add).then_inc(s["counted"], 1)

                def raise_bar(i, r):
                    if not search:
                        return
                    k = Steps(dve, s["found"], (i * ROUNDS + r) * STEPS + 1)
                    dve.wait_ge(s["count_out"], i * ROUNDS + r + 1)
                    k.step(dve.scalar_tensor_tensor(out=pass_[:], in0=psC[:], scalar=float(CAP), in1=bits[:],
                                                    op0=ALU.is_ge, op1=ALU.mult))
                    dve.tensor_scalar(bits[:], bits[:], 2, None, ALU.logical_shift_right)
                    k.step(dve.tensor_reduce(take[:], pass_[:].rearrange("p c e -> p e c"), AX.X, ALU.max))
                    k.step(dve.tensor_tensor(cur[:], cur[:], take[:], ALU.bitwise_or))
                    k.step(dve.tensor_tensor(cand[:], bits[:], cur[:].unsqueeze(1).to_broadcast([P, CANDS, NE]), ALU.bitwise_or))
                    assert k.n == STEPS - 1

                if search:
                    k = Steps(dve, s["start"])
                    for n in range(CANDS):
                        ins = dve.memset(bits[:, n, :], (n + 1) << 29)
                    k.step(ins)
                    k.step(dve.tensor_copy(cand[:], bits[:]))
                for q in range(NQ):
                    split(0, q)
                for i in range(PAIRS):
                    more = i + 1 < PAIRS
                    count_over(i, 0)
                    raise_bar(i, 0)
                    if more:
                        split(i + 1, 0)
                    count_over(i, 1)
                    if more:
                        split(i + 1, 1)
                    raise_bar(i, 1)
                    if more:
                        split(i + 1, 2)
                    count_over(i, 2)
                    if more:
                        split(i + 1, 3)
                    raise_bar(i, 2)
                    count_over(i, 3)
                    raise_bar(i, 3)


def places(nc, sb, ps, sem, NB, NE, CAP, NSLOT, NTOK, wmat, cur, hots, ws, into, back, wk, ones, upper, gates):
    with ExitStack() as c:
        over = sb("p1_over", [P, NB, NE], F32, c)
        equal = sb("p1_equal", [P, NB, NE], F32, c)
        tmp = sb("p1_tmp", [P, NB, NE], F32, c)
        tot = sb("p1_tot", [P, NB, NE], F32, c)
        pre = [sb(f"p1_pre{i}", [P, NB, NE], F32, c) for i in range(2)]
        rank = sb("p1_rank", [P, NB, NE], F32, c)
        kept = sb("p1_kept", [P, NB, NE], F32, c)
        nover = sb("p1_nover", [P, NE], F32, c)
        room = sb("p1_room", [P, NE], F32, c)
        first_i = sb("p1_first_i", [P, NE], I32, c)
        first = sb("p1_first", [P, NE], F32, c)
        token_i = sb("p1_token_i", [P, NB], I32, c)
        token = sb("p1_token", [P, NB], F32, c)
        at, has, lost = (sb(f"p1_{n}", [P, NB], F32, c) for n in ("at", "has", "lost"))
        psR = ps("p1_ps", [P, 3, NB * NE], F32, c)
        psK = ps("p1_psK", [P, 2, NB * NE], F32, c)
        s = {n: sem(f"p1_{n}", c) for n in "steps iota_done marked ranked kept_done ranked2".split()}
        flat = lambda t: t[:].rearrange("p b e -> p (b e)")
        three = lambda t: t.rearrange("p (b e) -> p b e", e=NE)
        wide = lambda a: a.unsqueeze(1).to_broadcast([P, NB, NE])
        with nc.Block() as block:
            @block.gpsimd
            def _(pool):
                pool.iota(first_i[:], pattern=[[CAP, NE]], base=0, channel_multiplier=0).then_inc(s["iota_done"], 1)
                pool.iota(token_i[:], pattern=[[P, NB]], base=NSLOT, channel_multiplier=1).then_inc(s["iota_done"], 1)

            @block.tensor
            def _(pe):
                pe.wait_ge(s["marked"], 1)
                pe.matmul(psR[:, 0, :], upper[:], flat(equal), start=True, stop=True)
                pe.matmul(psR[:, 1, :], ones[:], flat(equal), start=True, stop=True)
                pe.matmul(psR[:, 2, :], ones[:], flat(over), start=True, stop=True).then_inc(s["ranked"], 1)
                pe.wait_ge(s["kept_done"], 1)
                pe.matmul(psK[:, 0, :], upper[:], flat(kept), start=True, stop=True)
                pe.matmul(psK[:, 1, :], ones[:], flat(kept), start=True, stop=True).then_inc(s["ranked2"], 1)

            @block.vector
            def _(dve):
                k = Steps(dve, s["steps"])
                bar = cur[:].bitcast(F32)
                dve.tensor_tensor(over[:], wmat[:], wide(bar), ALU.is_gt)
                k.step(dve.tensor_tensor(tmp[:], wmat[:], wide(bar), ALU.is_equal))
                dve.scalar_tensor_tensor(out=equal[:], in0=wmat[:], scalar=0.0, in1=tmp[:], op0=ALU.is_gt, op1=ALU.mult)\
                   .then_inc(s["marked"], 1)
                dve.wait_ge(s["iota_done"], 2)
                dve.tensor_copy(first[:], first_i[:])
                k.step(dve.tensor_copy(token[:], token_i[:]))

                def before(psX):
                    k.step(dve.tensor_copy(tot[:], three(psX[:, 1, :])))
                    incl = prefix_steps(dve, k, tot, pre, NB)
                    k.step(dve.tensor_tensor(rank[:], three(psX[:, 0, :]), incl[:], ALU.add))
                    k.step(dve.tensor_tensor(rank[:], rank[:], tot[:], ALU.subtract))

                dve.wait_ge(s["ranked"], 1)
                before(psR)
                k.step(dve.tensor_reduce(nover[:], psR[:, 2, :].rearrange("p (b e) -> p e b", e=NE), AX.X, ALU.add))
                k.step(dve.tensor_scalar(room[:], nover[:], -1.0, float(CAP), ALU.mult, ALU.add))
                k.step(dve.tensor_tensor(rank[:], rank[:], wide(room[:]), ALU.is_lt))
                k.step(dve.tensor_tensor(rank[:], rank[:], equal[:], ALU.mult))
                k.step(dve.tensor_tensor(kept[:], rank[:], over[:], ALU.add))
                dve.tensor_copy(tmp[:], kept[:]).then_inc(s["kept_done"], 1)
                dve.wait_ge(s["ranked2"], 1)
                before(psK)
                k.step(dve.tensor_tensor(rank[:], rank[:], wide(first[:]), ALU.add))
                k.step(dve.tensor_tensor(rank[:], rank[:], kept[:], ALU.mult))
                for n in range(2):
                    k.step(dve.tensor_tensor(tmp[:], hots[n][:], rank[:], ALU.mult))
                    k.step(dve.tensor_reduce(at[:], tmp[:], AX.X, ALU.add))
                    k.step(dve.tensor_tensor(tmp[:], hots[n][:], kept[:], ALU.mult))
                    k.step(dve.tensor_reduce(has[:], tmp[:], AX.X, ALU.add))
                    k.step(dve.tensor_scalar(lost[:], has[:], -1.0, 1.0, ALU.mult, ALU.add))
                    k.step(dve.scalar_tensor_tensor(out=back[n][:], in0=lost[:], scalar=float(NSLOT), in1=at[:],
                                                    op0=ALU.mult, op1=ALU.add))
                    k.step(dve.scalar_tensor_tensor(out=lost[:], in0=token[:], scalar=float(n * NTOK), in1=lost[:],
                                                    op0=ALU.add, op1=ALU.mult))
                    k.step(dve.tensor_tensor(into[n][:], lost[:], at[:], ALU.add))
                    k.step(dve.tensor_tensor(wk[n][:], ws[n][:], has[:], ALU.mult))
                    k.step(dve.tensor_scalar(wk[n][:], wk[n][:], gates[:, 3:4], None, ALU.mult))


def experts_gelu(nc, A, sb, ps, sem, NB, NE, CAP, D, KD, F, x_sb, sh, b2s, ident, xg, yg, n_sb, back, wk, scattered):
    KF, NT, HALF = F // P, CAP // P, CAP // 2
    assert CAP % P == 0 and HALF <= 512 and KD * F == KF * D
    with ExitStack() as c:
        raw = [sb(f"x1_raw{i}", [P, 2, KD * F], F32, c) for i in range(2)]
        w1 = [[sb(f"x1_w1{n}{i}", [P, KD, F], F32R, c) for n in ("hi", "lo")] for i in range(2)]
        w2 = [[sb(f"x1_w2{n}{i}", [P, KF, D], F32R, c) for n in ("hi", "lo")] for i in range(2)]
        b1 = sb("x1_b1", [P, NE, KF], F32, c)
        b1e = [sb(f"x1_b1e{i}", [P, KF], F32, c) for i in range(2)]
        b2 = sb("x1_b2", [P, NE, D], F32, c)
        xin = [sb(f"x1_xin{i}", [P, NT, D], F32, c) for i in range(2)]
        xT = [sb(f"x1_xT{n}", [P, KD, CAP], F32R, c) for n in ("hi", "lo")]
        g = sb("x1_g", [P, KF, CAP], F32, c)
        gs = [sb(f"x1_g{n}", [P, KF, CAP], F32R, c) for n in ("hi", "lo")]
        y = [sb(f"x1_y{i}", [P, D], F32, c) for i in range(2)]
        psX = [ps(f"x1_psX{i}", [P, KD, P], F32, c) for i in range(2)]
        psH = [ps(f"x1_psH{i}", [P, HALF], F32, c) for i in range(4)]
        psY = [ps(f"x1_psY{i}", [P, D], F32, c) for i in range(2)]
        names = ("w_in0 w_in1 b_in x_in0 x_in1 turned xt_hi xt_lo w_hi w_lo up gelu g_hi g_lo down y_done y_out0 y_out1 "
                 "x_gated x_biased combined").split()
        s = {n: sem(f"x1_{n}", c) for n in names}
        w_in, x_in, y_out = [s["w_in0"], s["w_in1"]], [s["x_in0"], s["x_in1"]], [s["y_out0"], s["y_out1"]]
        xg_t = xg[0:NE * CAP].rearrange("(e t p) d -> e p t d", p=P, t=NT)
        yg_t = yg[0:NE * CAP].rearrange("(e t p) d -> e t p d", p=P, t=NT)
        NC = 2 * KF
        chunk = lambda m: (m % KF, m // KF)
        gathered = [[sem(f"x1_gathered{n}_{i}", c) for i in range(NB)] for n in range(2)]

        flat = lambda t: t.rearrange("p a n -> p (a n)")
        parts_of = lambda b: ((w1[b], raw[b][:, 0, :]), (w2[b], raw[b][:, 1, :]))

        with nc.Block() as block:
            @block.sync
            def _(sp):
                def load_w(e, b):
                    sp.dma_start(raw[b][:, 0, :].rearrange("p (k f) -> p k f", k=KD), A["fc1_T"][e].rearrange("(k p) f -> p k f", p=P))\
                      .then_inc(w_in[b], 16)
                    sp.dma_start(raw[b][:, 1, :].rearrange("p (k d) -> p k d", k=KF), A["fc2_T"][e].rearrange("(k p) d -> p k d", p=P))\
                      .then_inc(w_in[b], 16)

                def load_x(e, b):
                    sp.dma_start(xin[b][:], xg_t[e]).then_inc(x_in[b], 16)

                load_w(0, 0)
                load_w(1, 1)
                with nc.allow_non_contiguous_dma(reason="a few thousand small parameters"):
                    sp.dma_start(b1[:], A["L1_ffn_fc1_b"].rearrange("e (k p) -> p e k", p=P)).then_inc(s["b_in"], 16)
                    sp.dma_start(b2[:], A["L1_ffn_fc2_b"].partition_broadcast(P)).then_inc(s["b_in"], 16)
                sp.wait_ge(scattered, 2 * NB * 16)
                load_x(0, 0)
                load_x(1, 1)

                def stores(e):
                    for t in range(NT):
                        b = (e_par * NT + t) % 2
                        sp.wait_ge(s["y_done"], e * NT + t + 1)
                        sp.dma_start(yg_t[e, t], y[b][:]).then_inc(y_out[b], 16)

                with sp.Fori(0, NE // 2 - 1) as i:
                    for e_par in range(2):
                        sp.wait_ge(s["w_lo"], i * 2 + e_par + 1)
                        load_w(i * 2 + e_par + 2, e_par)
                        sp.wait_ge(s["turned"], (i * 2 + e_par + 1) * NT)
                        load_x(i * 2 + e_par + 2, e_par)
                        stores(i * 2 + e_par)
                for e_par in range(2):
                    stores(NE - 2 + e_par)

            @block.tensor
            def _(pe):
                def turn(e, b, pair, t):
                    if t == 0:
                        pe.wait_ge(x_in[b], pair * 16 + 16)
                    at_least(pe, s["xt_lo"], e * NT + t - 1)
                    for a in range(KD):
                        ins = pe.transpose(psX[(b * NT + t) % 2][:, a, :], xin[b][:, t, a * P:(a + 1) * P], ident[:])
                    ins.then_inc(s["turned"], 1)

                def up(e, b):
                    pe.wait_ge(s["w_lo"], e + 1)
                    pe.wait_ge(s["xt_lo"], e * NT + NT)
                    for m in range(NC):
                        f, half = chunk(m)
                        at_least(pe, s["gelu"], e * NC + m - 3)
                        rows = slice(half * HALF, (half + 1) * HALF)
                        for n, (a, (x, y_)) in enumerate([(a, xy) for a in range(KD) for xy in PARTS3]):
                            ins = pe.matmul(psH[m % 4][:], w1[b][x][:, a, f * P:(f + 1) * P], xT[y_][:, a, rows],
                                            start=(n == 0), stop=(n == 3 * KD - 1))
                        ins.then_inc(s["up"], 1)

                def down(e, b, t):
                    if t == 0:
                        pe.wait_ge(s["g_lo"], e * NC + KF)
                    if t == HALF // P:
                        pe.wait_ge(s["g_lo"], e * NC + NC)
                    at_least(pe, s["y_done"], e * NT + t - 1)
                    for n, (f, (x, y_)) in enumerate([(f, xy) for f in range(KF) for xy in PARTS3]):
                        ins = pe.matmul(psY[(b * NT + t) % 2][:], gs[x][:, f, t * P:(t + 1) * P], w2[b][y_][:, f, :],
                                        start=(n == 0), stop=(n == 3 * KF - 1))
                    ins.then_inc(s["down"], 1)

                def expert(e, b, pair, more=True):
                    up(e, b)
                    for t in range(NT):
                        if more:
                            turn(e + 1, 1 - b, pair + b, t)
                        down(e, b, t)

                for t in range(NT):
                    turn(0, 0, 0, t)
                expert(0, 0, 0)
                expert(1, 1, 0)
                with pe.Fori(1, NE // 2 - 1) as i:
                    for b in range(2):
                        expert(i * 2 + b, b, i)
                expert(NE - 2, 0, NE // 2 - 1)
                expert(NE - 1, 1, NE // 2 - 1, more=False)

            @block.scalar
            def _(act):
                def weights(e, b, pair):
                    act.wait_ge(w_in[b], pair * 32 + 32)
                    at_least(act, s["down"], (e - 1) * NT)
                    at_least(act, s["gelu"], (e - 1) * NC)
                    act.activation(b1e[b][:], b1[:, e, :], ACT.Copy)
                    for w, r in parts_of(b):
                        act.activation(flat(w[0][:]), r, ACT.Copy).then_inc(s["w_hi"], 1)

                def turn(e, b):
                    at_least(act, s["up"], e * NC)
                    for t in range(NT):
                        act.wait_ge(s["turned"], e * NT + t + 1)
                        act.activation(xT[0][:, :, t * P:(t + 1) * P], psX[(b * NT + t) % 2][:], ACT.Copy).then_inc(s["xt_hi"], 1)

                def gelu(e, b):
                    act.wait_ge(s["w_hi"], e * 2 + 2)
                    for m in range(NC):
                        f, half = chunk(m)
                        act.wait_ge(s["up"], e * NC + m + 1)
                        at_least(act, s["g_lo"], e * NC + m - NC + 1)
                        act.activation(g[:, f, half * HALF:(half + 1) * HALF], psH[m % 4][:], ACT.Gelu, bias=b1e[b][:, f:f + 1])\
                           .then_inc(s["gelu"], 1)

                def expert(e, b, pair, more=True):
                    gelu(e, b)
                    if more:
                        turn(e + 1, 1 - b)
                        if not (isinstance(e, int) and e == NE - 2):
                            weights(e + 2, b, pair + 1)

                act.wait_ge(s["b_in"], 32)
                weights(0, 0, 0)
                weights(1, 1, 0)
                turn(0, 0)
                expert(0, 0, 0)
                expert(1, 1, 0)
                with act.Fori(1, NE // 2 - 1) as i:
                    for b in range(2):
                        expert(i * 2 + b, b, i)
                expert(NE - 2, 0, NE // 2 - 1)
                expert(NE - 1, 1, NE // 2 - 1, more=False)

            @block.gpsimd
            def _(pool):
                def weights(e, b):
                    for n, (w, r) in enumerate(parts_of(b)):
                        pool.wait_ge(s["w_hi"], e * 2 + n + 1)
                        ins = pool.tensor_tensor(flat(w[1][:]), r, flat(w[0][:]).bitcast(F32), ALU.subtract)
                    ins.then_inc(s["w_lo"], 1)

                def residual(i):
                    pool.tensor_tensor(x_sb[:, i, :], x_sb[:, i, :], b2s[:], ALU.add).then_inc(s["x_biased"], 1)
                    pool.wait_ge(s["x_biased"], i + 1)
                    pool.tensor_tensor(x_sb[:, i, :], x_sb[:, i, :], sh[:, i, :], ALU.add).then_inc(s["x_gated"], 1)

                with pool.Fori(0, NE // 2) as i:
                    for b in range(2):
                        weights(i * 2 + b, b)
                        for n in range(NB // NE):
                            residual((i * 2 + b) * (NB // NE) + n)
                for b in range(2):
                    pool.wait_ge(y_out[b], NE * NT // 2 * 16)
                pool.wait_ge(s["x_gated"], NB)
                for i in range(NB):
                    for n, dst in enumerate((n_sb, sh)):
                        pool.indirect_dma_start(dst[:, i, :], None, yg, bass.IndirectOffsetOnAxis(ap=back[n][:, i:i + 1], axis=0))\
                            .then_inc(gathered[n][i], 16)

            @block.vector
            def _(dve):
                def turn(e, b, t):
                    at_least(dve, s["up"], e * NC)
                    cols = slice(t * P, (t + 1) * P)
                    dve.wait_ge(s["xt_hi"], e * NT + t + 1)
                    dve.tensor_tensor(xT[1][:, :, cols], psX[(b * NT + t) % 2][:], xT[0][:, :, cols].bitcast(F32), ALU.subtract)\
                       .then_inc(s["xt_lo"], 1)

                def split(e, b):
                    at_least(dve, s["down"], e * NT)
                    for m in range(NC):
                        f, half = chunk(m)
                        rows = slice(half * HALF, (half + 1) * HALF)
                        dve.wait_ge(s["gelu"], e * NC + m + 1)
                        dve.tensor_copy(gs[0][:, f, rows], g[:, f, rows]).then_inc(s["g_hi"], 1)
                        dve.wait_ge(s["g_hi"], e * NC + m + 1)
                        dve.tensor_tensor(gs[1][:, f, rows], g[:, f, rows], gs[0][:, f, rows].bitcast(F32), ALU.subtract)\
                           .then_inc(s["g_lo"], 1)

                def out(e, b, pair, t):
                    yb = (b * NT + t) % 2
                    dve.wait_ge(s["down"], e * NT + t + 1)
                    at_least(dve, y_out[yb], (pair * NT + (b * NT + t) // 2) * 16)
                    dve.tensor_tensor(y[yb][:], psY[yb][:], b2[:, e, :], ALU.add).then_inc(s["y_done"], 1)

                def expert(e, b, pair, more=True):
                    split(e, b)
                    for t in range(NT):
                        if more:
                            turn(e + 1, 1 - b, t)
                        out(e, b, pair, t)

                dve.wait_ge(s["b_in"], 32)
                for t in range(NT):
                    turn(0, 0, t)
                expert(0, 0, 0)
                expert(1, 1, 0)
                with dve.Fori(1, NE // 2 - 1) as i:
                    for b in range(2):
                        expert(i * 2 + b, b, i)
                expert(NE - 2, 0, NE // 2 - 1)
                expert(NE - 1, 1, NE // 2 - 1, more=False)
                for i in range(NB):
                    for n, src in enumerate((n_sb, sh)):
                        dve.wait_ge(gathered[n][i], 16)
                        dve.wait_ge(s["x_gated"], i + 1)
                        ins = dve.scalar_tensor_tensor(out=x_sb[:, i, :], in0=src[:, i, :], scalar=wk[n][:, i:i + 1],
                                                       in1=x_sb[:, i, :], op0=ALU.mult, op1=ALU.add)
                        ins.then_inc(s["combined"], 1)
                        dve.wait_ge(s["combined"], i * 2 + n + 1)


def laid_out(inputs):
    import numpy as np

    a = {k: np.ascontiguousarray(v) for k, v in inputs.items()}
    a["router_T"] = np.ascontiguousarray(a["L0_ffn_router_w"].T)
    a["proj_T"] = np.ascontiguousarray(a["L1_ffn_proj_w"].T)
    a["sh1_T"] = np.ascontiguousarray(a["L1_ffn_sh1_w"].T)
    a["sh2_T"] = np.ascontiguousarray(a["L1_ffn_sh2_w"].T)
    a["fc1_T"] = np.ascontiguousarray(a["L1_ffn_fc1_w"].transpose(0, 2, 1))
    a["fc2_T"] = np.ascontiguousarray(a["L1_ffn_fc2_w"].transpose(0, 2, 1))
    for k in ("L0_ffn_router_w", "L1_ffn_proj_w", "L1_ffn_sh1_w", "L1_ffn_sh2_w", "L1_ffn_fc1_w", "L1_ffn_fc2_w"):
        del a[k]
    return a


def kernel(**inputs):
    import concourse.bacc as bacc
    from concourse.bass_utils import run_bass_kernel_spmd

    nc = bacc.Bacc("TRN2", target_bir_lowering=False, num_devices=1)
    arrays = {f"in_{k}": v for k, v in laid_out(inputs).items()}
    A = {k[3:]: nc.dram_tensor(k, v.shape, mybir.dt.from_np(v.dtype), kind="ExternalInput").ap() for k, v in arrays.items()}
    out = nc.dram_tensor("out", arrays["in_x"].shape, F32, kind="ExternalOutput").ap()
    program(nc, A, out)
    return run_bass_kernel_spmd(nc, [arrays], core_ids=[0]).results[0]["out"]
```

```python
from contextlib import ExitStack

import concourse.bass as bass
from concourse import mybir

F32 = mybir.dt.float32
F32R = mybir.dt.float32r
BF16 = mybir.dt.bfloat16
I32 = mybir.dt.int32
U32 = mybir.dt.uint32
ALU = mybir.AluOpType
ACT = mybir.ActivationFunctionType
AX = mybir.AxisListType

P = 128
LN_EPS = 1e-5


PARTS3 = ((0, 0), (0, 1), (1, 0))


def at_least(eng, sem, value):
    if isinstance(value, int) and value <= 0:
        return
    eng.wait_ge(sem, value)


def recycle(nc):
    used = sorted(x for x in nc.released_uncleared_semaphores)
    with nc.Block() as block:
        @block.gpsimd
        def _(pool):
            start = 0
            for n in range(1, len(used) + 1):
                if n == len(used) or used[n] != used[n - 1] + 1:
                    pool.sem_clear(range(used[start], used[n - 1] + 1))
                    start = n


class Steps:

    def __init__(self, eng, sem, base=0):
        self.eng, self.sem, self.base, self.n = eng, sem, base, 0

    def step(self, ins):
        ins.then_inc(self.sem, 1)
        self.n += 1
        self.eng.wait_ge(self.sem, self.base + self.n)


def rsqrt_steps(dve, s, y, v, a, b):
    vi, ai = v.bitcast(I32), a.bitcast(I32)
    s.step(dve.tensor_scalar(ai, vi, 1, None, ALU.logical_shift_right))
    s.step(dve.tensor_scalar(y.bitcast(I32), ai, -1.0, float(0x5F3759DF), ALU.mult, ALU.add))
    for _ in range(4):
        s.step(dve.tensor_tensor(a, y, y, ALU.mult))
        s.step(dve.tensor_tensor(b, a, v, ALU.mult))
        s.step(dve.tensor_scalar(a, b, -0.5, 1.5, ALU.mult, ALU.add))
        s.step(dve.tensor_tensor(y, y, a, ALU.mult))


def norm_steps(dve, s, stats, mean, rstd, tmp, twice):
    a, b, v = tmp
    s.step(dve.tensor_tensor(mean, stats[:, :, 1], stats[:, :, 4], ALU.add))
    s.step(dve.tensor_scalar(mean, mean, 0.5, None, ALU.mult))
    s.step(dve.tensor_tensor(a, stats[:, :, 1], stats[:, :, 4], ALU.subtract))
    s.step(dve.scalar_tensor_tensor(out=b, in0=a, scalar=0.25, in1=a, op0=ALU.mult, op1=ALU.mult))
    s.step(dve.tensor_tensor(a, stats[:, :, 2], stats[:, :, 5], ALU.add))
    s.step(dve.scalar_tensor_tensor(out=v, in0=a, scalar=1.0 / 256, in1=b, op0=ALU.mult, op1=ALU.add))
    s.step(dve.tensor_scalar(a, v, LN_EPS, None, ALU.add))
    if not twice:
        s.step(dve.tensor_copy(v, a))
        rsqrt_steps(dve, s, rstd, v, a, b)
        return
    s.step(dve.scalar_tensor_tensor(out=v, in0=a, scalar=LN_EPS, in1=v, op0=ALU.mult, op1=ALU.add))
    rsqrt_steps(dve, s, rstd, v, a, b)


def program(nc, A, out):
    NB, S, D = A["x"].shape
    assert S == P and D == 256
    KD = D // P
    ctx = ExitStack()

    def sb(name, shape, dt=F32, where=ctx, side="left"):
        return where.enter_context(nc.sbuf_tensor(name, shape, dt, side=side))

    def ps(name, shape, dt=F32, where=ctx):
        return where.enter_context(nc.psum_tensor(name, shape, dt))

    def sem(name, where=ctx):
        return where.enter_context(nc.semaphore(name))

    with ctx:
        x_sb = sb("x_sb", [P, NB, D])
        ctx_sb = sb("ctx_sb", [P, NB, D])
        ident = sb("ident", [P, P])
        gates = sb("gates", [P, 4])
        x_mean, x_rstd = sb("x_mean", [P, NB]), sb("x_rstd", [P, NB])
        c_mean, c_rstd = sb("c_mean", [P, NB]), sb("c_rstd", [P, NB])
        x_stats, c_stats = sb("x_stats", [P, NB, 6]), sb("c_stats", [P, NB, 6])
        nt = [sb(f"norm_tmp{i}", [P, NB]) for i in range(3)]
        g = dict(nc=nc, A=A, sb=sb, ps=ps, sem=sem, NB=NB, D=D, KD=KD, x_sb=x_sb, ctx_sb=ctx_sb, ident=ident,
                 gates=gates, x_mean=x_mean, x_rstd=x_rstd, c_mean=c_mean, c_rstd=c_rstd,
                 x_stats=x_stats, c_stats=c_stats, nt=nt)
        attention_0(**g)
        with ExitStack() as over:
            begun = mixture_0(**g, over=over)
            ahead = attention_1(**g, over=over, begun=begun)
        recycle(nc)
        mixture_1(**g, out=out, ahead=ahead)
        ahead["over"].close()


def attention_0(nc, A, sb, ps, sem, NB, D, KD, x_sb, ctx_sb, ident, gates, x_mean, x_rstd, c_mean, c_rstd,
                x_stats, c_stats, nt):
    NH = 16
    HD = D // NH
    NG = 4
    with ExitStack() as c:
        W = {n: sb(f"a0_w{n}", [P, KD, D], F32, c) for n in "qkvo"}
        bq, bk = sb("a0_bq", [P, KD], F32, c), sb("a0_bk", [P, KD], F32, c)
        bv, bo = sb("a0_bv", [P, D], F32, c), sb("a0_bo", [P, D], F32, c)
        pidx = sb("a0_pidx", [P, 1], I32, c)
        mask = sb("a0_mask", [P, 2], F32, c)
        cst = sb("a0_cst", [P, D], F32, c)
        xn = sb("a0_xn", [P, D], F32, c)
        xcT = sb("a0_xcT", [P, 4, P], F32, c)
        q = [sb(f"a0_q{n}", [P, 2, P], F32R, c) for n in ("hi", "lo")]
        kT = sb("a0_kT", [P, 2, P], F32, c)
        km = [sb(f"a0_km{n}", [P, 2, 2, P], F32R, c) for n in ("hi", "lo")]
        v = sb("a0_v", [P, NB, D], F32, c)
        nmax = sb("a0_nmax", [P, NH], F32, c)
        probs = sb("a0_probs", [P, NH, P], F32, c)
        sums, rsum = sb("a0_sums", [P, NH], F32, c), sb("a0_rsum", [P, NH], F32, c)
        pT = sb("a0_pT", [P, NH, P], F32, c)
        vpad = sb("a0_vpad", [P, NH, P], F32, c)
        oT = sb("a0_oT", [P, 2, P], F32, c)
        psS = [ps(f"a0_psS{j}", [P, NG, P], F32, c) for j in range(NG)]
        psT = [ps(f"a0_psT{j}", [P, NG, P], F32, c) for j in range(2)]
        psM0 = ps("a0_psM0", [P, 512], F32, c)
        psM1 = ps("a0_psM1", [P, 512], F32, c)
        names = ("x_in0 x_in1 x_in2 x_in3 c_in0 c_in1 w_in small_in gates_done dve_steps norm_steps ident_zero ident_done pidx_done "
                 "bo_done xn_done cst_done resid_done tx_done txc_done qk_done v_done q_hi q_lo km_hi km_lo kT_done vs_done "
                 "s_done max_done exp_done rsum_done p_done t_done tcA_done tcV_done vpad_zero vpad_done pv_done oTc_done y_done "
                 "x_done").split()
        s = {n: sem(f"a0_{n}", c) for n in names}
        XPARTS, CFIRST = 4, 4


        with nc.Block() as block:
            @block.sync
            def _(sp):
                part = NB // XPARTS
                for n in range(XPARTS):
                    sp.dma_start(x_sb[:, n * part:(n + 1) * part, :], A["x"][n * part:(n + 1) * part].rearrange("b p d -> p b d"))\
                      .then_inc(s[f"x_in{n}"], 16)
                for n, key in (("q", "Wq"), ("k", "Wk"), ("v", "Wv"), ("o", "Wo")):
                    sp.dma_start(W[n][:], A["L0_xattn_" + key].rearrange("(k p) n -> p k n", p=P)).then_inc(s["w_in"], 16)
                sp.dma_start(ctx_sb[:, 0:CFIRST, :], A["ctx_1024"][0:CFIRST].rearrange("b p d -> p b d")).then_inc(s["c_in0"], 16)
                sp.dma_start(ctx_sb[:, CFIRST:NB, :], A["ctx_1024"][CFIRST:NB].rearrange("b p d -> p b d")).then_inc(s["c_in1"], 16)

            @block.gpsimd
            def _(pool):
                pool.memset(ident[:], 0.0).then_inc(s["ident_zero"], 1)
                pool.iota(pidx[:], pattern=[[0, 1]], base=0, channel_multiplier=1).then_inc(s["pidx_done"], 1)
                pool.wait_ge(s["ident_zero"], 1)
                pool.affine_select(out=ident[:], in_=ident[:], compare_op=ALU.not_equal, fill=1.0, base=0,
                                   pattern=[[-1, P]], channel_multiplier=1).then_inc(s["ident_done"], 1)

                def stage_context(i, first):
                    if not first:
                        pool.wait_ge(s["tx_done"], i)
                    pool.tensor_copy(cst[:], ctx_sb[:, i, :]).then_inc(s["cst_done"], 1)

                def residual(i):
                    pool.wait_ge(s["xn_done"], i + 1)
                    pool.tensor_tensor(x_sb[:, i, :], x_sb[:, i, :], bo[:], ALU.add).then_inc(s["resid_done"], 1)

                def pad_values(i):
                    pool.wait_ge(s["vs_done"], i + 1)
                    at_least(pool, s["pv_done"], i)
                    for m in range(2):
                        own = vpad[:, 8 * m:8 * m + 8, :].rearrange("p h (g d) -> p (h g) d", d=HD)[:, 0::9, :]
                        ins = pool.tensor_copy(own, v[:, i, m * P:(m + 1) * P].rearrange("p (h d) -> p h d", d=HD))
                    ins.then_inc(s["vpad_done"], 1)

                pool.memset(vpad[:], 0.0).then_inc(s["vpad_zero"], 1)
                pool.wait_ge(s["c_in0"], 16)
                stage_context(0, True)
                pool.wait_ge(s["bo_done"], 1)
                pool.wait_ge(s["c_in1"], 16)
                pool.wait_ge(s["vpad_zero"], 1)
                stage_context(1, False)
                pad_values(0)
                residual(0)
                with pool.Fori(2, NB) as i:
                    stage_context(i, False)
                    pad_values(i - 1)
                    residual(i - 1)
                pad_values(NB - 1)
                residual(NB - 1)

            @block.scalar
            def _(act):
                for dst, src in ((bq[:], A["L0_xattn_bq"].rearrange("(k p) -> p k", p=P)),
                                 (bk[:], A["L0_xattn_bk"].rearrange("(k p) -> p k", p=P)),
                                 (bv[:], A["L0_xattn_bv"].partition_broadcast(P)),
                                 (bo[:], A["L0_xattn_bo"].partition_broadcast(P)),
                                 (gates[:, 0:2], A["g_xattn"].partition_broadcast(P)),
                                 (gates[:, 2:4], A["g_ffn"].partition_broadcast(P))):
                    with nc.allow_non_contiguous_dma(reason="a few hundred small parameters"):
                        act.dma_start(dst, src).then_inc(s["small_in"], 16)
                act.wait_ge(s["small_in"], 96)
                act.activation(gates[:], gates[:], ACT.Tanh).then_inc(s["gates_done"], 1)

                def front(i):
                    act.wait_ge(s["tx_done"], i + 1)
                    act.activation(xcT[:], psT[1][:], ACT.Copy).then_inc(s["txc_done"], 1)

                def copy(i, gr):
                    act.wait_ge(s["t_done"], i * 4 + gr + 1)
                    act.activation(pT[:, 4 * gr:4 * gr + 4, :], psT[0][:], ACT.Copy).then_inc(s["tcA_done"], 1)

                def project(i):
                    act.wait_ge(s["qk_done"], i + 1)
                    for m in range(2):
                        ins = act.activation(q[0][:, m, :], psM1[:, m * P:(m + 1) * P], ACT.Identity, bias=bq[:, m:m + 1])
                    ins.then_inc(s["q_hi"], 1)
                    at_least(act, s["km_lo"], i)
                    for m in range(2):
                        ins = act.activation(kT[:, m, :], psM1[:, (2 + m) * P:(3 + m) * P], ACT.Identity, bias=bk[:, m:m + 1])
                    ins.then_inc(s["kT_done"], 1)
                    act.wait_ge(s["kT_done"], i + 1)
                    for par in range(2):
                        ins = act.activation(km[0][:, :, par, :], kT[:], ACT.Copy, scale=mask[:, par:par + 1])
                    ins.then_inc(s["km_hi"], 1)

                def exps(i, j):
                    act.wait_ge(s["max_done"], i * 4 + j + 1)
                    for slot in range(NG):
                        n = 4 * j + slot
                        act.activation(probs[:, n, :], psS[j][:, slot, :], ACT.Exp, bias=nmax[:, n:n + 1],
                                       accum_out=sums[:, n:n + 1]).then_inc(s["exp_done"], 1)

                def heads_out(i):
                    act.wait_ge(s["pv_done"], i + 1)
                    act.activation(oT[:], psM0[:, D:2 * D].rearrange("p (a t) -> p a t", a=2), ACT.Copy).then_inc(s["oTc_done"], 1)

                def tile(i, first=False, last=False):
                    exps(i, 0)
                    if not last:
                        front(i + 1)
                    for j in range(1, 4):
                        exps(i, j)
                    if not first:
                        heads_out(i - 1)
                    copy(i, 0)
                    if not last:
                        project(i + 1)
                    copy(i, 2)

                front(0)
                project(0)
                tile(0, first=True)
                with act.Fori(1, NB - 1) as i:
                    tile(i)
                tile(NB - 1, last=True)
                heads_out(NB - 1)

            @block.vector
            def _(dve):
                k = Steps(dve, s["dve_steps"])
                dve.wait_ge(s["pidx_done"], 1)
                k.step(dve.tensor_scalar(pidx[:], pidx[:], 16, None, ALU.bitwise_and))
                k.step(dve.tensor_scalar(mask[:, 1:2], pidx[:], 1.0 / 64, None, ALU.mult))
                k.step(dve.tensor_scalar(mask[:, 0:1], mask[:, 1:2], -1.0, 0.25, ALU.mult, ALU.add))
                for n in range(XPARTS):
                    dve.wait_ge(s[f"x_in{n}"], 16)
                    for j in range(n * NB // XPARTS, (n + 1) * NB // XPARTS):
                        ins = dve.bn_stats(x_stats[:, j, :], x_sb[:, j, :])
                k.step(ins)
                norm_steps(dve, k, x_stats, x_mean[:], x_rstd[:], [t[:] for t in nt], False)
                dve.wait_ge(s["gates_done"], 1)
                dve.tensor_scalar(bo[:], bo[:], gates[:, 0:1], None, ALU.mult).then_inc(s["bo_done"], 1)

                def normed(i):
                    at_least(dve, s["tx_done"], i)
                    at = slice(i, i + 1) if isinstance(i, int) else bass.ds(i, 1)
                    dve.tensor_scalar(xn[:], x_sb[:, i, :], x_mean[:, at], x_rstd[:, at],
                                      ALU.subtract, ALU.mult).then_inc(s["xn_done"], 1)

                def copy(i, gr):
                    dve.wait_ge(s["t_done"], i * 4 + gr + 1)
                    dve.tensor_copy(pT[:, 4 * gr:4 * gr + 4, :], psT[1][:]).then_inc(s["tcV_done"], 1)

                def queries(i):
                    dve.wait_ge(s["kT_done"], i + 1)
                    for m in range(2):
                        ins = dve.scalar_tensor_tensor(out=q[1][:, m, :], in0=psM1[:, m * P:(m + 1) * P], scalar=bq[:, m:m + 1],
                                                       in1=q[0][:, m, :].bitcast(F32), op0=ALU.add, op1=ALU.subtract)
                    ins.then_inc(s["q_lo"], 1)

                def keys(i):
                    dve.wait_ge(s["km_hi"], i + 1)
                    for par in range(2):
                        ins = dve.scalar_tensor_tensor(out=km[1][:, :, par, :], in0=kT[:], scalar=mask[:, par:par + 1],
                                                       in1=km[0][:, :, par, :].bitcast(F32), op0=ALU.mult, op1=ALU.subtract)
                    ins.then_inc(s["km_lo"], 1)

                def values(i):
                    dve.wait_ge(s["v_done"], i + 1)
                    dve.tensor_tensor(v[:, i, :], psM0[:, 0:D], bv[:], ALU.add).then_inc(s["vs_done"], 1)

                def normalize(i, j):
                    dve.wait_ge(s["exp_done"], i * 16 + 4 * j + 4)
                    own = slice(4 * j, 4 * j + 4)
                    dve.reciprocal(rsum[:, own], sums[:, own]).then_inc(s["rsum_done"], 1)
                    dve.wait_ge(s["rsum_done"], i * 4 + j + 1)
                    dve.tensor_tensor(probs[:, own, :], probs[:, own, :], rsum[:, own].unsqueeze(2).to_broadcast([P, NG, P]),
                                      ALU.mult).then_inc(s["p_done"], 1)

                def maximum(i, j):
                    dve.wait_ge(s["s_done"], i * 4 + j + 1)
                    dve.tensor_reduce(nmax[:, 4 * j:4 * j + 4], psS[j][:], AX.X, ALU.max, negate=True)\
                       .then_inc(s["max_done"], 1)

                def residual(i):
                    dve.wait_ge(s["y_done"], i + 1)
                    dve.wait_ge(s["resid_done"], i + 1)
                    dve.scalar_tensor_tensor(out=x_sb[:, i, :], in0=psM0[:, D:2 * D], scalar=gates[:, 0:1],
                                             in1=x_sb[:, i, :], op0=ALU.mult, op1=ALU.add).then_inc(s["x_done"], 1)

                def statistics(i):
                    dve.wait_ge(s["x_done"], i + 1)
                    dve.bn_stats(x_stats[:, i, :], x_sb[:, i, :])

                def tile(i, first=False, ahead=2):
                    for j in range(4):
                        maximum(i, j)
                    normalize(i, 0)
                    if ahead > 1:
                        normed(i + 2)
                    for j in range(1, 4):
                        normalize(i, j)
                    copy(i, 1)
                    if ahead > 0:
                        queries(i + 1)
                        values(i + 1)
                        keys(i + 1)
                    copy(i, 3)
                    dve.bn_stats(c_stats[:, i, :], ctx_sb[:, i, :])
                    if not first:
                        residual(i - 1)
                        statistics(i - 1)

                normed(0)
                normed(1)
                queries(0)
                values(0)
                keys(0)
                tile(0, first=True)
                with dve.Fori(1, NB - 2) as i:
                    tile(i)
                tile(NB - 2, ahead=1)
                tile(NB - 1, ahead=0)
                k = Steps(dve, s["norm_steps"])
                k.step(dve.tensor_copy(c_mean[:], c_stats[:, :, 1]))
                norm_steps(dve, k, c_stats, c_mean[:], c_rstd[:], [t[:] for t in nt], False)
                residual(NB - 1)
                statistics(NB - 1)

            @block.tensor
            def _(pe):
                def turn_in(i):
                    pe.wait_ge(s["xn_done"], i + 1)
                    pe.wait_ge(s["cst_done"], i + 1)
                    at_least(pe, s["tcV_done"], (i - 1) * 2)
                    for a in range(KD):
                        pe.transpose(psT[1][:, a, :], xn[:, a * P:(a + 1) * P], ident[:])
                    for a in range(KD):
                        ins = pe.transpose(psT[1][:, 2 + a, :], cst[:, a * P:(a + 1) * P], ident[:])
                    ins.then_inc(s["tx_done"], 1)

                def turn_probs(i, gr):
                    pe.wait_ge(s["p_done"], i * 4 + gr + 1)
                    if gr == 2:
                        pe.wait_ge(s["tcA_done"], i * 2 + 1)
                    if gr == 3:
                        pe.wait_ge(s["tcV_done"], i * 2 + 1)
                    for h in range(4):
                        ins = pe.transpose(psT[gr % 2][:, h, :], probs[:, 4 * gr + h, :], ident[:])
                    ins.then_inc(s["t_done"], 1)

                def value(i):
                    at_least(pe, s["vs_done"], i)
                    at_least(pe, s["oTc_done"], i - 1)
                    for a in range(KD):
                        ins = pe.matmul(psM0[:, 0:D], xcT[:, 2 + a, :], W["v"][:, a, :], start=(a == 0), stop=(a == KD - 1))
                    ins.then_inc(s["v_done"], 1)

                def project(i):
                    pe.wait_ge(s["txc_done"], i + 1)
                    for b, (w, src) in enumerate((("q", 0), ("q", 0), ("k", 2), ("k", 2))):
                        for a in range(KD):
                            m = b % 2
                            ins = pe.matmul(psM1[:, b * P:(b + 1) * P], W[w][:, a, m * P:(m + 1) * P], xcT[:, src + a, :],
                                            start=(a == 0), stop=(a == KD - 1))
                    ins.then_inc(s["qk_done"], 1)

                def weigh(i):
                    at_least(pe, s["x_done"], i)
                    pe.wait_ge(s["vpad_done"], i + 1)
                    pe.wait_ge(s["tcA_done"], i * 2 + 2)
                    pe.wait_ge(s["tcV_done"], i * 2 + 2)
                    for m in range(2):
                        for n in range(8):
                            j, parity = divmod(n, 2)
                            ins = pe.matmul(psM0[:, D + m * P:D + (m + 1) * P], vpad[:, 8 * m + n, :], pT[:, 4 * j + 2 * m + parity, :],
                                            start=(n == 0), stop=(n == 7))
                    ins.then_inc(s["pv_done"], 1)

                def scores(i):
                    pe.wait_ge(s["q_lo"], i + 1)
                    pe.wait_ge(s["km_lo"], i + 1)
                    for m in range(2):
                        for j in range(4):
                            r = slice(32 * j, 32 * j + 32)
                            for n, (x, y) in enumerate(PARTS3):
                                ins = pe.matmul(psS[j][:, 2 * m:2 * m + 2, :].rearrange("p a t -> p (a t)"), q[x][r, m, :],
                                                km[y][r, m, :, :].rearrange("p a t -> p (a t)"), start=(n == 0), stop=(n == 2))
                            if m == 1:
                                ins.then_inc(s["s_done"], 1)

                def output(i, last=False):
                    pe.wait_ge(s["oTc_done"], i + 1)
                    if not last:
                        pe.wait_ge(s["vs_done"], i + 3)
                    for a in range(KD):
                        ins = pe.matmul(psM0[:, D:2 * D], oT[:, a, :], W["o"][:, a, :], start=(a == 0), stop=(a == KD - 1))
                    ins.then_inc(s["y_done"], 1)

                def tile(i, first=False, last=False):
                    scores(i)
                    if not last:
                        turn_in(i + 1)
                    if not first:
                        weigh(i - 1)
                    turn_probs(i, 0)
                    turn_probs(i, 1)
                    if not last:
                        project(i + 1)
                        value(i + 1)
                    turn_probs(i, 2)
                    turn_probs(i, 3)
                    if not first:
                        output(i - 1, last)

                pe.wait_ge(s["ident_done"], 1)
                pe.wait_ge(s["w_in"], 64)
                turn_in(0)
                project(0)
                value(0)
                tile(0, first=True)
                with pe.Fori(1, NB - 1) as i:
                    tile(i)
                tile(NB - 1, last=True)
                weigh(NB - 1)
                output(NB - 1, True)


def prefix_steps(dve, s, src, bufs, n):
    a, b = src, bufs[0]
    shift, turn = 1, 0
    while shift < n:
        dve.tensor_copy(b[:, 0:shift], a[:, 0:shift])
        s.step(dve.tensor_tensor(b[:, shift:n], a[:, shift:n], a[:, 0:n - shift], ALU.add))
        turn += 1
        a, b = b, bufs[turn % 2]
        shift *= 2
    return a


def mixture_0(nc, A, sb, ps, sem, NB, D, KD, x_sb, ctx_sb, ident, gates, x_mean, x_rstd, c_mean, c_rstd,
              x_stats, c_stats, nt, over):
    NE = A["L0_ffn_expert_w1"].shape[0]
    F = A["L0_ffn_expert_w1"].shape[1]
    KF = F // P
    NT = NB + NE
    SH = NE
    xg = nc.dram_tensor("m0_sorted", (NT * P, D), F32, kind="Internal").ap()
    yg = nc.dram_tensor("m0_expert_out", (NT * P, D), F32, kind="Internal").ap()
    n_sb = sb("m0_n", [P, NB, D], F32, over, "right")
    prob = sb("m0_prob", [P, NB], F32, over, "right")
    pos = sb("m0_pos", [P, NB], U32, over, "right")
    with ExitStack() as c:
        w1t = sb("m0_w1t", [P, NE + 1, KD, F], F32R, c)
        w2t = sb("m0_w2t", [P, NE + 1, KF, D], F32R, c)
        s1 = sb("m0_s1", [P, NE + 1, KF], F32, c)
        s2 = sb("m0_s2", [P, NE + 1, D], F32, c)
        logits = sb("m0_logits", [P, NB, NE], F32, c)
        owner = sb("m0_owner", [P, NT], I32, c)
        gamma, beta = sb("m0_gamma", [P, KD], F32, c), sb("m0_beta", [P, KD], F32, c)
        router = sb("m0_router", [P, KD, NE], F32, c)
        zeros = sb("m0_zeros", [P, D], F32, c)
        ones = sb("m0_ones", [P, P], F32, c)
        upper = sb("m0_upper", [P, P], F32, c)
        scattered = sem("m0_scattered", c)
        ternary_weights(nc, A, sb, ps, sem, NE, F, KF, KD, D, w1t, w2t, s1, s2, ident, ones, zeros, xg,
                        gamma, beta, router, upper)
        sh = sb("m0_shared", [P, NB, D], F32, c)
        with ExitStack() as turned:
            hT = [sb(f"m0_hT{n}", [P, KD, NB, P], F32R, turned) for n in ("hi", "lo")]
            token_norms(nc, sb, ps, sem, NB, D, KD, x_sb, ident, x_mean, x_rstd, x_stats, nt, n_sb, hT,
                        logits, router, gamma, beta, NE, "m0", True)
            route_top1(nc, sb, ps, sem, NB, NE, NT, D, logits, prob, pos, owner, ones, upper, gates)
            shared_ternary(nc, sb, ps, sem, NB, D, KD, KF, SH, hT, w1t, w2t, s1, sh, n_sb, pos, xg, scattered)
        weights = dict(q=sb("a1_rawq", [P, KD, A["L1_xattn_Wq"].shape[1]], F32, over, "right"),
                       kv=sb("a1_rawkv", [P, KD, A["L1_xattn_Wkv"].shape[1]], F32, over, "right"))
        loaded = {n: sem(f"a1w_{n}_in", over) for n in weights}
        expert_tiles(nc, sb, ps, sem, NB, NT, D, KD, KF, SH, x_sb, sh, s2, s1, w1t, w2t, gamma, beta, ident, owner,
                     xg, yg, gates, scattered, A, weights, loaded)
    return dict(n_sb=n_sb, prob=prob, pos=pos, yg=yg, weights=weights, loaded=loaded)


def ternary_weights(nc, A, sb, ps, sem, NE, F, KF, KD, D, w1t, w2t, s1, s2, ident, ones, zeros, xg,
                    gamma, beta, router, upper):
    with ExitStack() as c:
        raw1 = [sb(f"t_raw1_{i}", [P, KF, D], F32, c) for i in range(2)]
        raw2 = [sb(f"t_raw2_{i}", [P, KD, F], F32, c) for i in range(2)]
        identb = sb("t_identb", [P, P], BF16, c)
        sums = [sb(f"t_sums{i}", [P, KF + KD], F32, c) for i in range(2)]
        mag = sb("t_mag", [P, KF + KD], F32, c)
        thr, nthr = sb("t_thr", [P, KF + KD], F32, c), sb("t_nthr", [P, KF + KD], F32, c)
        neg = sb("t_neg", [P, KF * D + KD * F], BF16, c)
        unused = sb("t_unused", [P, KF * D + KD * F], BF16, c)
        tern = sb("t_tern", [P, KF * D + KD * F], BF16, c)
        diag = sb("t_diag", [P, KD, P], F32, c)
        psA = [ps(f"t_ps{i}", [P, 8, P], BF16, c) for i in range(2)]
        psB = ps("t_psB", [P, D], F32, c)
        names = ("const_done upper_zero raw0 raw1 small_in zero_out steps sum_done mag_done diag_done tern_done turned1 turned2 spread "
                 "w1_done w2_done").split()
        s = {n: sem(f"t_{n}", c) for n in names}
        raw_in = [s["raw0"], s["raw1"]]

        def source(e):
            if isinstance(e, int) and e == NE:
                return A["L0_ffn_shared_w1"], A["L0_ffn_shared_w2"]
            return A["L0_ffn_expert_w1"][e], A["L0_ffn_expert_w2"][e]

        def loads_of(n, buf):
            return (n - buf) * 16 + 32

        with nc.Block() as block:
            @block.sync
            def _(sp):
                with nc.allow_non_contiguous_dma(reason="a few hundred small parameters"):
                    sp.dma_start(gamma[:], A["L0_ffn_ln_gamma"].rearrange("(k p) -> p k", p=P)).then_inc(s["small_in"], 16)
                    sp.dma_start(beta[:], A["L0_ffn_ln_beta"].rearrange("(k p) -> p k", p=P)).then_inc(s["small_in"], 16)
                    sp.dma_start(router[:], A["router_T"].rearrange("(k p) e -> p k e", p=P)).then_inc(s["small_in"], 16)

                def load(e, buf):
                    a, b = source(e)
                    sp.dma_start(raw1[buf][:], a.rearrange("(t p) d -> p t d", p=P)).then_inc(raw_in[buf], 16)
                    sp.dma_start(raw2[buf][:], b.rearrange("(t p) f -> p t f", p=P)).then_inc(raw_in[buf], 16)

                load(NE, 0)
                load(0, 1)
                sp.wait_ge(s["const_done"], 2)
                sp.dma_start(xg.rearrange("(t p) d -> p t d", p=P), zeros[:].unsqueeze(1).to_broadcast([P, xg.shape[0] // P, D]))\
                  .then_inc(s["zero_out"], 16)
                with sp.Fori(0, NE // 2 - 1) as i:
                    for half in range(2):
                        sp.wait_ge(s["tern_done"], i * 2 + half + 1)
                        load(i * 2 + half + 1, half)
                sp.wait_ge(s["tern_done"], NE - 1)
                load(NE - 1, 0)
                sp.wait_ge(s["zero_out"], 16)
                sp.wait_ge(s["small_in"], 48)

            @block.gpsimd
            def _(pool):
                pool.memset(zeros[:], 0.0).then_inc(s["const_done"], 1)
                pool.memset(ones[:], 1.0).then_inc(s["const_done"], 1)
                pool.wait_ge(s["const_done"], 2)
                pool.affine_select(out=upper[:], in_=ones[:], compare_op=ALU.is_gt, fill=0.0, base=0,
                                   pattern=[[1, P]], channel_multiplier=-1).then_inc(s["const_done"], 1)

                def spread(n, e):
                    pool.wait_ge(s["mag_done"], n + 1)
                    at_least(pool, s["spread"], n)
                    for t in range(KD):
                        pool.tensor_tensor(diag[:, t, :], ident[:], mag[:, KF + t:KF + t + 1].to_broadcast([P, P]), ALU.mult)
                    pool.tensor_copy(s1[:, e, :], mag[:, 0:KF]).then_inc(s["diag_done"], 1)

                spread(0, NE)
                with pool.Fori(1, NE + 1) as n:
                    spread(n, n - 1)

            @block.vector
            def _(dve):
                dve.tensor_copy(identb[:], ident[:]).then_inc(s["steps"], 1)
                per = 3

                def signs(n, e, buf, first=False):
                    k = Steps(dve, s["steps"], 1 + n * per)
                    dve.wait_ge(s["sum_done"], n + 1)
                    if not first:
                        dve.wait_ge(s["diag_done"], n)
                    dve.tensor_scalar(mag[:, 0:KF], sums[buf][:, 0:KF], 1.0 / D, 1e-5, ALU.mult, ALU.max)
                    dve.tensor_scalar(mag[:, KF:], sums[buf][:, KF:], 1.0 / F, 1e-5, ALU.mult, ALU.max).then_inc(s["mag_done"], 1)
                    dve.wait_ge(s["mag_done"], n + 1)
                    dve.tensor_scalar(thr[:], mag[:], 0.5, None, ALU.mult)
                    k.step(dve.tensor_scalar(nthr[:], mag[:], -0.5, None, ALU.mult))
                    rows = [(raw1[buf][:, t, :], t * D, D) for t in range(KF)] + \
                           [(raw2[buf][:, t, :], KF * D + t * F, F) for t in range(KD)]
                    for t, (w, at, width) in enumerate(rows):
                        ins = dve.tensor_scalar(neg[:, at:at + width], w, nthr[:, t:t + 1], None, ALU.is_lt)
                    k.step(ins)
                    if not first:
                        dve.wait_ge(s["turned2"], n)
                    for t, (w, at, width) in enumerate(rows):
                        ins = dve.scalar_tensor_tensor(out=tern[:, at:at + width], in0=w, scalar=thr[:, t:t + 1],
                                                       in1=neg[:, at:at + width], op0=ALU.is_gt, op1=ALU.subtract)
                    ins.then_inc(s["tern_done"], 1)
                    dve.wait_ge(s["spread"], n + 1)
                    k.step(dve.tensor_copy(s2[:, e, :], psB[:]))
                    assert k.n == per

                signs(0, NE, 0, True)
                with dve.Fori(0, NE // 2) as i:
                    signs(i * 2 + 1, i * 2, 1)
                    signs(i * 2 + 2, i * 2 + 1, 0)

            @block.tensor
            def _(pe):
                pe.wait_ge(s["const_done"], 3)

                def turn(n, first=False):
                    pe.wait_ge(s["tern_done"], n + 1)
                    if not first:
                        pe.wait_ge(s["w1_done"], n)
                    for a in range(KD):
                        for t in range(KF):
                            ins = pe.transpose(psA[0][:, a * KF + t, :], tern[:, t * D + a * P:t * D + (a + 1) * P], identb[:])
                    ins.then_inc(s["turned1"], 1)
                    if not first:
                        pe.wait_ge(s["w2_done"], n)
                    for a in range(KF):
                        for t in range(KD):
                            at = KF * D + t * F + a * P
                            ins = pe.transpose(psA[1][:, a * KD + t, :], tern[:, at:at + P], identb[:])
                    ins.then_inc(s["turned2"], 1)

                def spread(n, first=False):
                    pe.wait_ge(s["diag_done"], n + 1)
                    if not first:
                        pe.wait_ge(s["steps"], 1 + n * 3)
                    for t in range(KD):
                        ins = pe.matmul(psB[:, t * P:(t + 1) * P], ones[:], diag[:, t, :], start=True, stop=True)
                    ins.then_inc(s["spread"], 1)

                spread(0, True)
                turn(0, True)
                with pe.Fori(1, NE + 1) as n:
                    spread(n)
                    turn(n)

            @block.scalar
            def _(act):
                def keep(n, e):
                    act.wait_ge(s["turned1"], n + 1)
                    act.activation(w1t[:, e, :, :].rearrange("p k f -> p (k f)"), psA[0][:].rearrange("p a t -> p (a t)"),
                                   ACT.Copy).then_inc(s["w1_done"], 1)
                    act.wait_ge(s["turned2"], n + 1)
                    act.activation(w2t[:, e, :, :].rearrange("p k f -> p (k f)"), psA[1][:].rearrange("p a t -> p (a t)"),
                                   ACT.Copy).then_inc(s["w2_done"], 1)

                def magnitudes(n, buf):
                    act.wait_ge(raw_in[buf], loads_of(n, buf))
                    at_least(act, s["mag_done"], n - 1)
                    at_least(act, s["sum_done"], n)
                    for t in range(KF):
                        act.activation(unused[:, t * D:(t + 1) * D], raw1[buf][:, t, :], ACT.Abs, accum_out=sums[buf][:, t:t + 1])
                    for t in range(KD):
                        ins = act.activation(unused[:, KF * D + t * F:KF * D + (t + 1) * F], raw2[buf][:, t, :], ACT.Abs, accum_out=sums[buf][:, KF + t:KF + t + 1])
                    ins.then_inc(s["sum_done"], 1)

                magnitudes(0, 0)
                magnitudes(1, 1)
                keep(0, NE)
                with act.Fori(1, NE // 2) as i:
                    magnitudes(i * 2, 0)
                    keep(i * 2 - 1, i * 2 - 2)
                    magnitudes(i * 2 + 1, 1)
                    keep(i * 2, i * 2 - 1)
                magnitudes(NE, 0)
                keep(NE - 1, NE - 2)
                keep(NE, NE - 1)


def token_norms(nc, sb, ps, sem, NB, D, KD, x_sb, ident, x_mean, x_rstd, x_stats, nt, n_sb, hT,
                logits, router, gamma, beta, NE, tag, twice):
    with ExitStack() as c:
        n_t = [sb(f"{tag}_nt{i}", [P, D], F32, c) for i in range(2)]
        h = [sb(f"{tag}_h{i}", [P, KD, P], F32, c) for i in range(2)]
        psT = [ps(f"{tag}_psN{i}", [P, KD, P], F32, c) for i in range(2)]
        psL = [ps(f"{tag}_psL{i}", [P, NE], F32, c) for i in range(2)]
        s = {n: sem(f"{tag}_n_{n}", c) for n in ("steps normed kept turned scaled split scored logits_out".split())}
        with nc.Block() as block:
            @block.vector
            def _(dve):
                k = Steps(dve, s["steps"])
                norm_steps(dve, k, x_stats, x_mean[:], x_rstd[:], [t[:] for t in nt], twice)
                base = k.n

                def norm(i, b, first=False):
                    if not first:
                        dve.wait_ge(s["turned"], i - 1)
                        dve.wait_ge(s["kept"], i - 1)
                    dve.tensor_scalar(n_t[b][:], x_sb[:, i, :], x_mean[:, bass.ds(i, 1)], x_rstd[:, bass.ds(i, 1)],
                                      ALU.subtract, ALU.mult).then_inc(s["normed"], 1)

                def split(i, b):
                    dve.wait_ge(s["scaled"], i + 1)
                    k = Steps(dve, s["steps"], base + i)
                    k.step(dve.tensor_copy(hT[0][:, :, i, :], h[b][:]))
                    dve.tensor_tensor(hT[1][:, :, i, :], h[b][:], hT[0][:, :, i, :].bitcast(F32), ALU.subtract)\
                       .then_inc(s["split"], 1)

                def keep_logits(i, b):
                    dve.wait_ge(s["scored"], i + 1)
                    dve.tensor_copy(logits[:, i, :], psL[b][:]).then_inc(s["logits_out"], 1)

                norm(0, 0, True)
                norm(1, 1, True)
                for b in range(2):
                    split(b, b)
                    norm(b + 2, b)
                    if b == 1:
                        keep_logits(0, 0)
                with dve.Fori(1, NB // 2 - 1) as i:
                    for b in range(2):
                        split(i * 2 + b, b)
                        norm(i * 2 + b + 2, b)
                        keep_logits(i * 2 + b - 1, 1 - b)
                for b in range(2):
                    split(NB - 2 + b, b)
                    keep_logits(NB - 3 + b, 1 - b)
                keep_logits(NB - 1, 1)

            @block.gpsimd
            def _(pool):
                with pool.Fori(0, NB // 2) as i:
                    for b in range(2):
                        pool.wait_ge(s["normed"], i * 2 + b + 1)
                        pool.tensor_copy(n_sb[:, i * 2 + b, :], n_t[b][:]).then_inc(s["kept"], 1)

            @block.tensor
            def _(pe):
                def turn(i, b, first=False):
                    pe.wait_ge(s["normed"], i + 1)
                    if not first:
                        pe.wait_ge(s["scaled"], i - 1)
                    for a in range(KD):
                        ins = pe.transpose(psT[b][:, a, :], n_t[b][:, a * P:(a + 1) * P], ident[:])
                    ins.then_inc(s["turned"], 1)

                def score(i, b, first=False):
                    pe.wait_ge(s["scaled"], i + 1)
                    if not first:
                        pe.wait_ge(s["logits_out"], i - 1)
                    for a in range(KD):
                        ins = pe.matmul(psL[b][:], h[b][:, a, :], router[:, a, :], start=(a == 0), stop=(a == KD - 1))
                    ins.then_inc(s["scored"], 1)

                turn(0, 0, True)
                turn(1, 1, True)
                score(0, 0, True)
                turn(2, 0)
                score(1, 1, True)
                turn(3, 1)
                with pe.Fori(1, NB // 2 - 1) as i:
                    for b in range(2):
                        score(i * 2 + b, b)
                        turn(i * 2 + b + 2, b)
                for b in range(2):
                    score(NB - 2 + b, b)

            @block.scalar
            def _(act):
                def scale(i, b, first=False):
                    act.wait_ge(s["turned"], i + 1)
                    if not first:
                        act.wait_ge(s["scored"], i - 1)
                        act.wait_ge(s["split"], i - 1)
                    if gamma is None:
                        act.activation(h[b][:], psT[b][:], ACT.Copy).then_inc(s["scaled"], 1)
                        return
                    for a in range(KD):
                        ins = act.activation(h[b][:, a, :], psT[b][:, a, :], ACT.Identity, bias=beta[:, a:a + 1],
                                             scale=gamma[:, a:a + 1])
                    ins.then_inc(s["scaled"], 1)

                scale(0, 0, True)
                scale(1, 1, True)
                with act.Fori(1, NB // 2) as i:
                    for b in range(2):
                        scale(i * 2 + b, b)


def route_top1(nc, sb, ps, sem, NB, NE, NT, D, logits, prob, pos, owner, ones, upper, gates):
    with ExitStack() as c:
        best = sb("r0_best", [P, NB, 8], F32, c)
        index = sb("r0_index", [P, NB, 8], U32, c)
        shifted = sb("r0_shifted", [P, NB, NE], F32, c)
        expd = sb("r0_exp", [P, NB, NE], F32, c)
        which = sb("r0_which", [P, NB], F32, c)
        iota_i = sb("r0_iota_i", [P, NT], I32, c)
        iota = sb("r0_iota", [P, NT], F32, c)
        hot = sb("r0_hot", [P, NB, NE], F32, c)
        rank = sb("r0_rank", [P, NB, NE], F32, c)
        tot = sb("r0_tot", [P, NB, NE], F32, c)
        pre = [sb(f"r0_pre{i}", [P, NB, NE], F32, c) for i in range(2)]
        cnt_i = sb("r0_cnt_i", [P, NE], I32, c)
        tiles = sb("r0_tiles", [P, NE], F32, c)
        ends = [sb(f"r0_ends{i}", [P, NE], F32, c) for i in range(2)]
        base = sb("r0_base", [P, NE], F32, c)
        after = sb("r0_after", [P, NT, NE], F32, c)
        nown = sb("r0_nown", [P, NT], F32, c)
        posf = sb("r0_posf", [P, NB], F32, c)
        psR = ps("r0_ps", [P, 2, NB * NE], F32, c)
        s = {n: sem(f"r0_{n}", c) for n in "steps iota_done shifted_done exp_done hot_done ranked".split()}

        with nc.Block() as block:
            @block.gpsimd
            def _(pool):
                pool.iota(iota_i[:], pattern=[[1, NT]], base=0, channel_multiplier=0).then_inc(s["iota_done"], 1)

            @block.scalar
            def _(act):
                act.wait_ge(s["shifted_done"], 1)
                act.activation(expd[:], shifted[:], ACT.Exp).then_inc(s["exp_done"], 1)

            @block.tensor
            def _(pe):
                pe.wait_ge(s["hot_done"], 1)
                flat = hot[:].rearrange("p b e -> p (b e)")
                pe.matmul(psR[:, 0, :], upper[:], flat, start=True, stop=True)
                pe.matmul(psR[:, 1, :], ones[:], flat, start=True, stop=True).then_inc(s["ranked"], 1)

            @block.vector
            def _(dve):
                k = Steps(dve, s["steps"])
                for i in range(NB):
                    ins = dve.max(best[:, i, :], logits[:, i, :])
                k.step(ins)
                for i in range(NB):
                    dve.max_index(index[:, i, :], best[:, i, :], logits[:, i, :])
                dve.tensor_tensor(shifted[:], logits[:], best[:, :, 0:1].to_broadcast([P, NB, NE]), ALU.subtract)\
                   .then_inc(s["shifted_done"], 1)
                dve.wait_ge(s["iota_done"], 1)
                k.step(dve.tensor_copy(iota[:], iota_i[:]))
                k.step(dve.tensor_copy(which[:], index[:, :, 0]))
                dve.tensor_tensor(hot[:], which[:].unsqueeze(2).to_broadcast([P, NB, NE]),
                                  iota[:, 0:NE].unsqueeze(1).to_broadcast([P, NB, NE]), ALU.is_equal).then_inc(s["hot_done"], 1)
                dve.wait_ge(s["exp_done"], 1)
                k.step(dve.tensor_reduce(prob[:], expd[:], AX.X, ALU.add))
                k.step(dve.reciprocal(prob[:], prob[:]))
                k.step(dve.tensor_scalar(prob[:], prob[:], gates[:, 2:3], None, ALU.mult))
                dve.wait_ge(s["ranked"], 1)
                three = lambda t: t.rearrange("p (b e) -> p b e", e=NE)
                k.step(dve.tensor_copy(tot[:], three(psR[:, 1, :])))
                incl = prefix_steps(dve, k, tot, pre, NB)
                k.step(dve.tensor_tensor(rank[:], three(psR[:, 0, :]), incl[:], ALU.add))
                k.step(dve.tensor_tensor(rank[:], rank[:], tot[:], ALU.subtract))
                k.step(dve.tensor_scalar(cnt_i[:], incl[:, NB - 1, :], float(P - 1), None, ALU.add))
                k.step(dve.tensor_scalar(cnt_i[:], cnt_i[:], 7, None, ALU.logical_shift_right))
                k.step(dve.tensor_copy(tiles[:], cnt_i[:]))
                end = prefix_steps(dve, k, tiles, ends, NE)
                k.step(dve.tensor_tensor(base[:], end[:], tiles[:], ALU.subtract))
                k.step(dve.tensor_scalar(base[:], base[:], float(P), None, ALU.mult))
                k.step(dve.tensor_tensor(rank[:], rank[:], base[:].unsqueeze(1).to_broadcast([P, NB, NE]), ALU.add))
                k.step(dve.tensor_tensor(rank[:], rank[:], hot[:], ALU.mult))
                k.step(dve.tensor_reduce(posf[:], rank[:], AX.X, ALU.add))
                k.step(dve.tensor_copy(pos[:], posf[:]))
                k.step(dve.tensor_tensor(after[:], iota[:].unsqueeze(2).to_broadcast([P, NT, NE]),
                                         end[:].unsqueeze(1).to_broadcast([P, NT, NE]), ALU.is_ge))
                k.step(dve.tensor_reduce(nown[:], after[:], AX.X, ALU.add))
                k.step(dve.tensor_scalar(owner[:], nown[:], float(NE - 1), None, ALU.min))


def shared_ternary(nc, sb, ps, sem, NB, D, KD, KF, SH, hT, w1t, w2t, s1, sh, n_sb, pos, xg, scattered):
    with ExitStack() as c:
        NQ = KF // 2
        PAIRS = NB // 2
        g = [sb(f"s0_g{i}", [P, KF, 2 * P], F32, c) for i in range(2)]
        gs = [[sb(f"s0_g{n}{i}", [P, KF, 2 * P], F32R, c) for n in ("hi", "lo")] for i in range(2)]
        psH = [[ps(f"s0_psH{i}{q}", [P, 2, 2 * P], F32, c) for q in range(NQ)] for i in range(2)]
        psY = [ps(f"s0_psY{i}", [P, D], F32, c) for i in range(2)]
        s = {n: sem(f"s0_{n}", c) for n in "up silu g_hi g_lo down kept".split()}
        with nc.Block() as block:
            @block.gpsimd
            def _(pool):
                for i in range(NB):
                    pool.indirect_dma_start(xg, bass.IndirectOffsetOnAxis(ap=pos[:, i:i + 1], axis=0), n_sb[:, i, :], None)\
                        .then_inc(scattered, 16)

            @block.tensor
            def _(pe):
                def up(i, b):
                    for q in range(NQ):
                        at_least(pe, s["silu"], (i - 2) * NQ + q + 1)
                        for j in range(2):
                            t = 2 * q + j
                            for n, (a, part) in enumerate([(a, part) for a in range(KD) for part in range(2)]):
                                ins = pe.matmul(psH[b][q][:, j, :], w1t[:, SH, a, t * P:(t + 1) * P],
                                                hT[part][:, a, bass.ds(i * 2, 2), :].rearrange("p b t -> p (b t)"),
                                                start=(n == 0), stop=(n == 2 * KD - 1))
                        ins.then_inc(s["up"], 1)

                def down(i, b):
                    pe.wait_ge(s["g_lo"], i * NQ + NQ)
                    for j in range(2):
                        at_least(pe, s["kept"], (i - 1) * 2 + j + 1)
                        for n, (t, part) in enumerate([(t, part) for t in range(KF) for part in range(2)]):
                            ins = pe.matmul(psY[j][:], gs[b][part][:, t, j * P:(j + 1) * P], w2t[:, SH, t, :],
                                            start=(n == 0), stop=(n == 2 * KF - 1))
                        ins.then_inc(s["down"], 1)

                up(0, 0)
                up(1, 1)
                for b in range(2):
                    down(b, b)
                    up(b + 2, b)
                with pe.Fori(1, PAIRS // 2 - 1) as i:
                    for b in range(2):
                        down(i * 2 + b, b)
                        up(i * 2 + b + 2, b)
                for b in range(2):
                    down(PAIRS - 2 + b, b)

            @block.scalar
            def _(act):
                def silu(i, b):
                    for q in range(NQ):
                        act.wait_ge(s["up"], i * NQ + q + 1)
                        at_least(act, s["g_lo"], (i - 2) * NQ + q + 1)
                        for j in range(2):
                            t = 2 * q + j
                            ins = act.activation(g[b][:, t, :], psH[b][q][:, j, :], ACT.Silu, scale=s1[:, SH, t:t + 1])
                        ins.then_inc(s["silu"], 1)

                def keep(i):
                    for j in range(2):
                        act.wait_ge(s["down"], i * 2 + j + 1)
                        act.activation(sh[:, i * 2 + j, :], psY[j][:], ACT.Copy).then_inc(s["kept"], 1)

                silu(0, 0)
                silu(1, 1)
                for b in range(2):
                    keep(b)
                    silu(b + 2, b)
                with act.Fori(1, PAIRS // 2 - 1) as i:
                    for b in range(2):
                        keep(i * 2 + b)
                        silu(i * 2 + b + 2, b)
                for b in range(2):
                    keep(PAIRS - 2 + b)

            @block.vector
            def _(dve):
                def split(i, b):
                    at_least(dve, s["down"], (i - 1) * 2)
                    for q in range(NQ):
                        own = slice(2 * q, 2 * q + 2)
                        dve.wait_ge(s["silu"], i * NQ + q + 1)
                        dve.tensor_copy(gs[b][0][:, own, :], g[b][:, own, :]).then_inc(s["g_hi"], 1)
                        dve.wait_ge(s["g_hi"], i * NQ + q + 1)
                        dve.tensor_tensor(gs[b][1][:, own, :], g[b][:, own, :], gs[b][0][:, own, :].bitcast(F32), ALU.subtract)\
                           .then_inc(s["g_lo"], 1)

                for i in range(4):
                    split(i, i % 2)
                with dve.Fori(2, PAIRS // 2) as i:
                    for b in range(2):
                        split(i * 2 + b, b)


def expert_tiles(nc, sb, ps, sem, NB, NT, D, KD, KF, SH, x_sb, sh, s2, s1, w1t, w2t, gamma, beta, ident, owner,
                 xg, yg, gates, scattered, A, weights, loaded):
    F = KF * P
    with ExitStack() as c:
        xin = [sb(f"e0_xin{i}", [P, D], F32, c) for i in range(2)]
        h = [sb(f"e0_h{i}", [P, KD, P], F32, c) for i in range(2)]
        hs = [[sb(f"e0_h{n}{i}", [P, KD, P], F32R, c) for n in ("hi", "lo")] for i in range(2)]
        u = [sb(f"e0_u{i}", [P, F], F32, c) for i in range(2)]
        g = [sb(f"e0_g{i}", [P, KF, P], F32, c) for i in range(2)]
        gs = [[sb(f"e0_g{n}{i}", [P, KF, P], F32R, c) for n in ("hi", "lo")] for i in range(2)]
        y = [sb(f"e0_y{i}", [P, D], F32, c) for i in range(2)]
        s2g = sb("e0_s2g", [P, D], F32, c)
        psA = [ps(f"e0_psA{i}", [P, KD, P], F32, c) for i in range(2)]
        psH = [ps(f"e0_psH{i}", [P, F], F32, c) for i in range(2)]
        psT = [ps(f"e0_psT{i}", [P, KF, P], F32, c) for i in range(2)]
        psY = [ps(f"e0_psY{i}", [P, D], F32, c) for i in range(2)]
        names = "in0 in1 turned scaled steps steps2 split up up_out turned2 silu split2 down y_done out0 out1 shared_in s2g".split()
        s = {n: sem(f"e0_{n}", c) for n in names}
        x_in, y_out = [s["in0"], s["in1"]], [s["out0"], s["out1"]]

        LAG_UP, LAG_TURN2, LAG_DOWN, LAG_OUT = 2, 4, 6, 7
        PEEL = 10

        def steps(eng, step):
            for t in range(PEEL):
                step(t, t // 2, t % 2)
            with eng.Fori(PEEL // 2, NT // 2) as i:
                for b in range(2):
                    step(i * 2 + b, i, b)
            for t in range(NT, NT + LAG_OUT):
                step(t, t // 2, t % 2)

        def tile_at(t, i, b, lag):
            if isinstance(t, int) and not 0 <= t - lag < NT:
                return None
            buf = (b - lag) % 2
            return t - lag, i + (b - lag - buf) // 2, buf

        with nc.Block() as block:
            @block.sync
            def _(sp):
                sp.wait_ge(scattered, 16 * NB)

                def load(j, b):
                    sp.dma_start(xin[b][:], xg.rearrange("(t p) d -> t p d", p=P)[j]).then_inc(x_in[b], 16)

                def store(j, b):
                    sp.wait_ge(s["y_done"], j + 1)
                    sp.dma_start(yg.rearrange("(t p) d -> t p d", p=P)[j], y[b][:]).then_inc(y_out[b], 16)

                def step(t, i, b):
                    if tile_at(t, i, b, LAG_OUT):
                        store(t - LAG_OUT, 1 - b)
                    if isinstance(t, int) and (t == 0 or t + 1 >= NT):
                        return
                    sp.wait_ge(s["turned"], t)
                    load(t + 1, 1 - b)

                for b in range(2):
                    load(b, b)
                for t in range(PEEL):
                    step(t, t // 2, t % 2)
                sp.dma_start(weights["kv"][:], A["L1_xattn_Wkv"].rearrange("(k p) n -> p k n", p=P)).then_inc(loaded["kv"], 16)
                sp.dma_start(weights["q"][:], A["L1_xattn_Wq"].rearrange("(k p) n -> p k n", p=P)).then_inc(loaded["q"], 16)
                with sp.Fori(PEEL // 2, NT // 2 - 1) as i:
                    for b in range(2):
                        step(i * 2 + b, i, b)
                for t in range(NT - 2, NT + LAG_OUT):
                    step(t, t // 2, t % 2)

            @block.tensor
            def _(pe):
                def turn(j, i, b):
                    pe.wait_ge(x_in[b], i * 16 + 16)
                    at_least(pe, s["scaled"], j - 1)
                    for a in range(KD):
                        ins = pe.transpose(psA[b][:, a, :], xin[b][:, a * P:(a + 1) * P], ident[:])
                    ins.then_inc(s["turned"], 1)

                def up(j, i, b):
                    e = pe.value_load(owner[0:1, bass.ds(j, 1)], min_val=0, max_val=SH - 1)
                    pe.wait_ge(s["split"], j + 1)
                    at_least(pe, s["up_out"], j - 1)
                    for n, (a, part) in enumerate([(a, part) for a in range(KD) for part in range(2)]):
                        ins = pe.matmul(psH[b][:], hs[b][part][:, a, :], w1t[:, e, a, :], start=(n == 0), stop=(n == 2 * KD - 1))
                    ins.then_inc(s["up"], 1)

                def turn2(j, i, b):
                    pe.wait_ge(s["up_out"], j + 1)
                    at_least(pe, s["silu"], j - 1)
                    for t in range(KF):
                        ins = pe.transpose(psT[b][:, t, :], u[b][:, t * P:(t + 1) * P], ident[:])
                    ins.then_inc(s["turned2"], 1)

                def down(j, i, b):
                    e = pe.value_load(owner[0:1, bass.ds(j, 1)], min_val=0, max_val=SH - 1)
                    pe.wait_ge(s["split2"], j + 1)
                    at_least(pe, s["y_done"], j - 1)
                    for n, (t, part) in enumerate([(t, part) for t in range(KF) for part in range(2)]):
                        ins = pe.matmul(psY[b][:], gs[b][part][:, t, :], w2t[:, e, t, :], start=(n == 0), stop=(n == 2 * KF - 1))
                    ins.then_inc(s["down"], 1)

                def step(t, i, b):
                    for lag, do in ((0, turn), (LAG_TURN2, turn2), (LAG_UP, up), (LAG_DOWN, down)):
                        at = tile_at(t, i, b, lag)
                        if at:
                            do(*at)

                steps(pe, step)

            @block.scalar
            def _(act):
                def scale(j, i, b):
                    act.wait_ge(s["turned"], j + 1)
                    at_least(act, s["split"], j - 1)
                    for a in range(KD):
                        ins = act.activation(h[b][:, a, :], psA[b][:, a, :], ACT.Identity, bias=beta[:, a:a + 1],
                                             scale=gamma[:, a:a + 1])
                    ins.then_inc(s["scaled"], 1)

                def silu(j, i, b):
                    e = act.value_load(owner[0:1, bass.ds(j, 1)], min_val=0, max_val=SH - 1)
                    act.wait_ge(s["turned2"], j + 1)
                    at_least(act, s["split2"], j - 1)
                    for t in range(KF):
                        ins = act.activation(g[b][:, t, :], psT[b][:, t, :], ACT.Silu, scale=s1[:, e, t:t + 1])
                    ins.then_inc(s["silu"], 1)

                def step(t, i, b):
                    for lag, do in ((0, scale), (LAG_TURN2, silu)):
                        at = tile_at(t, i, b, lag)
                        if at:
                            do(*at)

                steps(act, step)

            @block.vector
            def _(dve):
                dve.tensor_scalar(s2g[:], s2[:, SH, :], gates[:, 2:3], None, ALU.mult).then_inc(s["s2g"], 1)

                def split(j, i, b):
                    dve.wait_ge(s["scaled"], j + 1)
                    at_least(dve, s["up"], j - 1)
                    k = Steps(dve, s["steps"], j)
                    k.step(dve.tensor_copy(hs[b][0][:], h[b][:]))
                    dve.tensor_tensor(hs[b][1][:], h[b][:], hs[b][0][:].bitcast(F32), ALU.subtract).then_inc(s["split"], 1)

                def up_out(j, i, b):
                    dve.wait_ge(s["up"], j + 1)
                    at_least(dve, s["turned2"], j - 1)
                    dve.tensor_copy(u[b][:], psH[b][:]).then_inc(s["up_out"], 1)

                def split2(j, i, b):
                    dve.wait_ge(s["silu"], j + 1)
                    at_least(dve, s["down"], j - 1)
                    k = Steps(dve, s["steps2"], j)
                    k.step(dve.tensor_copy(gs[b][0][:], g[b][:]))
                    dve.tensor_tensor(gs[b][1][:], g[b][:], gs[b][0][:].bitcast(F32), ALU.subtract).then_inc(s["split2"], 1)

                def out(j, i, b):
                    e = dve.value_load(owner[0:1, bass.ds(j, 1)], min_val=0, max_val=SH - 1)
                    dve.wait_ge(s["down"], j + 1)
                    at_least(dve, y_out[b], i * 16)
                    dve.tensor_tensor(y[b][:], psY[b][:], s2[:, e, :], ALU.mult).then_inc(s["y_done"], 1)

                def step(t, i, b):
                    for lag, do in ((LAG_OUT, out), (LAG_UP + 1, up_out), (LAG_TURN2 + 1, split2), (1, split)):
                        at = tile_at(t, i, b, lag)
                        if at:
                            do(*at)

                steps(dve, step)

            @block.gpsimd
            def _(pool):
                pool.wait_ge(s["s2g"], 1)
                with pool.Fori(0, NB) as i:
                    pool.tensor_tensor(sh[:, i, :], sh[:, i, :], s2g[:], ALU.mult).then_inc(s["shared_in"], 1)
                    pool.wait_ge(s["shared_in"], i * 2 + 1)
                    pool.tensor_tensor(x_sb[:, i, :], x_sb[:, i, :], sh[:, i, :], ALU.add).then_inc(s["shared_in"], 1)
                for b in range(2):
                    pool.wait_ge(y_out[b], NT // 2 * 16)


def attention_1(nc, A, sb, ps, sem, NB, D, KD, x_sb, ctx_sb, ident, gates, x_mean, x_rstd, c_mean, c_rstd,
                x_stats, c_stats, nt, over, begun):
    DH = 128
    NI = A["L1_xattn_Wq"].shape[1]
    NH = NI // DH
    NK = 2 * P
    scale = float(DH) ** -0.5
    with ExitStack() as c:
        wq = [sb(f"a1_wq{n}", [P, KD, NI], F32R, c) for n in ("hi", "lo")]
        wkv = [sb(f"a1_wkv{n}", [P, KD, 2 * NI], F32R, c) for n in ("hi", "lo")]
        wo = [sb(f"a1_wo{n}", [P, NH, D], F32R, c) for n in ("hi", "lo")]
        bq, bk = sb("a1_bq", [P, NH], F32, c), sb("a1_bk", [P, NH], F32, c)
        bv, bo = sb("a1_bv", [P, NI], F32, c), sb("a1_bo", [P, D], F32, c)
        gam, bet = sb("a1_gam", [P, 2, KD], F32, c), sb("a1_bet", [P, 2, KD], F32, c)

        with ExitStack() as r:
            rawq, rawkv = begun["weights"]["q"], begun["weights"]["kv"]
            n_sb, prob, pos, yg = (begun[n] for n in ("n_sb", "prob", "pos", "yg"))
            gathered = [sem(f"e0_gathered{i}", r) for i in range(NB)]
            rawo = sb("a1_rawo", [P, NH, D], F32, r)
            s = {n: sem(f"a1w_{n}", r) for n in "o_in small_in scaled hi lo steps combined".split()}
            q_in, kv_in = begun["loaded"]["q"], begun["loaded"]["kv"]
            with nc.Block() as block:
                @block.sync
                def _(sp):
                    sp.dma_start(rawo[:], A["L1_xattn_Wo"].rearrange("(h p) n -> p h n", p=P)).then_inc(s["o_in"], 16)
                    with nc.allow_non_contiguous_dma(reason="a few hundred small parameters"):
                        for dst, src in ((bq[:], A["L1_xattn_bq"].rearrange("(h p) -> p h", p=P)),
                                         (bk[:], A["L1_xattn_bkv"][0:NI].rearrange("(h p) -> p h", p=P)),
                                         (bv[:], A["L1_xattn_bkv"][NI:2 * NI].partition_broadcast(P)),
                                         (bo[:], A["L1_xattn_bo"].partition_broadcast(P)),
                                         (gam[:, 0, :], A["L1_xattn_gamma_media"].rearrange("(k p) -> p k", p=P)),
                                         (gam[:, 1, :], A["L1_xattn_gamma_lat"].rearrange("(k p) -> p k", p=P)),
                                         (bet[:, 0, :], A["L1_xattn_beta_media"].rearrange("(k p) -> p k", p=P)),
                                         (bet[:, 1, :], A["L1_xattn_beta_lat"].rearrange("(k p) -> p k", p=P))):
                            sp.dma_start(dst, src).then_inc(s["small_in"], 16)
                    sp.wait_ge(s["small_in"], 128)

                flat = lambda t: t.rearrange("p a n -> p (a n)")
                chunks = [(wq, rawq, 0)] + [(wkv, rawkv, n) for n in range(2)] + [(wo, rawo, 0)]

                @block.scalar
                def _(act):
                    act.wait_ge(q_in, 16)
                    act.activation(rawq[:], rawq[:], ACT.Copy, scale=scale).then_inc(s["scaled"], 1)
                    act.wait_ge(s["scaled"], 1)
                    for n, (w, raw, part) in enumerate(chunks):
                        if n == 1:
                            act.wait_ge(kv_in, 16)
                        if n == 3:
                            act.wait_ge(s["o_in"], 16)
                        cols = slice(2048 * part, 2048 * (part + 1))
                        act.activation(flat(w[0][:])[:, cols], flat(raw[:])[:, cols], ACT.Copy).then_inc(s["hi"], 1)

                @block.gpsimd
                def _(pool):
                    for i in range(NB):
                        pool.indirect_dma_start(n_sb[:, i, :], None, yg, bass.IndirectOffsetOnAxis(ap=pos[:, i:i + 1], axis=0))\
                            .then_inc(gathered[i], 16)
                    pool.wait_ge(s["hi"], len(chunks))
                    pool.tensor_tensor(flat(wo[1][:]), flat(rawo[:]), flat(wo[0][:]).bitcast(F32), ALU.subtract)

                @block.vector
                def _(dve):
                    def combine(i):
                        dve.wait_ge(gathered[i], 16)
                        dve.scalar_tensor_tensor(out=x_sb[:, i, :], in0=n_sb[:, i, :], scalar=prob[:, i:i + 1],
                                                 in1=x_sb[:, i, :], op0=ALU.mult, op1=ALU.add).then_inc(s["combined"], 1)

                    def statistics(i):
                        dve.wait_ge(s["combined"], i + 1)
                        return dve.bn_stats(x_stats[:, i, :], x_sb[:, i, :])

                    k = Steps(dve, s["steps"])
                    per = NB // len(chunks)
                    for n, (w, raw, part) in enumerate(chunks):
                        cols = slice(2048 * part, 2048 * (part + 1))
                        if n + 1 < len(chunks):
                            dve.wait_ge(s["hi"], n + 1)
                            dve.tensor_tensor(flat(w[1][:])[:, cols], flat(raw[:])[:, cols], flat(w[0][:])[:, cols].bitcast(F32),
                                              ALU.subtract)
                        for i in range(n * per, (n + 1) * per):
                            combine(i)
                            if i > 0:
                                statistics(i - 1)
                    k.step(statistics(NB - 1))
                    norm_steps(dve, k, x_stats, x_mean[:], x_rstd[:], [t[:] for t in nt], True)
                    dve.wait_ge(s["small_in"], 128)
                    dve.tensor_scalar(bq[:], bq[:], scale, None, ALU.mult)
                    dve.tensor_scalar(bo[:], bo[:], gates[:, 1:2], None, ALU.mult)

        over.close()
        after = ExitStack()
        ahead = dict(over=after, raw1=sb("d_raw1", [P, KD, A["sh1_T"].shape[1]], F32, after, "right"),
                     raw2=sb("d_raw2", [P, A["sh2_T"].shape[0] // P, D], F32, after, "right"),
                     w1_in=sem("d_w1_in", after), w2_in=sem("d_w2_in", after))

        normed = [sb(f"a1_n{n}", [P, D], F32, c) for n in ("media", "lat")]
        kvf = sb("a1_kvf", [P, KD, NK], F32, c)
        kv = [[sb(f"a1_kv{n}{i}", [P, KD, NK], F32R, c) for n in ("hi", "lo")] for i in range(2)]
        q = [sb(f"a1_q{n}", [P, NH, P], F32R, c) for n in ("hi", "lo")]
        k_ = [sb(f"a1_k{n}", [P, NH, NK], F32R, c) for n in ("hi", "lo")]
        vf = sb("a1_vf", [P, 512], F32, c)
        v = [sb(f"a1_v{n}", [P, 2, NI], F32R, c) for n in ("hi", "lo")]
        nmax, sums, rsum = (sb(f"a1_{n}", [P, NH], F32, c) for n in ("nmax", "sums", "rsum"))
        probs = sb("a1_probs", [P, NH, NK], F32, c)
        pT = [sb(f"a1_pT{n}", [P, NH, 2, P], F32R, c) for n in ("hi", "lo")]
        oT = [sb(f"a1_oT{n}", [P, NH, P], F32R, c) for n in ("hi", "lo")]
        psA = [ps(f"a1_psA{i}", [P, 3 * P], F32, c) for i in range(2)]
        psS = [ps(f"a1_psS{i}", [P, NK], F32, c) for i in range(2)]
        psT = ps("a1_psT", [P, 2, P], F32, c)
        psO = ps("a1_psO", [P, P], F32, c)
        psV = ps("a1_psV", [P, 512], F32, c)
        psY = ps("a1_psY", [P, D], F32, c)
        names = ("normed resid kv_turned kv_scaled kv_hi kv_lo qk_done qk_hi qk_lo s_done max_done exp_done rsum_done "
                 "p_done t_done pt_hi pt_lo pv_done o_hi o_lo v_done v_f v_hi v_lo y_done x_done").split()
        s = {n: sem(f"a1_{n}", c) for n in names}
        CHUNKS = {0: 0, 1: 1, 3: 2, 5: 3}

        def schedule(batch, finish, eng):
            batch(0, 0, True)
            batch(1, 1, True)
            with eng.Fori(1, NB // 2 - 1) as i:
                for par in range(2):
                    batch(i * 2 + par, par, True)
            batch(NB - 2, 0, True)
            batch(NB - 1, 1, False)
            finish()

        def exists(n):
            return not isinstance(n, int) or 0 <= n < NH * NB

        with nc.Block() as block:
            @block.sync
            def _(sp):
                sp.dma_start(ahead["raw1"][:], A["sh1_T"].rearrange("(k p) f -> p k f", p=P)).then_inc(ahead["w1_in"], 16)
                sp.dma_start(ahead["raw2"][:], A["sh2_T"].rearrange("(k p) d -> p k d", p=P)).then_inc(ahead["w2_in"], 16)

            @block.tensor
            def _(pe):
                def turn_kv(b):
                    pe.wait_ge(s["normed"], b * 2 + 2)
                    at_least(pe, s["v_f"], b * 4)
                    for m in range(2):
                        for a in range(KD):
                            ins = pe.transpose(psV[:, (a * 2 + m) * P:(a * 2 + m + 1) * P], normed[m][:, a * P:(a + 1) * P], ident[:])
                    ins.then_inc(s["kv_turned"], 1)

                def project(n, b, h, par):
                    if h == 0:
                        pe.wait_ge(s["kv_lo"], b + 1)
                    at_least(pe, s["qk_lo"], n - 1)
                    for w, col, lo, width, at in ((wq, h, P, P, 0), (wkv, h, 0, NK, P)):
                        for m, (a, (x, y)) in enumerate([(a, xy) for a in range(KD) for xy in PARTS3]):
                            ins = pe.matmul(psA[h % 2][:, at:at + width], w[x][:, a, col * DH:(col + 1) * DH],
                                            kv[par][y][:, a, lo:lo + width], start=(m == 0), stop=(m == 3 * KD - 1))
                    ins.then_inc(s["qk_done"], 1)

                def values(b, ch, par):
                    half, kt = divmod(ch, 2)
                    at_least(pe, s["v_f"], b * 4 + ch)
                    if ch == 0:
                        pe.wait_ge(s["kv_scaled"], b + 1)
                    for m, (a, (x, y)) in enumerate([(a, xy) for a in range(KD) for xy in PARTS3]):
                        ins = pe.matmul(psV[:], kv[par][x][:, a, kt * P:(kt + 1) * P],
                                        wkv[y][:, a, NI + half * 512:NI + (half + 1) * 512], start=(m == 0), stop=(m == 3 * KD - 1))
                    ins.then_inc(s["v_done"], 1)

                def score(n, h):
                    pe.wait_ge(s["qk_lo"], n + 1)
                    at_least(pe, s["exp_done"], n - 1)
                    for m, (x, y) in enumerate(PARTS3):
                        ins = pe.matmul(psS[h % 2][:], q[x][:, h, :], k_[y][:, h, :], start=(m == 0), stop=(m == 2))
                    ins.then_inc(s["s_done"], 1)

                def turn(n, h):
                    pe.wait_ge(s["p_done"], n + 1)
                    at_least(pe, s["pt_lo"], n)
                    for kt in range(2):
                        ins = pe.transpose(psT[:, kt, :], probs[:, h, kt * P:(kt + 1) * P], ident[:])
                    ins.then_inc(s["t_done"], 1)

                def apply(n, b, h):
                    pe.wait_ge(s["pt_lo"], n + 1)
                    at_least(pe, s["o_lo"], n)
                    if h in (0, 4):
                        pe.wait_ge(s["v_lo"], b * 4 + (2 if h == 0 else 4))
                    for m, (kt, (x, y)) in enumerate([(kt, xy) for kt in range(2) for xy in PARTS3]):
                        ins = pe.matmul(psO[:], v[x][:, kt, h * DH:(h + 1) * DH], pT[y][:, h, kt, :], start=(m == 0), stop=(m == 5))
                    ins.then_inc(s["pv_done"], 1)

                def output(b):
                    pe.wait_ge(s["o_lo"], b * NH + NH)
                    at_least(pe, s["x_done"], b)
                    for m, (h, (x, y)) in enumerate([(h, xy) for h in range(NH) for xy in PARTS3]):
                        ins = pe.matmul(psY[:], oT[x][:, h, :], wo[y][:, h, :], start=(m == 0), stop=(m == 3 * NH - 1))
                    ins.then_inc(s["y_done"], 1)

                def later(b, h, lag):
                    return (b, h - lag) if h >= lag else (b - 1, h - lag + NH)

                def rest(b, h):
                    for lag, do in ((1, "s"), (3, "t"), (4, "a")):
                        bb, hh = later(b, h, lag)
                        n = bb * NH + hh
                        if do == "a" and h == 4 and exists((b - 1) * NH):
                            output(b - 1)
                        if not exists(n):
                            continue
                        if do == "s":
                            score(n, hh)
                        elif do == "t":
                            turn(n, hh)
                        else:
                            apply(n, bb, hh)

                def batch(b, par, more):
                    for h in range(NH):
                        project(b * NH + h, b, h, par)
                        if h in CHUNKS:
                            values(b, CHUNKS[h], par)
                        if h == 6 and more:
                            turn_kv(b + 1)
                        rest(b, h)

                def finish():
                    for h in range(5):
                        rest(NB, h)

                turn_kv(0)
                schedule(batch, finish, pe)

            @block.scalar
            def _(act):
                def scale_kv(b):
                    act.wait_ge(s["kv_turned"], b + 1)
                    at_least(act, s["kv_lo"], b)
                    for m in range(2):
                        for a in range(KD):
                            ins = act.activation(kvf[:, a, m * P:(m + 1) * P], psV[:, (a * 2 + m) * P:(a * 2 + m + 1) * P], ACT.Identity,
                                                 bias=bet[:, m, a:a + 1], scale=gam[:, m, a:a + 1])
                    ins.then_inc(s["kv_scaled"], 1)

                def project(n, h):
                    act.wait_ge(s["qk_done"], n + 1)
                    act.activation(q[0][:, h, :], psA[h % 2][:, 0:P], ACT.Identity, bias=bq[:, h:h + 1])
                    act.activation(k_[0][:, h, :], psA[h % 2][:, P:3 * P], ACT.Identity, bias=bk[:, h:h + 1]).then_inc(s["qk_hi"], 1)

                def exps(n, h):
                    act.wait_ge(s["max_done"], n + 1)
                    act.activation(probs[:, h, :], psS[h % 2][:], ACT.Exp, bias=nmax[:, h:h + 1],
                                   accum_out=sums[:, h:h + 1]).then_inc(s["exp_done"], 1)

                def turn(n, h):
                    act.wait_ge(s["t_done"], n + 1)
                    act.activation(pT[0][:, h, :, :], psT[:], ACT.Copy).then_inc(s["pt_hi"], 1)

                def apply(n, h):
                    act.wait_ge(s["pv_done"], n + 1)
                    act.activation(oT[0][:, h, :], psO[:], ACT.Copy).then_inc(s["o_hi"], 1)

                def values(b, ch):
                    half, kt = divmod(ch, 2)
                    act.wait_ge(s["v_f"], b * 4 + ch + 1)
                    act.activation(v[0][:, kt, half * 512:(half + 1) * 512], vf[:], ACT.Copy).then_inc(s["v_hi"], 1)

                def rest(b, h, lags):
                    for lag, do in lags:
                        bb, hh = (b, h - lag) if h >= lag else (b - 1, h - lag + NH)
                        if exists(bb * NH + hh):
                            do(bb * NH + hh, hh)

                def batch(b, par, more):
                    for h in range(NH):
                        rest(b, h, ((4, turn), (5, apply)))
                        if h - 1 in CHUNKS:
                            values(b, CHUNKS[h - 1])
                        rest(b, h, ((2, exps),))
                        if h == 7 and more:
                            scale_kv(b + 1)
                        project(b * NH + h, h)

                def finish():
                    for h in range(5):
                        rest(NB, h, ((4, turn), (5, apply), (2, exps)))

                scale_kv(0)
                schedule(batch, finish, act)

            @block.gpsimd
            def _(pool):
                with pool.Fori(0, NB) as i:
                    pool.wait_ge(s["normed"], i * 2 + 2)
                    pool.tensor_tensor(x_sb[:, i, :], x_sb[:, i, :], bo[:], ALU.add).then_inc(s["resid"], 1)

            @block.vector
            def _(dve):
                def norm(b):
                    at_least(dve, s["kv_turned"], b)
                    for m, (src, mean, rstd) in enumerate(((ctx_sb, c_mean, c_rstd), (x_sb, x_mean, x_rstd))):
                        at = b if isinstance(b, int) else bass.ds(b, 1)
                        one = slice(b, b + 1) if isinstance(b, int) else bass.ds(b, 1)
                        dve.tensor_scalar(normed[m][:], src[:, b, :], mean[:, one], rstd[:, one],
                                          ALU.subtract, ALU.mult).then_inc(s["normed"], 1)

                def split_kv(b, par):
                    dve.wait_ge(s["kv_scaled"], b + 1)
                    dve.tensor_copy(kv[par][0][:], kvf[:]).then_inc(s["kv_hi"], 1)
                    dve.wait_ge(s["kv_hi"], b + 1)
                    dve.tensor_tensor(kv[par][1][:], kvf[:], kv[par][0][:].bitcast(F32), ALU.subtract).then_inc(s["kv_lo"], 1)

                def project(n, h):
                    dve.wait_ge(s["qk_hi"], n + 1)
                    dve.scalar_tensor_tensor(out=q[1][:, h, :], in0=psA[h % 2][:, 0:P], scalar=bq[:, h:h + 1],
                                             in1=q[0][:, h, :].bitcast(F32), op0=ALU.add, op1=ALU.subtract)
                    dve.scalar_tensor_tensor(out=k_[1][:, h, :], in0=psA[h % 2][:, P:3 * P], scalar=bk[:, h:h + 1],
                                             in1=k_[0][:, h, :].bitcast(F32), op0=ALU.add, op1=ALU.subtract).then_inc(s["qk_lo"], 1)

                def values(b, ch):
                    half, kt = divmod(ch, 2)
                    dve.wait_ge(s["v_done"], b * 4 + ch + 1)
                    at_least(dve, s["v_lo"], b * 4 + ch)
                    cols = slice(half * 512, (half + 1) * 512)
                    dve.tensor_tensor(vf[:], psV[:], bv[:, cols], ALU.add).then_inc(s["v_f"], 1)

                def values_lo(b, ch):
                    half, kt = divmod(ch, 2)
                    cols = slice(half * 512, (half + 1) * 512)
                    dve.wait_ge(s["v_hi"], b * 4 + ch + 1)
                    dve.tensor_tensor(v[1][:, kt, cols], vf[:], v[0][:, kt, cols].bitcast(F32), ALU.subtract).then_inc(s["v_lo"], 1)

                def maximum(n, h):
                    dve.wait_ge(s["s_done"], n + 1)
                    dve.tensor_reduce(nmax[:, h:h + 1], psS[h % 2][:], AX.X, ALU.max, negate=True).then_inc(s["max_done"], 1)

                def normalize(n, h):
                    dve.wait_ge(s["exp_done"], n + 1)
                    dve.reciprocal(rsum[:, h:h + 1], sums[:, h:h + 1]).then_inc(s["rsum_done"], 1)
                    dve.wait_ge(s["rsum_done"], n + 1)
                    dve.tensor_scalar(probs[:, h, :], probs[:, h, :], rsum[:, h:h + 1], None, ALU.mult).then_inc(s["p_done"], 1)

                def turn(n, h):
                    dve.wait_ge(s["pt_hi"], n + 1)
                    dve.tensor_tensor(pT[1][:, h, :, :], psT[:], pT[0][:, h, :, :].bitcast(F32), ALU.subtract).then_inc(s["pt_lo"], 1)

                def apply(n, h):
                    dve.wait_ge(s["o_hi"], n + 1)
                    dve.tensor_tensor(oT[1][:, h, :], psO[:], oT[0][:, h, :].bitcast(F32), ALU.subtract).then_inc(s["o_lo"], 1)

                def residual(b):
                    dve.wait_ge(s["y_done"], b + 1)
                    dve.wait_ge(s["resid"], b + 1)
                    dve.scalar_tensor_tensor(out=x_sb[:, b, :], in0=psY[:], scalar=gates[:, 1:2], in1=x_sb[:, b, :],
                                             op0=ALU.mult, op1=ALU.add).then_inc(s["x_done"], 1)

                def statistics(b):
                    dve.wait_ge(s["x_done"], b + 1)
                    dve.bn_stats(x_stats[:, b, :], x_sb[:, b, :])

                def steps(b, h, lags):
                    for lag, do in lags:
                        bb, hh = (b, h - lag) if h >= lag else (b - 1, h - lag + NH)
                        if exists(bb * NH + hh):
                            do(bb * NH + hh, hh)

                def batch(b, par, more):
                    for h in range(NH):
                        steps(b, h, ((2, maximum), (4, turn), (5, apply)))
                        if h - 1 in CHUNKS:
                            values_lo(b, CHUNKS[h - 1])
                        steps(b, h, ((2, normalize),))
                        if h == 2 and more:
                            norm(b + 1)
                        if h == 5 and exists((b - 1) * NH):
                            residual(b - 1)
                        if h == 6 and exists((b - 1) * NH):
                            statistics(b - 1)
                        if h == 7 and more:
                            split_kv(b + 1, 1 - par)
                        project(b * NH + h, h)
                        if h in CHUNKS:
                            values(b, CHUNKS[h])

                def finish():
                    for h in range(5):
                        steps(NB, h, ((2, maximum), (4, turn), (5, apply), (2, normalize)))
                    residual(NB - 1)
                    statistics(NB - 1)

                norm(0)
                split_kv(0, 0)
                schedule(batch, finish, dve)
    return ahead


def mixture_1(nc, A, sb, ps, sem, NB, D, KD, x_sb, ctx_sb, ident, gates, x_mean, x_rstd, c_mean, c_rstd,
              x_stats, c_stats, nt, out, ahead):
    NE, _, F = A["fc1_T"].shape
    FS = A["sh1_T"].shape[1]
    NTOK = NB * P
    CAP = -(-(-(-NTOK * 2 // NE) * 5) // 4)
    NSLOT = NE * CAP
    xg = nc.dram_tensor("m1_sorted", (NSLOT + 2 * NTOK, D), F32, kind="Internal").ap()
    yg = nc.dram_tensor("m1_expert_out", (NSLOT + P, D), F32, kind="Internal").ap()
    KS = FS // P
    with ExitStack() as c:
        n_sb = sb("m1_n", [P, NB, D], F32, c)
        sh = sb("m1_shared", [P, NB, D], F32, c)
        b2s = sb("m1_b2s", [P, D], F32, c)
        into = [sb(f"m1_into{i}", [P, NB], U32, c) for i in range(2)]
        back = [sb(f"m1_back{i}", [P, NB], U32, c) for i in range(2)]
        wk = [sb(f"m1_wk{i}", [P, NB], F32, c) for i in range(2)]
        ones = sb("m1_ones", [P, P], F32, c)
        upper = sb("m1_upper", [P, P], F32, c)
        zeros = sb("m1_zeros", [P, D], F32, c)
        scattered = [sem(f"m1_scattered{n}", c) for n in range(2)]
        zeroed = sem("m1_zeroed", c)
        with ExitStack() as t:
            w1 = [sb(f"m1_ws1{n}", [P, KD, FS], F32R, t) for n in ("hi", "lo")]
            w2 = [sb(f"m1_ws2{n}", [P, KS, D], F32R, t) for n in ("hi", "lo")]
            b1 = sb("m1_bs1", [P, KS], F32, t)
            logits = sb("m1_logits", [P, NB, NE], F32, t)
            proj = sb("m1_proj", [P, KD, NE], F32, t)
            pb, eb = sb("m1_pb", [P, NE], F32, t), sb("m1_eb", [P, NE], F32, t)
            shared_weights(nc, A, sb, ps, sem, D, KD, KS, FS, w1, w2, b1, b2s, proj, pb, eb, ones, upper, gates, xg, yg, NSLOT, NE, zeros, zeroed, ahead)
            hT = [sb(f"m1_hT{n}", [P, KD, NB, P], F32R, t) for n in ("hi", "lo")]
            token_norms(nc, sb, ps, sem, NB, D, KD, x_sb, ident, x_mean, x_rstd, x_stats, nt, n_sb, hT,
                        logits, proj, None, None, NE, "m1", False)
            wmat, cur, hots, ws = top2(nc, sb, ps, sem, NB, NE, logits, pb, eb, t)
            shared_gelu(nc, sb, ps, sem, NB, NE, CAP, NSLOT, NTOK, D, KD, KS, hT, w1, w2, b1, sh, gates, wmat, cur, hots, ws,
                        into, back, wk, ones, upper, n_sb, xg, scattered, zeroed)
        experts_gelu(nc, A, sb, ps, sem, NB, NE, CAP, D, KD, F, x_sb, sh, b2s, ident, xg, yg, n_sb, into, back, wk, scattered, out)


def shared_weights(nc, A, sb, ps, sem, D, KD, KS, FS, w1, w2, b1, b2s, proj, pb, eb, ones, upper, gates, xg, yg, NSLOT, NE, zeros, zeroed, ahead):
    with ExitStack() as c:
        raw1, raw2 = ahead["raw1"], ahead["raw2"]
        s = {n: sem(f"d_{n}", c) for n in "small_in hi const_done".split()}
        flat = lambda t: t.rearrange("p a n -> p (a n)")
        with nc.Block() as block:
            @block.sync
            def _(sp):
                with nc.allow_non_contiguous_dma(reason="a few hundred small parameters"):
                    for dst, src in ((b1[:], A["L1_ffn_sh1_b"].rearrange("(k p) -> p k", p=P)),
                                     (b2s[:], A["L1_ffn_sh2_b"].partition_broadcast(P)),
                                     (proj[:], A["proj_T"].rearrange("(k p) e -> p k e", p=P)),
                                     (pb[:], A["L1_ffn_proj_b"].partition_broadcast(P)),
                                     (eb[:], A["L1_ffn_expert_bias"].partition_broadcast(P))):
                        sp.dma_start(dst, src).then_inc(s["small_in"], 16)
                sp.wait_ge(s["const_done"], 2)
                sp.dma_start(xg[0:NSLOT].rearrange("(t p) d -> p t d", p=P), zeros[:].unsqueeze(1).to_broadcast([P, NSLOT // P, D]))\
                  .then_inc(zeroed, 16)
                last = NSLOT - NSLOT // NE
                sp.dma_start(yg[last:NSLOT + P].rearrange("(t p) d -> p t d", p=P),
                             zeros[:].unsqueeze(1).to_broadcast([P, (NSLOT + P - last) // P, D])).then_inc(zeroed, 16)
                sp.wait_ge(s["small_in"], 80)

            @block.gpsimd
            def _(pool):
                pool.memset(zeros[:], 0.0).then_inc(s["const_done"], 1)
                pool.memset(ones[:], 1.0).then_inc(s["const_done"], 1)
                pool.wait_ge(s["const_done"], 2)
                pool.affine_select(out=upper[:], in_=ones[:], compare_op=ALU.is_gt, fill=0.0, base=0,
                                   pattern=[[1, P]], channel_multiplier=-1).then_inc(s["const_done"], 1)

            @block.scalar
            def _(act):
                act.wait_ge(ahead["w1_in"], 16)
                act.activation(flat(w1[0][:]), flat(raw1[:]), ACT.Copy).then_inc(s["hi"], 1)
                act.wait_ge(ahead["w2_in"], 16)
                act.activation(flat(w2[0][:]), flat(raw2[:]), ACT.Copy).then_inc(s["hi"], 1)

            @block.vector
            def _(dve):
                for n, (w, raw) in enumerate(((w1, raw1), (w2, raw2))):
                    dve.wait_ge(s["hi"], n + 1)
                    dve.tensor_tensor(flat(w[1][:]), flat(raw[:]), flat(w[0][:]).bitcast(F32), ALU.subtract)
                dve.wait_ge(s["small_in"], 80)
                dve.tensor_scalar(b2s[:], b2s[:], gates[:, 3:4], None, ALU.mult)


def top2(nc, sb, ps, sem, NB, NE, logits, pb, eb, c):
    wmat = sb("r1_wmat", [P, NB, NE], F32, c)
    hots = [sb(f"r1_hot{i}", [P, NB, NE], F32, c) for i in range(2)]
    ws = [sb(f"r1_w{i}", [P, NB], F32, c) for i in range(2)]
    cur = sb("r1_cur", [P, NE], I32, c)
    with ExitStack() as t:
        z = sb("r1_z", [P, NB, NE], F32, t)
        sg = sb("r1_sg", [P, NB, NE], F32, t)
        best = sb("r1_best", [P, NB, 8], F32, t)
        index = sb("r1_index", [P, NB, 8], U32, t)
        which, ordered = sb("r1_which", [P, 2, NB], F32, t), sb("r1_ordered", [P, 2, NB], F32, t)
        iota_i = sb("r1_iota_i", [P, NE], I32, t)
        iota = sb("r1_iota", [P, NE], F32, t)
        tmp = sb("r1_tmp", [P, NB, NE], F32, t)
        total = sb("r1_total", [P, NB], F32, t)
        s = {n: sem(f"r1_{n}", t) for n in "steps iota_done biased sigmoid".split()}
        wide = lambda a: a.unsqueeze(2).to_broadcast([P, NB, NE])
        with nc.Block() as block:
            @block.gpsimd
            def _(pool):
                pool.iota(iota_i[:], pattern=[[1, NE]], base=0, channel_multiplier=0).then_inc(s["iota_done"], 1)

            @block.scalar
            def _(act):
                act.wait_ge(s["biased"], 1)
                act.activation(sg[:], z[:], ACT.Sigmoid).then_inc(s["sigmoid"], 1)

            @block.vector
            def _(dve):
                k = Steps(dve, s["steps"])
                dve.tensor_tensor(z[:], logits[:], pb[:].unsqueeze(1).to_broadcast([P, NB, NE]), ALU.add).then_inc(s["biased"], 1)
                dve.memset(cur[:], 0)
                dve.wait_ge(s["iota_done"], 1)
                k.step(dve.tensor_copy(iota[:], iota_i[:]))
                dve.wait_ge(s["sigmoid"], 1)
                k.step(dve.tensor_tensor(sg[:], sg[:], eb[:].unsqueeze(1).to_broadcast([P, NB, NE]), ALU.add))
                k.step(dve.tensor_scalar(sg[:], sg[:], 1e-12, None, ALU.max))
                for i in range(NB):
                    ins = dve.max(best[:, i, :], sg[:, i, :])
                k.step(ins)
                for i in range(NB):
                    ins = dve.max_index(index[:, i, :], best[:, i, :], sg[:, i, :])
                k.step(ins)
                for n in range(2):
                    ins = dve.tensor_copy(which[:, n, :], index[:, :, n])
                k.step(ins)
                k.step(dve.tensor_tensor(total[:], best[:, :, 0], best[:, :, 1], ALU.add))
                k.step(dve.reciprocal(total[:], total[:]))
                for n in range(2):
                    dve.tensor_tensor(ws[n][:], best[:, :, n], total[:], ALU.mult)
                    ins = dve.tensor_tensor(hots[n][:], wide(which[:, n, :]), iota[:].unsqueeze(1).to_broadcast([P, NB, NE]),
                                            ALU.is_equal)
                k.step(ins)
                dve.tensor_tensor(wmat[:], hots[0][:], wide(ws[0][:]), ALU.mult)
                k.step(dve.tensor_tensor(tmp[:], hots[1][:], wide(ws[1][:]), ALU.mult))
                k.step(dve.tensor_tensor(wmat[:], wmat[:], tmp[:], ALU.add))
                for n, op in enumerate((ALU.min, ALU.max)):
                    ins = dve.tensor_tensor(ordered[:, n, :], which[:, 0, :], which[:, 1, :], op)
                k.step(ins)
                for n in range(2):
                    ins = dve.tensor_tensor(hots[n][:], wide(ordered[:, n, :]), iota[:].unsqueeze(1).to_broadcast([P, NB, NE]),
                                            ALU.is_equal)
                k.step(ins)
                for n in range(2):
                    ins = dve.tensor_tensor((tmp, z)[n][:], hots[n][:], wmat[:], ALU.mult)
                k.step(ins)
                for n in range(2):
                    dve.tensor_reduce(ws[n][:], (tmp, z)[n][:], AX.X, ALU.add)
    return wmat, cur, hots, ws


def shared_gelu(nc, sb, ps, sem, NB, NE, CAP, NSLOT, NTOK, D, KD, KS, hT, w1, w2, b1, sh, gates, wmat, cur, hots, ws,
                into, back, wk, ones, upper, n_sb, xg, scattered, zeroed):
    PAIRS = NB // 2
    NQ = KS // 2
    with ExitStack() as c:
        g = [sb(f"s1_g{i}", [P, 2, 2 * P], F32, c) for i in range(2)]
        gs = [[sb(f"s1_g{n}{i}", [P, KS, 2 * P], F32R, c) for n in ("hi", "lo")] for i in range(2)]
        psH = [ps(f"s1_psH{i}", [P, 2, 2 * P], F32, c) for i in range(NQ)]
        psY = [ps(f"s1_psY{i}", [P, D], F32, c) for i in range(2)]
        s = {n: sem(f"s1_{n}", c) for n in "up gelu g_hi g_lo down kept start counted count_out found".split()}
        ROUNDS, CANDS = 4, 3
        SEARCH = 4
        assert SEARCH * ROUNDS * 2 >= 31 and SEARCH + 2 <= PAIRS
        bits = sb("s1_bits", [P, CANDS, NE], I32, c)
        cand = sb("s1_cand", [P, CANDS, NE], I32, c)
        pass_ = sb("s1_pass", [P, CANDS, NE], F32, c)
        take = sb("s1_take", [P, NE], I32, c)
        over = sb("s1_over", [P, CANDS * NE, NB], F32, c)
        count = sb("s1_count", [P, CANDS * NE], F32, c)
        psC = ps("s1_psC", [P, CANDS, NE], F32, c)
        pl = places(nc, sb, ps, sem, NB, NE, CAP, NSLOT, NTOK, wmat, cur, hots, ws, into, back, wk, ones, upper, gates, c)
        with nc.Block() as block:
            @block.gpsimd
            def _(pool):
                pl["on_pool"](pool)
                pool.wait_ge(zeroed, 32)
                pool.wait_ge(pl["placed"][0], 1)
                scatter(pool, NB, into[0], n_sb, xg, scattered[0])

            @block.tensor
            def _(pe):
                def up(i, q):
                    at_least(pe, s["gelu"], (i - 1) * NQ + q + 1)
                    tiles = slice(2 * i, 2 * i + 2)
                    for j in range(2):
                        t = 2 * q + j
                        for m, (a, (x, y)) in enumerate([(a, xy) for a in range(KD) for xy in PARTS3]):
                            ins = pe.matmul(psH[q][:, j, :], w1[x][:, a, t * P:(t + 1) * P],
                                            hT[y][:, a, tiles, :].rearrange("p b t -> p (b t)"), start=(m == 0), stop=(m == 3 * KD - 1))
                    ins.then_inc(s["up"], 1)

                def down(i, j):
                    pe.wait_ge(s["g_lo"], i * NQ + NQ)
                    at_least(pe, s["kept"], (i - 1) * 2 + j + 1)
                    for m, (t, (x, y)) in enumerate([(t, xy) for t in range(KS) for xy in PARTS3]):
                        ins = pe.matmul(psY[j][:], gs[i % 2][x][:, t, j * P:(j + 1) * P], w2[y][:, t, :], start=(m == 0), stop=(m == 3 * KS - 1))
                    ins.then_inc(s["down"], 1)

                def tally(i, r):
                    pe.wait_ge(s["counted"], i * ROUNDS + r + 1)
                    pe.matmul(psC[:].rearrange("p c e -> p (c e)"), ones[:], count[:], start=True, stop=True).then_inc(s["count_out"], 1)

                def aside(i, r):
                    if i < SEARCH:
                        tally(i, r)
                    elif (i, r) == (SEARCH, 1):
                        pl["rank_marked"](pe)
                    elif (i, r) == (SEARCH + 1, 0):
                        pl["rank_kept"](pe)

                for q in range(NQ):
                    up(0, q)
                for i in range(PAIRS):
                    for q in range(NQ):
                        if i + 1 < PAIRS:
                            up(i + 1, q)
                        if q in (1, 3):
                            aside(i, q // 2)
                    down(i, 0)
                    aside(i, 2)
                    down(i, 1)
                    aside(i, 3)

            @block.scalar
            def _(act):
                def gelu(i, q):
                    act.wait_ge(s["up"], i * NQ + q + 1)
                    at_least(act, s["g_lo"], i * NQ + q - 1)
                    at_least(act, s["down"], (i - 1) * 2)
                    for j in range(2):
                        t = 2 * q + j
                        ins = act.activation(g[q % 2][:, j, :], psH[q][:, j, :], ACT.Gelu, bias=b1[:, t:t + 1])
                    ins.then_inc(s["gelu"], 1)
                    act.wait_ge(s["gelu"], i * NQ + q + 1)
                    act.activation(gs[i % 2][0][:, 2 * q:2 * q + 2, :], g[q % 2][:], ACT.Copy).then_inc(s["g_hi"], 1)

                def keep(i, j):
                    act.wait_ge(s["down"], i * 2 + j + 1)
                    act.activation(sh[:, 2 * i + j, :], psY[j][:], ACT.Copy, scale=gates[:, 3:4]).then_inc(s["kept"], 1)

                for i in range(PAIRS + 1):
                    for q in range(NQ):
                        if i < PAIRS:
                            gelu(i, q)
                        if i > 0 and q == 1:
                            keep(i - 1, 0)
                    if i > 0:
                        keep(i - 1, 1)

            @block.vector
            def _(dve):
                def split(i, q):
                    dve.wait_ge(s["g_hi"], i * NQ + q + 1)
                    dve.tensor_tensor(gs[i % 2][1][:, 2 * q:2 * q + 2, :], g[q % 2][:], gs[i % 2][0][:, 2 * q:2 * q + 2, :].bitcast(F32),
                                      ALU.subtract).then_inc(s["g_lo"], 1)

                STEPS = 5

                def count_over(i, r):
                    k = Steps(dve, s["found"], (i * ROUNDS + r) * STEPS)
                    k.step(dve.tensor_tensor(over[:].rearrange("p (c e) b -> p c b e", e=NE),
                                             wmat[:].unsqueeze(1).to_broadcast([P, CANDS, NB, NE]),
                                             cand[:].bitcast(F32).unsqueeze(2).to_broadcast([P, CANDS, NB, NE]), ALU.is_ge))
                    dve.tensor_reduce(count[:], over[:], AX.X, ALU.add).then_inc(s["counted"], 1)

                def raise_bar(i, r):
                    k = Steps(dve, s["found"], (i * ROUNDS + r) * STEPS + 1)
                    dve.wait_ge(s["count_out"], i * ROUNDS + r + 1)
                    k.step(dve.scalar_tensor_tensor(out=pass_[:], in0=psC[:], scalar=float(CAP), in1=bits[:],
                                                    op0=ALU.is_ge, op1=ALU.mult))
                    dve.tensor_scalar(bits[:], bits[:], 2, None, ALU.logical_shift_right)
                    k.step(dve.tensor_reduce(take[:], pass_[:].rearrange("p c e -> p e c"), AX.X, ALU.max))
                    k.step(dve.tensor_tensor(cur[:], cur[:], take[:], ALU.bitwise_or))
                    k.step(dve.tensor_tensor(cand[:], bits[:], cur[:].unsqueeze(1).to_broadcast([P, CANDS, NE]), ALU.bitwise_or))
                    assert k.n == STEPS - 1

                k = Steps(dve, s["start"])
                for n in range(CANDS):
                    ins = dve.memset(bits[:, n, :], (n + 1) << 29)
                k.step(ins)
                k.step(dve.tensor_copy(cand[:], bits[:]))
                count_over(0, 0)
                for q in range(NQ):
                    split(0, q)
                k = Steps(dve, pl["steps"])
                parts = list(pl["parts"])
                for i in range(PAIRS):
                    for r in range(ROUNDS):
                        if i < SEARCH:
                            raise_bar(i, r)
                            if r + 1 < ROUNDS:
                                count_over(i, r + 1)
                            elif i + 1 < SEARCH:
                                count_over(i + 1, 0)
                        elif parts:
                            parts.pop(0)(k)
                        if i + 1 < PAIRS:
                            split(i + 1, r)


def places(nc, sb, ps, sem, NB, NE, CAP, NSLOT, NTOK, wmat, cur, hots, ws, into, back, wk, ones, upper, gates, c):
    over = sb("p1_over", [P, NB, NE], F32, c)
    equal = sb("p1_equal", [P, NB, NE], F32, c)
    tmp = sb("p1_tmp", [P, NB, NE], F32, c)
    tot = sb("p1_tot", [P, NB, NE], F32, c)
    pre = [sb(f"p1_pre{i}", [P, NB, NE], F32, c) for i in range(2)]
    rank = sb("p1_rank", [P, NB, NE], F32, c)
    kept = sb("p1_kept", [P, NB, NE], F32, c)
    nover = sb("p1_nover", [P, NE], F32, c)
    room = sb("p1_room", [P, NE], F32, c)
    first_i = sb("p1_first_i", [P, NE], I32, c)
    first = sb("p1_first", [P, NE], F32, c)
    token_i = sb("p1_token_i", [P, NB], I32, c)
    token = sb("p1_token", [P, NB], F32, c)
    at, has, lost = (sb(f"p1_{n}", [P, NB], F32, c) for n in ("at", "has", "lost"))
    psR = ps("p1_ps", [P, 3, NB * NE], F32, c)
    psK = psR
    s = {n: sem(f"p1_{n}", c) for n in "steps iota_done marked ranked kept_done ranked2 placed0 placed1".split()}
    flat = lambda t: t[:].rearrange("p b e -> p (b e)")
    three = lambda t: t.rearrange("p (b e) -> p b e", e=NE)
    wide = lambda a: a.unsqueeze(1).to_broadcast([P, NB, NE])

    def on_pool(pool):
        pool.iota(first_i[:], pattern=[[CAP, NE]], base=0, channel_multiplier=0).then_inc(s["iota_done"], 1)
        pool.iota(token_i[:], pattern=[[P, NB]], base=NSLOT, channel_multiplier=1).then_inc(s["iota_done"], 1)

    def rank_marked(pe):
        pe.wait_ge(s["marked"], 1)
        pe.matmul(psR[:, 0, :], upper[:], flat(equal), start=True, stop=True)
        pe.matmul(psR[:, 1, :], ones[:], flat(equal), start=True, stop=True)
        pe.matmul(psR[:, 2, :], ones[:], flat(over), start=True, stop=True).then_inc(s["ranked"], 1)

    def rank_kept(pe):
        pe.wait_ge(s["kept_done"], 1)
        pe.matmul(psK[:, 0, :], upper[:], flat(kept), start=True, stop=True)
        pe.matmul(psK[:, 1, :], ones[:], flat(kept), start=True, stop=True).then_inc(s["ranked2"], 1)

    def before(k, psX):
        k.step(k.eng.tensor_copy(tot[:], three(psX[:, 1, :])))
        incl = prefix_steps(k.eng, k, tot, pre, NB)
        k.step(k.eng.tensor_tensor(rank[:], three(psX[:, 0, :]), incl[:], ALU.add))
        k.step(k.eng.tensor_tensor(rank[:], rank[:], tot[:], ALU.subtract))

    def mark(k):
        dve, bar = k.eng, cur[:].bitcast(F32)
        dve.tensor_tensor(over[:], wmat[:], wide(bar), ALU.is_gt)
        k.step(dve.tensor_tensor(tmp[:], wmat[:], wide(bar), ALU.is_equal))
        dve.scalar_tensor_tensor(out=equal[:], in0=wmat[:], scalar=0.0, in1=tmp[:], op0=ALU.is_gt, op1=ALU.mult)\
           .then_inc(s["marked"], 1)
        dve.wait_ge(s["iota_done"], 2)
        dve.tensor_copy(first[:], first_i[:])
        k.step(dve.tensor_copy(token[:], token_i[:]))

    def order_equals(k):
        k.eng.wait_ge(s["ranked"], 1)
        before(k, psR)

    def keep(k):
        dve = k.eng
        k.step(dve.tensor_reduce(nover[:], psR[:, 2, :].rearrange("p (b e) -> p e b", e=NE), AX.X, ALU.add))
        k.step(dve.tensor_scalar(room[:], nover[:], -1.0, float(CAP), ALU.mult, ALU.add))
        k.step(dve.tensor_tensor(rank[:], rank[:], wide(room[:]), ALU.is_lt))
        k.step(dve.tensor_tensor(rank[:], rank[:], equal[:], ALU.mult))
        k.step(dve.tensor_tensor(kept[:], rank[:], over[:], ALU.add))
        dve.tensor_copy(tmp[:], kept[:]).then_inc(s["kept_done"], 1)

    def order_kept(k):
        dve = k.eng
        dve.wait_ge(s["ranked2"], 1)
        before(k, psK)
        k.step(dve.tensor_tensor(rank[:], rank[:], wide(first[:]), ALU.add))
        k.step(dve.tensor_tensor(rank[:], rank[:], kept[:], ALU.mult))

    def place(n):
        def part(k):
            dve = k.eng
            k.step(dve.tensor_tensor(tmp[:], hots[n][:], rank[:], ALU.mult))
            k.step(dve.tensor_reduce(at[:], tmp[:], AX.X, ALU.add))
            k.step(dve.tensor_tensor(tmp[:], hots[n][:], kept[:], ALU.mult))
            k.step(dve.tensor_reduce(has[:], tmp[:], AX.X, ALU.add))
            k.step(dve.tensor_scalar(lost[:], has[:], -1.0, 1.0, ALU.mult, ALU.add))
            k.step(dve.scalar_tensor_tensor(out=back[n][:], in0=lost[:], scalar=float(NSLOT), in1=at[:],
                                            op0=ALU.mult, op1=ALU.add))
            k.step(dve.scalar_tensor_tensor(out=lost[:], in0=token[:], scalar=float(n * NTOK), in1=lost[:],
                                            op0=ALU.add, op1=ALU.mult))
            dve.tensor_tensor(into[n][:], lost[:], at[:], ALU.add).then_inc(s[f"placed{n}"], 1)
            dve.wait_ge(s[f"placed{n}"], 1)
            k.step(dve.tensor_tensor(wk[n][:], ws[n][:], has[:], ALU.mult))
            k.step(dve.tensor_scalar(wk[n][:], wk[n][:], gates[:, 3:4], None, ALU.mult))
        return part

    return dict(on_pool=on_pool, rank_marked=rank_marked, rank_kept=rank_kept,
                parts=[mark, order_equals, keep, order_kept, place(0), place(1)], steps=s["steps"],
                placed=[s["placed0"], s["placed1"]])


def scatter(pool, NB, rows, n_sb, xg, done):
    for i in range(NB):
        pool.indirect_dma_start(xg, bass.IndirectOffsetOnAxis(ap=rows[:, i:i + 1], axis=0), n_sb[:, i, :], None).then_inc(done, 16)


def experts_gelu(nc, A, sb, ps, sem, NB, NE, CAP, D, KD, F, x_sb, sh, b2s, ident, xg, yg, n_sb, into, back, wk, scattered, out):
    KF, NT, HALF = F // P, CAP // P, CAP // 2
    assert CAP % P == 0 and HALF <= 512 and KD * F == KF * D
    with ExitStack() as c:
        raw = [sb(f"x1_raw{i}", [P, 2, KD * F], F32, c) for i in range(2)]
        w1 = [[sb(f"x1_w1{n}{i}", [P, KD, F], F32R, c) for n in ("hi", "lo")] for i in range(2)]
        w2 = [[sb(f"x1_w2{n}{i}", [P, KF, D], F32R, c) for n in ("hi", "lo")] for i in range(2)]
        b1 = sb("x1_b1", [P, NE, KF], F32, c)
        b1e = [sb(f"x1_b1e{i}", [P, KF], F32, c) for i in range(2)]
        b2 = sb("x1_b2", [P, NE, D], F32, c)
        xin = [sb(f"x1_xin{i}", [P, NT, D], F32, c) for i in range(2)]
        xT = [sb(f"x1_xT{n}", [P, KD, CAP], F32R, c) for n in ("hi", "lo")]
        g = sb("x1_g", [P, KF, CAP], F32, c)
        gs = [sb(f"x1_g{n}", [P, KF, CAP], F32R, c) for n in ("hi", "lo")]
        y = [sb(f"x1_y{i}", [P, D], F32, c) for i in range(2)]
        psX = [ps(f"x1_psX{i}", [P, KD, P], F32, c) for i in range(2)]
        psH = [ps(f"x1_psH{i}", [P, HALF], F32, c) for i in range(4)]
        psY = [ps(f"x1_psY{i}", [P, D], F32, c) for i in range(2)]
        names = ("w_in0 w_in1 b_in x_in0 x_in1 turned xt_hi xt_lo w_hi w_lo up gelu g_hi g_lo down y_done y_out0 y_out1 "
                 "x_gated x_biased combined out_done").split()
        s = {n: sem(f"x1_{n}", c) for n in names}
        w_in, x_in, y_out = [s["w_in0"], s["w_in1"]], [s["x_in0"], s["x_in1"]], [s["y_out0"], s["y_out1"]]
        xg_t = xg[0:NE * CAP].rearrange("(e t p) d -> e p t d", p=P, t=NT)
        yg_t = yg[0:NE * CAP].rearrange("(e t p) d -> e t p d", p=P, t=NT)
        NC = 2 * KF
        chunk = lambda m: (m % KF, m // KF)
        gathered = [[sem(f"x1_gathered{n}_{i}", c) for i in range(NB)] for n in range(2)]

        flat = lambda t: t.rearrange("p a n -> p (a n)")
        parts_of = lambda b: ((w1[b], raw[b][:, 0, :]), (w2[b], raw[b][:, 1, :]))

        with nc.Block() as block:
            @block.sync
            def _(sp):
                def load_w(e, b):
                    sp.dma_start(raw[b][:, 0, :].rearrange("p (k f) -> p k f", k=KD), A["fc1_T"][e].rearrange("(k p) f -> p k f", p=P))\
                      .then_inc(w_in[b], 16)
                    sp.dma_start(raw[b][:, 1, :].rearrange("p (k d) -> p k d", k=KF), A["fc2_T"][e].rearrange("(k p) d -> p k d", p=P))\
                      .then_inc(w_in[b], 16)

                def load_x(e, b):
                    sp.dma_start(xin[b][:], xg_t[e]).then_inc(x_in[b], 16)

                load_w(0, 0)
                load_w(1, 1)
                with nc.allow_non_contiguous_dma(reason="a few thousand small parameters"):
                    sp.dma_start(b1[:], A["L1_ffn_fc1_b"].rearrange("e (k p) -> p e k", p=P)).then_inc(s["b_in"], 16)
                    sp.dma_start(b2[:], A["L1_ffn_fc2_b"].partition_broadcast(P)).then_inc(s["b_in"], 16)
                sp.wait_ge(scattered[0], NB * 16)
                load_x(0, 0)
                sp.wait_ge(scattered[1], NB * 16)
                load_x(1, 1)

                def stores(e):
                    for t in range(NT):
                        b = (e_par * NT + t) % 2
                        sp.wait_ge(s["y_done"], e * NT + t + 1)
                        sp.dma_start(yg_t[e, t], y[b][:]).then_inc(y_out[b], 16)

                with sp.Fori(0, NE // 2 - 1) as i:
                    for e_par in range(2):
                        sp.wait_ge(s["w_lo"], i * 2 + e_par + 1)
                        load_w(i * 2 + e_par + 2, e_par)
                        sp.wait_ge(s["turned"], (i * 2 + e_par + 1) * NT)
                        load_x(i * 2 + e_par + 2, e_par)
                        stores(i * 2 + e_par)
                for e_par in range(2):
                    stores(NE - 2 + e_par)
                for i in range(NB):
                    sp.wait_ge(s["combined"], NB + i + 1)
                    sp.dma_start(out[i], x_sb[:, i, :]).then_inc(s["out_done"], 16)
                sp.wait_ge(s["out_done"], NB * 16)

            @block.tensor
            def _(pe):
                def turn(e, b, pair, t):
                    if t == 0:
                        pe.wait_ge(x_in[b], pair * 16 + 16)
                    at_least(pe, s["xt_lo"], e * NT + t - 1)
                    for a in range(KD):
                        ins = pe.transpose(psX[(b * NT + t) % 2][:, a, :], xin[b][:, t, a * P:(a + 1) * P], ident[:])
                    ins.then_inc(s["turned"], 1)

                def up(e, b):
                    pe.wait_ge(s["w_lo"], e + 1)
                    pe.wait_ge(s["xt_lo"], e * NT + NT)
                    for m in range(NC):
                        f, half = chunk(m)
                        at_least(pe, s["gelu"], e * NC + m - 3)
                        rows = slice(half * HALF, (half + 1) * HALF)
                        for n, (a, (x, y_)) in enumerate([(a, xy) for a in range(KD) for xy in PARTS3]):
                            ins = pe.matmul(psH[m % 4][:], w1[b][x][:, a, f * P:(f + 1) * P], xT[y_][:, a, rows],
                                            start=(n == 0), stop=(n == 3 * KD - 1))
                        ins.then_inc(s["up"], 1)

                def down(e, b, t):
                    if t == 0:
                        pe.wait_ge(s["g_lo"], e * NC + KF)
                    if t == HALF // P:
                        pe.wait_ge(s["g_lo"], e * NC + NC)
                    at_least(pe, s["y_done"], e * NT + t - 1)
                    for n, (f, (x, y_)) in enumerate([(f, xy) for f in range(KF) for xy in PARTS3]):
                        ins = pe.matmul(psY[(b * NT + t) % 2][:], gs[x][:, f, t * P:(t + 1) * P], w2[b][y_][:, f, :],
                                        start=(n == 0), stop=(n == 3 * KF - 1))
                    ins.then_inc(s["down"], 1)

                def expert(e, b, pair, more=True):
                    up(e, b)
                    for t in range(NT):
                        if more:
                            turn(e + 1, 1 - b, pair + b, t)
                        down(e, b, t)

                for t in range(NT):
                    turn(0, 0, 0, t)
                expert(0, 0, 0)
                expert(1, 1, 0)
                with pe.Fori(1, NE // 2 - 1) as i:
                    for b in range(2):
                        expert(i * 2 + b, b, i)
                expert(NE - 2, 0, NE // 2 - 1)
                expert(NE - 1, 1, NE // 2 - 1, more=False)

            @block.scalar
            def _(act):
                def weights(e, b, pair):
                    act.wait_ge(w_in[b], pair * 32 + 32)
                    at_least(act, s["down"], (e - 1) * NT)
                    at_least(act, s["gelu"], (e - 1) * NC)
                    act.activation(b1e[b][:], b1[:, e, :], ACT.Copy)
                    for w, r in parts_of(b):
                        act.activation(flat(w[0][:]), r, ACT.Copy).then_inc(s["w_hi"], 1)

                def turn(e, b):
                    at_least(act, s["up"], e * NC)
                    for t in range(NT):
                        act.wait_ge(s["turned"], e * NT + t + 1)
                        act.activation(xT[0][:, :, t * P:(t + 1) * P], psX[(b * NT + t) % 2][:], ACT.Copy).then_inc(s["xt_hi"], 1)

                def gelu(e, b):
                    act.wait_ge(s["w_hi"], e * 2 + 2)
                    for m in range(NC):
                        f, half = chunk(m)
                        act.wait_ge(s["up"], e * NC + m + 1)
                        at_least(act, s["g_lo"], e * NC + m - NC + 1)
                        act.activation(g[:, f, half * HALF:(half + 1) * HALF], psH[m % 4][:], ACT.Gelu, bias=b1e[b][:, f:f + 1])\
                           .then_inc(s["gelu"], 1)

                def expert(e, b, pair, more=True):
                    gelu(e, b)
                    if more:
                        turn(e + 1, 1 - b)
                        if not (isinstance(e, int) and e == NE - 2):
                            weights(e + 2, b, pair + 1)

                act.wait_ge(s["b_in"], 32)
                weights(0, 0, 0)
                weights(1, 1, 0)
                turn(0, 0)
                expert(0, 0, 0)
                expert(1, 1, 0)
                with act.Fori(1, NE // 2 - 1) as i:
                    for b in range(2):
                        expert(i * 2 + b, b, i)
                expert(NE - 2, 0, NE // 2 - 1)
                expert(NE - 1, 1, NE // 2 - 1, more=False)

            @block.gpsimd
            def _(pool):
                def weights(e, b):
                    for n, (w, r) in enumerate(parts_of(b)):
                        pool.wait_ge(s["w_hi"], e * 2 + n + 1)
                        ins = pool.tensor_tensor(flat(w[1][:]), r, flat(w[0][:]).bitcast(F32), ALU.subtract)
                    ins.then_inc(s["w_lo"], 1)

                def residual(i):
                    pool.tensor_tensor(x_sb[:, i, :], x_sb[:, i, :], b2s[:], ALU.add).then_inc(s["x_biased"], 1)
                    pool.wait_ge(s["x_biased"], i + 1)
                    pool.tensor_tensor(x_sb[:, i, :], x_sb[:, i, :], sh[:, i, :], ALU.add).then_inc(s["x_gated"], 1)

                scatter(pool, NB, into[1], n_sb, xg, scattered[1])
                with pool.Fori(0, 2 * (NB // NE)) as i:
                    residual(i)
                with pool.Fori(1, NE // 2) as i:
                    for b in range(2):
                        weights(i * 2 + b, b)
                        for n in range(NB // NE):
                            residual((i * 2 + b) * (NB // NE) + n)
                pool.wait_ge(s["x_gated"], NB)
                for n, dst in enumerate((n_sb, sh)):
                    stored = (NE - 1 + n) * NT
                    for b in range(2):
                        pool.wait_ge(y_out[b], (stored + 1 - b) // 2 * 16)
                    for i in range(NB):
                        pool.indirect_dma_start(dst[:, i, :], None, yg, bass.IndirectOffsetOnAxis(ap=back[n][:, i:i + 1], axis=0))\
                            .then_inc(gathered[n][i], 16)

            @block.vector
            def _(dve):
                def turn(e, b, t):
                    at_least(dve, s["up"], e * NC)
                    cols = slice(t * P, (t + 1) * P)
                    dve.wait_ge(s["xt_hi"], e * NT + t + 1)
                    dve.tensor_tensor(xT[1][:, :, cols], psX[(b * NT + t) % 2][:], xT[0][:, :, cols].bitcast(F32), ALU.subtract)\
                       .then_inc(s["xt_lo"], 1)

                def split(e, b):
                    at_least(dve, s["down"], e * NT)
                    for m in range(NC):
                        f, half = chunk(m)
                        rows = slice(half * HALF, (half + 1) * HALF)
                        dve.wait_ge(s["gelu"], e * NC + m + 1)
                        dve.tensor_copy(gs[0][:, f, rows], g[:, f, rows]).then_inc(s["g_hi"], 1)
                        dve.wait_ge(s["g_hi"], e * NC + m + 1)
                        dve.tensor_tensor(gs[1][:, f, rows], g[:, f, rows], gs[0][:, f, rows].bitcast(F32), ALU.subtract)\
                           .then_inc(s["g_lo"], 1)

                def out(e, b, pair, t):
                    yb = (b * NT + t) % 2
                    dve.wait_ge(s["down"], e * NT + t + 1)
                    at_least(dve, y_out[yb], (pair * NT + (b * NT + t) // 2) * 16)
                    dve.tensor_tensor(y[yb][:], psY[yb][:], b2[:, e, :], ALU.add).then_inc(s["y_done"], 1)

                def expert(e, b, pair, more=True):
                    split(e, b)
                    for t in range(NT):
                        if more:
                            turn(e + 1, 1 - b, t)
                        out(e, b, pair, t)

                for e in range(2):
                    for n, (w, r) in enumerate(parts_of(e)):
                        dve.wait_ge(s["w_hi"], e * 2 + n + 1)
                        ins = dve.tensor_tensor(flat(w[1][:]), r, flat(w[0][:]).bitcast(F32), ALU.subtract)
                    ins.then_inc(s["w_lo"], 1)
                dve.wait_ge(s["b_in"], 32)
                for t in range(NT):
                    turn(0, 0, t)
                expert(0, 0, 0)
                expert(1, 1, 0)
                with dve.Fori(1, NE // 2 - 1) as i:
                    for b in range(2):
                        expert(i * 2 + b, b, i)
                expert(NE - 2, 0, NE // 2 - 1)
                expert(NE - 1, 1, NE // 2 - 1, more=False)
                for n, src in enumerate((n_sb, sh)):
                    for i in range(NB):
                        dve.wait_ge(gathered[n][i], 16)
                        dve.wait_ge(s["x_gated"], i + 1)
                        if n == 1:
                            dve.wait_ge(s["combined"], i + 1)
                        ins = dve.scalar_tensor_tensor(out=x_sb[:, i, :], in0=src[:, i, :], scalar=wk[n][:, i:i + 1],
                                                       in1=x_sb[:, i, :], op0=ALU.mult, op1=ALU.add)
                        ins.then_inc(s["combined"], 1)


def laid_out(inputs):
    import numpy as np

    a = {k: np.ascontiguousarray(v) for k, v in inputs.items()}
    a["router_T"] = np.ascontiguousarray(a["L0_ffn_router_w"].T)
    a["proj_T"] = np.ascontiguousarray(a["L1_ffn_proj_w"].T)
    a["sh1_T"] = np.ascontiguousarray(a["L1_ffn_sh1_w"].T)
    a["sh2_T"] = np.ascontiguousarray(a["L1_ffn_sh2_w"].T)
    a["fc1_T"] = np.ascontiguousarray(a["L1_ffn_fc1_w"].transpose(0, 2, 1))
    a["fc2_T"] = np.ascontiguousarray(a["L1_ffn_fc2_w"].transpose(0, 2, 1))
    for k in ("L0_ffn_router_w", "L1_ffn_proj_w", "L1_ffn_sh1_w", "L1_ffn_sh2_w", "L1_ffn_fc1_w", "L1_ffn_fc2_w"):
        del a[k]
    return a


def kernel(**inputs):
    import concourse.bacc as bacc
    from concourse.bass_utils import run_bass_kernel_spmd

    nc = bacc.Bacc("TRN2", target_bir_lowering=False, num_devices=1)
    arrays = {f"in_{k}": v for k, v in laid_out(inputs).items()}
    A = {k[3:]: nc.dram_tensor(k, v.shape, mybir.dt.from_np(v.dtype), kind="ExternalInput").ap() for k, v in arrays.items()}
    out = nc.dram_tensor("out", arrays["in_x"].shape, F32, kind="ExternalOutput").ap()
    program(nc, A, out)
    return run_bass_kernel_spmd(nc, [arrays], core_ids=[0]).results[0]["out"]
```
